# Optimizing a Trainium2 kernel written in Bass

```python
import numpy as np
import jax
import jax.numpy as jnp

def _softmax(x, axis=-1):
    return jax.nn.softmax(x, axis=axis)

def _gelu(x):
    return jax.nn.gelu(x, approximate=True)

def _silu(x):
    return jax.nn.silu(x)

def _sigmoid(x):
    return jax.nn.sigmoid(x)

def _layernorm(x, axis=-1, eps=1e-05):
    m = jnp.mean(x, axis=axis, keepdims=True)
    v = jnp.var(x, axis=axis, keepdims=True)
    return (x - m) / jnp.sqrt(v + eps)

def _scatter_add(tgt, idx, src, axis=0):
    return tgt.at[idx].add(src)

def _segment_sum(src, seg, n):
    return jax.ops.segment_sum(src, seg, n)
kernel_name = 'mk_flamingo_gated_d2_seqx_r4_308216'

def setup_inputs(seed: int=0):
    np.random.seed(seed)
    _w = jnp.asarray

    def _rec_inputs():
        import jax
        import jax.numpy as jnp
        _rk = jax.random.key(seed)
        x = -0.0002928 + 1 * jax.random.normal(jax.random.fold_in(_rk, 1), (16, 100, 256), jnp.float32)
        _lenS = 100 - jax.random.randint(jax.random.fold_in(_rk, 7), (16,), 0, max(1, 100 // 4) + 1, jnp.int32)
        _lenS2 = 361 - jax.random.randint(jax.random.fold_in(_rk, 8), (16,), 0, max(1, 361 // 4) + 1, jnp.int32)
        _ctx_1024P = jax.random.normal(jax.random.fold_in(_rk, 11), (16, 16, 256), jnp.float32)
        _ctx_1024c = jax.random.dirichlet(jax.random.fold_in(_rk, 511), 0.3 * jnp.ones((16,), jnp.float32), (16, 361))
        _ctx_1024t = jnp.einsum('bsk,bkd->bsd', _ctx_1024c, _ctx_1024P)
        _ctx_1024t = _ctx_1024t * jax.lax.rsqrt(jnp.mean(jnp.square(_ctx_1024t)) + 1e-12) * 0.953939
        ctx_1024 = -1.39393e-06 + 0.999914 * (_ctx_1024t + 0.3 * jax.random.normal(jax.random.fold_in(_rk, 611), (16, 361, 256), jnp.float32))
        _g = jax.random.normal(jax.random.fold_in(_rk, 9001), (2, 2), jnp.float32)
        _g = jnp.sign(_g) * jnp.maximum(jnp.abs(_g), 1.0) + (_g == 0) * 1.0
        g_xattn = _g[0]
        g_ffn = _g[1]
        return (x, ctx_1024, g_xattn, g_ffn)
    x, ctx_1024, g_xattn, g_ffn = _rec_inputs()

    def _L0_xattn_setup():
        import jax, jax.numpy as jnp
        import numpy as np
        import math
        D_MODEL = 256
        N_HEADS = 16
        D_HEAD = D_MODEL // N_HEADS
        key = jax.random.key(seed)
        ks = jax.random.split(key, 11)
        N, L, S = (2, 512, 512)
        inp = {'queries': jax.random.normal(ks[0], (N, L, D_MODEL), dtype=jnp.float32), 'keys': jax.random.normal(ks[1], (N, S, D_MODEL), dtype=jnp.float32), 'values': jax.random.normal(ks[2], (N, S, D_MODEL), dtype=jnp.float32), 'Wq': jax.random.normal(ks[3], (D_MODEL, N_HEADS * D_HEAD), dtype=jnp.float32) / math.sqrt(D_MODEL), 'bq': jnp.zeros((N_HEADS * D_HEAD,), dtype=jnp.float32), 'Wk': jax.random.normal(ks[4], (D_MODEL, N_HEADS * D_HEAD), dtype=jnp.float32) / math.sqrt(D_MODEL), 'bk': jnp.zeros((N_HEADS * D_HEAD,), dtype=jnp.float32), 'Wv': jax.random.normal(ks[5], (D_MODEL, N_HEADS * D_HEAD), dtype=jnp.float32) / math.sqrt(D_MODEL), 'bv': jnp.zeros((N_HEADS * D_HEAD,), dtype=jnp.float32), 'Wo': jax.random.normal(ks[6], (N_HEADS * D_HEAD, D_MODEL), dtype=jnp.float32) / math.sqrt(N_HEADS * D_HEAD), 'bo': jnp.zeros((D_MODEL,), dtype=jnp.float32)}
        return inp
    _L0_xattn_all = _L0_xattn_setup()
    _L0_xattn_in = {k: v for k, v in _L0_xattn_all.items() if k in ('Wq', 'bq', 'Wk', 'bk', 'Wv', 'bv', 'Wo', 'bo')}
    del _L0_xattn_all

    def _L0_ffn_setup():
        import jax, jax.numpy as jnp
        import numpy as np
        TOP_K = 2
        key = jax.random.key(seed)
        ks = jax.random.split(key, 6)
        B, T, H, E, F = (2, 512, 256, 8, 1024)
        s = 0.02
        return {'hidden_states': jax.random.normal(ks[0], (B, T, H), dtype=jnp.float32), 'router_w': jax.random.normal(ks[1], (E, H), dtype=jnp.float32) * s, 'w1': jax.random.normal(ks[2], (E, F, H), dtype=jnp.float32) * s, 'b1': jax.random.normal(ks[3], (E, F), dtype=jnp.float32) * s, 'w2': jax.random.normal(ks[4], (E, H, F), dtype=jnp.float32) * s, 'b2': jax.random.normal(ks[5], (E, H), dtype=jnp.float32) * s}
    _L0_ffn_all = _L0_ffn_setup()
    _L0_ffn_in = {k: v for k, v in _L0_ffn_all.items() if k in ('router_w', 'w1', 'b1', 'w2', 'b2')}
    del _L0_ffn_all

    def _L1_xattn_setup():
        import jax, jax.numpy as jnp
        import numpy as np
        D, H = (256, 16)
        DH = D // H

        def _split_heads(z):
            b, t, _ = z.shape
            return z.reshape(b, t, H, DH).transpose(0, 2, 1, 3)
        key = jax.random.key(seed)
        ks = jax.random.split(key, 11)
        b, t, ta = (2, 512, 375)
        s = 1.0 / np.sqrt(D)
        return {'x': jax.random.normal(ks[0], (b, t, D), dtype=jnp.float32), 'xa': jax.random.normal(ks[1], (b, ta, D), dtype=jnp.float32), 'Wqkv': jax.random.normal(ks[2], (D, 3 * D), dtype=jnp.float32) * s, 'bqkv': jax.random.normal(ks[3], (3 * D,), dtype=jnp.float32) * 0.01, 'Wqkv_aux': jax.random.normal(ks[4], (D, 3 * D), dtype=jnp.float32) * s, 'bqkv_aux': jax.random.normal(ks[5], (3 * D,), dtype=jnp.float32) * 0.01, 'Wo': jax.random.normal(ks[6], (D, D), dtype=jnp.float32) * s, 'bo': jax.random.normal(ks[7], (D,), dtype=jnp.float32) * 0.01, 'g': jnp.zeros((H,), dtype=jnp.float32)}
    _L1_xattn_all = _L1_xattn_setup()
    _L1_xattn_in = {k: v for k, v in _L1_xattn_all.items() if k in ('Wqkv', 'bqkv', 'Wqkv_aux', 'bqkv_aux', 'Wo', 'bo', 'g')}
    del _L1_xattn_all

    def _L1_ffn_setup():
        import jax, jax.numpy as jnp
        import numpy as np
        D_MODEL = 256
        D_FF = 1024
        NUM_M = 2
        E_ROUTER = 8 * NUM_M - 1
        D_FF_R = D_FF // NUM_M
        TOP_K = NUM_M * 2 - 1
        B, T = (2, 512)

        def _expert_stack(x, W1, b1, W2, b2):
            h = jax.nn.gelu(jnp.einsum('btd,edf->ebtf', x, W1) + b1[:, None, None, :], approximate=False)
            return jnp.einsum('ebtf,efd->ebtd', h, W2) + b2[:, None, None, :]
        key = jax.random.key(seed)
        ks = jax.random.split(key, 12)
        s = lambda fan_in: 1.0 / np.sqrt(fan_in)
        x = jax.random.normal(ks[0], (B, T, D_MODEL), dtype=jnp.float32)
        sW1 = jax.random.uniform(ks[1], (1, D_MODEL, D_FF), jnp.float32, -s(D_MODEL), s(D_MODEL))
        sb1 = jax.random.uniform(ks[2], (1, D_FF), jnp.float32, -s(D_MODEL), s(D_MODEL))
        sW2 = jax.random.uniform(ks[3], (1, D_FF, D_MODEL), jnp.float32, -s(D_FF), s(D_FF))
        sb2 = jax.random.uniform(ks[4], (1, D_MODEL), jnp.float32, -s(D_FF), s(D_FF))
        rW1 = jax.random.uniform(ks[5], (E_ROUTER, D_MODEL, D_FF_R), jnp.float32, -s(D_MODEL), s(D_MODEL))
        rb1 = jax.random.uniform(ks[6], (E_ROUTER, D_FF_R), jnp.float32, -s(D_MODEL), s(D_MODEL))
        rW2 = jax.random.uniform(ks[7], (E_ROUTER, D_FF_R, D_MODEL), jnp.float32, -s(D_FF_R), s(D_FF_R))
        rb2 = jax.random.uniform(ks[8], (E_ROUTER, D_MODEL), jnp.float32, -s(D_FF_R), s(D_FF_R))
        gW = jax.random.uniform(ks[9], (D_MODEL, E_ROUTER), jnp.float32, -s(D_MODEL), s(D_MODEL))
        gb = jax.random.uniform(ks[10], (E_ROUTER,), jnp.float32, -s(D_MODEL), s(D_MODEL))
        return {'x': x, 'sW1': sW1, 'sb1': sb1, 'sW2': sW2, 'sb2': sb2, 'rW1': rW1, 'rb1': rb1, 'rW2': rW2, 'rb2': rb2, 'gW': gW, 'gb': gb}
    _L1_ffn_all = _L1_ffn_setup()
    _L1_ffn_in = {k: v for k, v in _L1_ffn_all.items() if k in ('sW1', 'sb1', 'sW2', 'sb2', 'rW1', 'rb1', 'rW2', 'rb2', 'gW', 'gb')}
    del _L1_ffn_all
    return {'x': x, 'ctx_1024': ctx_1024, 'g_xattn': g_xattn, 'g_ffn': g_ffn, 'L0_xattn_Wq': _L0_xattn_in['Wq'], 'L0_xattn_bq': _L0_xattn_in['bq'], 'L0_xattn_Wk': _L0_xattn_in['Wk'], 'L0_xattn_bk': _L0_xattn_in['bk'], 'L0_xattn_Wv': _L0_xattn_in['Wv'], 'L0_xattn_bv': _L0_xattn_in['bv'], 'L0_xattn_Wo': _L0_xattn_in['Wo'], 'L0_xattn_bo': _L0_xattn_in['bo'], 'L0_ffn_router_w': _L0_ffn_in['router_w'], 'L0_ffn_w1': _L0_ffn_in['w1'], 'L0_ffn_b1': _L0_ffn_in['b1'], 'L0_ffn_w2': _L0_ffn_in['w2'], 'L0_ffn_b2': _L0_ffn_in['b2'], 'L1_xattn_Wqkv': _L1_xattn_in['Wqkv'], 'L1_xattn_bqkv': _L1_xattn_in['bqkv'], 'L1_xattn_Wqkv_aux': _L1_xattn_in['Wqkv_aux'], 'L1_xattn_bqkv_aux': _L1_xattn_in['bqkv_aux'], 'L1_xattn_Wo': _L1_xattn_in['Wo'], 'L1_xattn_bo': _L1_xattn_in['bo'], 'L1_xattn_g': _L1_xattn_in['g'], 'L1_ffn_sW1': _L1_ffn_in['sW1'], 'L1_ffn_sb1': _L1_ffn_in['sb1'], 'L1_ffn_sW2': _L1_ffn_in['sW2'], 'L1_ffn_sb2': _L1_ffn_in['sb2'], 'L1_ffn_rW1': _L1_ffn_in['rW1'], 'L1_ffn_rb1': _L1_ffn_in['rb1'], 'L1_ffn_rW2': _L1_ffn_in['rW2'], 'L1_ffn_rb2': _L1_ffn_in['rb2'], 'L1_ffn_gW': _L1_ffn_in['gW'], 'L1_ffn_gb': _L1_ffn_in['gb']}

def reference(x, ctx_1024, g_xattn, g_ffn, L0_xattn_Wq, L0_xattn_bq, L0_xattn_Wk, L0_xattn_bk, L0_xattn_Wv, L0_xattn_bv, L0_xattn_Wo, L0_xattn_bo, L0_ffn_router_w, L0_ffn_w1, L0_ffn_b1, L0_ffn_w2, L0_ffn_b2, L1_xattn_Wqkv, L1_xattn_bqkv, L1_xattn_Wqkv_aux, L1_xattn_bqkv_aux, L1_xattn_Wo, L1_xattn_bo, L1_xattn_g, L1_ffn_sW1, L1_ffn_sb1, L1_ffn_sW2, L1_ffn_sb2, L1_ffn_rW1, L1_ffn_rb1, L1_ffn_rW2, L1_ffn_rb2, L1_ffn_gW, L1_ffn_gb):
    import jax
    import jax.numpy as jnp

    def _L0_xattn_ref(queries, keys, values, Wq, bq, Wk, bk, Wv, bv, Wo, bo):
        import jax, jax.numpy as jnp
        import numpy as np
        import math
        D_MODEL = 256
        N_HEADS = 16
        D_HEAD = D_MODEL // N_HEADS
        N, L, _ = queries.shape
        S = keys.shape[1]
        H, D = (N_HEADS, D_HEAD)
        q = (queries @ Wq + bq).reshape(N, L, H, D)
        k = (keys @ Wk + bk).reshape(N, S, H, D)
        v = (values @ Wv + bv).reshape(N, S, H, D)
        sm = jnp.einsum('nlhd,nshd->nlhs', q, k) / math.sqrt(D)
        sm = jax.nn.softmax(sm, axis=1)
        attn = jnp.einsum('nlhs,nshd->nlhd', sm, v).reshape(N, L, H * D)
        return attn @ Wo + bo

    def _L0_ffn_ref(hidden_states, router_w, w1, b1, w2, b2):
        import jax, jax.numpy as jnp
        import numpy as np
        TOP_K = 2
        x = hidden_states
        router_logits = jnp.einsum('bth,eh->bte', x, router_w)
        topk_values, topk_indices = jax.lax.top_k(router_logits, TOP_K)
        topk_weights = jax.nn.softmax(topk_values.astype(jnp.float32), axis=-1).astype(x.dtype)
        h1 = jnp.einsum('bth,efh->btef', x, w1) + b1
        h1 = jax.nn.gelu(h1, approximate=False)
        expert_outputs = jnp.einsum('btef,ehf->bteh', h1, w2) + b2
        gather_idx = topk_indices[..., None]
        topk_expert_outputs = jnp.take_along_axis(expert_outputs, gather_idx, axis=2)
        mixed_output = jnp.sum(topk_expert_outputs * topk_weights[..., None], axis=2)
        return mixed_output

    def _L1_xattn_ref(x, xa, Wqkv, bqkv, Wqkv_aux, bqkv_aux, Wo, bo, g):
        import jax, jax.numpy as jnp
        import numpy as np
        D, H = (256, 16)
        DH = D // H

        def _split_heads(z):
            b, t, _ = z.shape
            return z.reshape(b, t, H, DH).transpose(0, 2, 1, 3)
        qkv = x @ Wqkv + bqkv
        qkv_a = xa @ Wqkv_aux + bqkv_aux
        q, k, v = (_split_heads(c) for c in jnp.split(qkv, 3, axis=-1))
        qa, ka, va = (_split_heads(c) for c in jnp.split(qkv_a, 3, axis=-1))
        scale = 1.0 / jnp.sqrt(jnp.float32(DH))
        dots = jnp.einsum('bhqd,bhkd->bhqk', q, k) * scale
        dots_aux = jnp.einsum('bhqd,bhkd->bhqk', q, ka) * scale
        p = jax.nn.softmax(dots, axis=-1)
        pa = jax.nn.softmax(dots_aux, axis=-1)
        h_main = jnp.einsum('bhqk,bhkd->bhqd', p, v)
        h_aux = jnp.einsum('bhqk,bhkd->bhqd', pa, va)
        gate = jax.nn.sigmoid(g).reshape(1, H, 1, 1)
        out = h_main * (1.0 - gate) + h_aux * gate
        b, _, t, _ = out.shape
        out = out.transpose(0, 2, 1, 3).reshape(b, t, H * DH)
        return out @ Wo + bo

    def _L1_ffn_ref(x, sW1, sb1, sW2, sb2, rW1, rb1, rW2, rb2, gW, gb):
        import jax, jax.numpy as jnp
        import numpy as np
        D_MODEL = 256
        D_FF = 1024
        NUM_M = 2
        E_ROUTER = 8 * NUM_M - 1
        D_FF_R = D_FF // NUM_M
        TOP_K = NUM_M * 2 - 1
        B, T = (2, 512)

        def _expert_stack(x, W1, b1, W2, b2):
            h = jax.nn.gelu(jnp.einsum('btd,edf->ebtf', x, W1) + b1[:, None, None, :], approximate=False)
            return jnp.einsum('ebtf,efd->ebtd', h, W2) + b2[:, None, None, :]
        shared_enc = _expert_stack(x, sW1, sb1, sW2, sb2).sum(0)
        weights = jax.nn.softmax(x @ gW + gb, axis=-1)
        topv, topi = jax.lax.top_k(weights, TOP_K)
        gated = (jax.nn.one_hot(topi, E_ROUTER, dtype=weights.dtype) * topv[..., None]).sum(axis=-2)
        router_out = _expert_stack(x, rW1, rb1, rW2, rb2)
        router_enc = jnp.einsum('ebtd,bte->btd', router_out, gated)
        return shared_enc + router_enc + x
    x = x + jnp.tanh(g_xattn[0]) * _L0_xattn_ref(_layernorm(x, axis=-1), ctx_1024, ctx_1024, L0_xattn_Wq, L0_xattn_bq, L0_xattn_Wk, L0_xattn_bk, L0_xattn_Wv, L0_xattn_bv, L0_xattn_Wo, L0_xattn_bo)
    x = x + jnp.tanh(g_ffn[0]) * _L0_ffn_ref(_layernorm(x, axis=-1), L0_ffn_router_w, L0_ffn_w1, L0_ffn_b1, L0_ffn_w2, L0_ffn_b2)
    x = x + jnp.tanh(g_xattn[1]) * _L1_xattn_ref(_layernorm(x, axis=-1), ctx_1024, L1_xattn_Wqkv, L1_xattn_bqkv, L1_xattn_Wqkv_aux, L1_xattn_bqkv_aux, L1_xattn_Wo, L1_xattn_bo, L1_xattn_g)
    x = x + jnp.tanh(g_ffn[1]) * _L1_ffn_ref(_layernorm(x, axis=-1), L1_ffn_sW1, L1_ffn_sb1, L1_ffn_sW2, L1_ffn_sb2, L1_ffn_rW1, L1_ffn_rb1, L1_ffn_rW2, L1_ffn_rb2, L1_ffn_gW, L1_ffn_gb)
    return x

_drawn_inputs = setup_inputs


def setup_inputs(seed=0):
    import zlib

    import numpy as np

    out = dict(_drawn_inputs(seed))
    spreads = {'g_ffn': (-1.0, 0.2),
     'L0_xattn_bq': (0.0, 2.0),
     'L0_xattn_bk': (0.0, 0.1),
     'L0_xattn_bv': (0.0, 0.1),
     'L0_xattn_bo': (0.0, 0.1),
     'L1_xattn_g': (0.0, 0.675)}
    factors = {'L0_ffn_b1': 29.111,
     'L0_ffn_b2': 8.0,
     'L1_xattn_bqkv': 27.354,
     'L1_xattn_bqkv_aux': 21.962,
     'L1_xattn_bo': 8.0,
     'L1_ffn_sb1': 6.934,
     'L1_ffn_sb2': 4.892,
     'L1_ffn_rb1': 28.49,
     'L1_ffn_rb2': 8.0,
     'L1_ffn_gb': 8.0}
    for name, (base, spread) in spreads.items():
        noise = np.random.default_rng([zlib.crc32(name.encode()), seed]).standard_normal(out[name].shape)
        drawn = base * np.exp(spread * noise) if base else spread * noise
        out[name] = jnp.asarray(drawn.astype(out[name].dtype))
    for name, factor in factors.items():
        out[name] = (out[name] * factor).astype(out[name].dtype)
    return out
```

```python
from contextlib import ExitStack

import concourse.bass as bass
from concourse import mybir

F32 = mybir.dt.float32
F16 = mybir.dt.float16
I32 = mybir.dt.int32
U32 = mybir.dt.uint32
ACT = mybir.ActivationFunctionType
ALU = mybir.AluOpType
AX = mybir.AxisListType.X

P = 128
B, T, D = 16, 100, 256
S = 361
H, DH = 16, 16
KC = D // P
CHUNKS = [(0, 121), (121, 120), (241, 120)]
NJ = len(CHUNKS)
CT = 4
HG = H // CT
PARTS = 4
STACK = PARTS * DH
EPS = 1e-5
Q_PARTS = (0, 1, 0, 1)
K_PARTS = (0, 0, 1, 1)


def on(b):
    return not isinstance(b, int) or 0 <= b < B


def need(eng, sem, value):
    if not isinstance(value, int) or value > 0:
        eng.wait_ge(sem, value)


def landed(b, slot, dmas=1):
    return (b - slot) * (8 * dmas) + 16 * dmas


def pipeline(eng, step, lead, tail, n=2, first=0):
    lo = -(-max(tail, first) // n) * n
    hi = lo + (B - lead - lo) // n * n
    for b in range(-lead, lo):
        step(b, b % n)
    with eng.Fori(lo, hi - n + 1, n) as b:
        for i in range(n):
            step(b + i, i)
    for b in range(hi, B + tail):
        step(b, b % n)


def heads(ap):
    return ap.rearrange("p (h d) -> p h d", d=DH)


class Pool:

    def __init__(self, nc, ctx, stage):
        self.nc, self.ctx, self.stage = nc, ctx, stage
        self.allocated = []

    def close(self):
        self.nc.clear_and_free_semaphores(self.allocated)
        self.nc.all_engine_barrier()

    def sb(self, name, shape, dt=F32):
        return self.ctx.enter_context(self.nc.sbuf_tensor(f"{self.stage}_{name}", shape, dt))

    def ps(self, name, shape, dt=F32):
        return self.ctx.enter_context(self.nc.psum_tensor(f"{self.stage}_{name}", shape, dt))

    def sem(self, name):
        self.allocated.append(self.nc.alloc_semaphore(f"{self.stage}_{name}"))
        return self.allocated[-1]

    def sems(self, name):
        return [self.sem(f"{name}{i}") for i in range(2)]


def constants(nc, ctx, g_xattn, g_ffn):
    m = Pool(nc, ctx, "const")
    ident = m.sb("ident", [P, P])
    gates = m.sb("gates", [P, 4])
    tanhs = m.sb("tanhs", [P, 4])
    mhalf = m.sb("mhalf", [P, 1])
    zeroed, built, loaded, squashed = (m.sem(n) for n in ("zeroed", "built", "loaded", "squashed"))
    with nc.Block() as block:
        @block.gpsimd
        def _(pool):
            pool.memset(ident[:, :], 0.0).then_inc(zeroed, 1)
            pool.wait_ge(zeroed, 1)
            pool.affine_select(out=ident[:, :], in_=ident[:, :], compare_op=ALU.not_equal, fill=1.0,
                               base=0, pattern=[[-1, P]], channel_multiplier=1).then_inc(built, 1)
            pool.memset(mhalf[:, :], -0.5).then_inc(built, 1)
            pool.wait_ge(built, 2)

        @block.sync
        def _(sp):
            sp.dma_start(gates[:, 0:2], g_xattn.partition_broadcast(P)).then_inc(loaded, 16)
            sp.dma_start(gates[:, 2:4], g_ffn.partition_broadcast(P)).then_inc(loaded, 16)

        @block.scalar
        def _(act):
            act.wait_ge(loaded, 32)
            act.activation(tanhs[:, :], gates[:, :], ACT.Tanh).then_inc(squashed, 1)
            act.wait_ge(squashed, 1)
    return ident, mhalf, tanhs[:, 0:2], tanhs[:, 2:4]


class Norm:

    OPS = 6

    def __init__(self, m, mhalf):
        self.mhalf = mhalf
        self.stats, self.mv = m.sb("ln_stats", [T, 6]), m.sb("ln_mv", [T, 2])
        self.var, self.r0 = m.sb("ln_var", [T, 1]), m.sb("ln_r0", [T, 1])
        self.turn = m.sb("ln_turn", [T, 1])
        self.t, self.rstd = m.sb("ln_t", [T, 1]), m.sb("ln_rstd", [T, 1])
        self.step = m.sem("ln_step")
        self.root = m.sem("ln_root")

    def moments(self, dve, b, x):
        at = b * self.OPS
        need(dve, self.step, at)
        dve.bn_stats(self.stats[:, :], x).then_inc(self.step, 1)
        dve.wait_ge(self.step, at + 1)
        dve.memset(self.turn[:, :], 0.0)
        dve.bn_aggr(self.mv[:, :], self.stats[:, :]).then_inc(self.step, 1)
        dve.wait_ge(self.step, at + 2)
        dve.tensor_scalar(self.var[:, :], self.mv[:, 1:2], EPS, None, ALU.add).then_inc(self.step, 1)

    def power(self, pool, b):
        pool.wait_ge(self.step, b * self.OPS + 3)
        pool.tensor_tensor(self.r0[:, :], self.var[:, :], self.mhalf[0:T, :], ALU.pow).then_inc(self.root, 1)

    def newton(self, dve, b):
        at = b * self.OPS
        dve.wait_ge(self.root, b + 1)
        dve.scalar_tensor_tensor(out=self.t[:, :], in0=self.r0[:, :], scalar=self.var[:, 0:1], in1=self.r0[:, :],
                                 op0=ALU.mult, op1=ALU.mult).then_inc(self.step, 1)
        dve.wait_ge(self.step, at + 4)
        dve.tensor_scalar(self.t[:, :], self.t[:, :], -0.5, 1.5, ALU.mult, ALU.add).then_inc(self.step, 1)
        dve.wait_ge(self.step, at + 5)
        dve.tensor_tensor(self.rstd[:, :], self.r0[:, :], self.t[:, :], ALU.mult).then_inc(self.step, 1)

    def apply(self, dve, b, out, x):
        dve.wait_ge(self.step, (b + 1) * self.OPS)
        return dve.tensor_scalar(out, x, self.mv[:, 0:1], self.rstd[:, 0:1], ALU.subtract, ALU.mult)


def stack_views(scratch, slot):
    wr = scratch[slot].rearrange("s (c p) n -> p s c n", p=P)
    rd = scratch[slot].rearrange("s (h d) n -> s d h n", d=DH)
    return wr, rd


def attend0(nc, consts, x_in, x_out, ctxT, Wq, bq, Wk, bk, Wv, bv, Wo, bo):
    ident, mhalf, tanhg = consts
    with ExitStack() as ctx:
        m = Pool(nc, ctx, "at0")
        ctx.callback(m.close)
        RING = 6
        UNITS = 2 * NJ
        HU = H // 2
        wq, wk, wv = (m.sb(n, [P, KC, D]) for n in ("wq", "wk", "wv"))
        wo = m.sb("wo", [P, HG, D])
        bqs, bks = m.sb("bq", [P, KC]), m.sb("bk", [P, KC])
        bvb, bob = m.sb("bv", [P, D]), m.sb("bo", [P, D])
        ctxt = [m.sb(f"ctx{i}", [P, KC, S]) for i in range(2)]
        xin = [m.sb(f"xin{i}", [T, D]) for i in range(2)]
        xres = [m.sb(f"xres{i}", [T, D]) for i in range(2)]
        xout = [m.sb(f"xout{i}", [T, D]) for i in range(2)]
        xhat = [m.sb(f"xhat{i}", [T, D]) for i in range(2)]
        xT = [m.sb(f"xT{i}", [P, KC, T]) for i in range(2)]
        qparts = m.sb("qparts", [P, 2, KC, T], F16)
        kparts = m.sb("kparts", [P, 2, KC, S], F16)
        qst = [m.sb(f"qst{i}", [STACK, H, T], F16) for i in range(2)]
        kst = [m.sb(f"kst{i}", [STACK, H, S], F16) for i in range(2)]
        v = [m.sb(f"v{i}", [P, NJ, D]) for i in range(2)]
        vn = [m.sb(f"vn{i}", [P, NJ, H, 32]) for i in range(2)]
        probs = [m.sb(f"probs{i}", [P, NJ, H * T]) for i in range(2)]
        den = [m.sb(f"den{i}", [P, NJ * H]) for i in range(2)]
        rden = m.sb("rden", [P, NJ * H])
        negmax = [m.sb(f"negmax{i}", [P, HU]) for i in range(2)]
        oT = m.sb("oT", [P, HG * T])
        qd = nc.dram_tensor("at0_qd", (2, 2, D, T), F16).ap()
        kd = nc.dram_tensor("at0_kd", (2, 2, D, S), F16).ap()
        ps_s = m.ps("scores", [P, 4, 512])
        ps_r = m.ps("ring", [P, 2, 512])
        ps_o = m.ps("o", [P, 512])
        ps_y = m.ps("y", [P, 512])
        ln = Norm(m, mhalf)
        w_loaded, zeroed, wo_loaded = m.sem("w_loaded"), m.sem("zeroed"), m.sem("wo_loaded")
        scaled = m.sem("scaled")
        x_loaded, ctx_loaded, res_loaded = m.sems("x_loaded"), m.sems("ctx_loaded"), m.sems("res_loaded")
        xhat_ready, ring_ready, ring_free = m.sem("xhat_ready"), m.sem("ring_ready"), m.sem("ring_free")
        high_ready = m.sem("high_ready")
        q_saved, k_saved = m.sem("q_saved"), m.sem("k_saved")
        q_stacked, k_stacked = m.sems("q_stacked"), m.sems("k_stacked")
        scores_ready, negmax_ready, exp_done = m.sem("scores_ready"), m.sem("negmax_ready"), m.sem("exp_done")
        rden_ready, vn_ready, pv_done = m.sem("rden_ready"), m.sem("vn_ready"), m.sem("pv_done")
        oT_ready, y_ready, x_ready = m.sem("oT_ready"), m.sem("y_ready"), m.sem("x_ready")
        res_ready, x_stored, sp_turns = m.sem("res_ready"), m.sems("x_stored"), m.sem("sp_turns")
        NW = 7

        with nc.Block() as block:
            @block.sync
            def _(sp):
                def hold(sem, value):
                    need(sp, sem, value)
                    sp.sem_inc(sp_turns, 1)

                def load_inputs(b, s):
                    hold(xhat_ready, b - 1)
                    sp.dma_start(xin[s][:, :], x_in[b]).then_inc(x_loaded[s], 16)
                    hold(ring_ready, (b - 1) * RING)
                    sp.dma_start(ctxt[s][:, :, :], ctxT[b].rearrange("(c p) s -> p c s", p=P)).then_inc(ctx_loaded[s], 16)

                def stack(b, s):
                    qw, qr = stack_views(qd, s)
                    kw, kr = stack_views(kd, s)
                    hold(scores_ready, (b - 1) * UNITS)
                    for item, saved, parts, wr in ((1, q_saved, qparts, qw), (3, k_saved, kparts, kw)):
                        hold(ring_free, b * RING + item + 1)
                        for i in range(2):
                            sp.dma_start(wr[:, i], parts[:, i]).then_inc(saved, 16)
                    for saved, stacked, st, rd, order in ((q_saved, q_stacked, qst, qr, Q_PARTS),
                                                          (k_saved, k_stacked, kst, kr, K_PARTS)):
                        hold(saved, (b + 1) * 32)
                        for r, part in enumerate(order):
                            sp.dma_start(st[s][r * DH:(r + 1) * DH, :, :], rd[part]).then_inc(stacked[s], 16)

                def step(b, s):
                    if on(b + 2):
                        load_inputs(b + 2, s)
                    if on(b + 1):
                        stack(b + 1, 1 - s)
                    if on(b - 2):
                        hold(x_ready, b - 1)
                        sp.dma_start(x_out[b - 2], xout[s][:, :]).then_inc(x_stored[s], 16)
                    if on(b):
                        sp.dma_start(xres[s][:, :], x_in[b]).then_inc(res_loaded[s], 16)

                for w, src in ((wq, Wq), (wk, Wk), (wv, Wv)):
                    sp.dma_start(w[:, :, :], src.rearrange("(c p) n -> p c n", p=P)).then_inc(w_loaded, 16)
                for t, src in ((bqs, bq), (bks, bk)):
                    with nc.allow_non_contiguous_dma("one bias a partition"):
                        sp.dma_start(t[:, :], src.rearrange("(c p) -> p c", p=P)).then_inc(w_loaded, 16)
                for t, src in ((bvb, bv), (bob, bo)):
                    sp.dma_start(t[:, :], src.partition_broadcast(P)).then_inc(w_loaded, 16)
                sp.wait_ge(zeroed, 1)
                for h in range(H):
                    sp.dma_start(wo[32 * (h % CT):32 * (h % CT) + DH, h // CT, :],
                                 Wo[h * DH:(h + 1) * DH, :]).then_inc(wo_loaded, 16)
                pipeline(sp, step, 2, 2, first=4)
                for s in range(2):
                    sp.wait_ge(x_stored[s], landed(B - 2 + s, s))

            @block.gpsimd
            def _(pool):
                def step(b, s):
                    if on(b + 2):
                        ln.power(pool, b + 2)
                    if on(b):
                        pool.wait_ge(res_loaded[s], landed(b, s))
                        pool.tensor_tensor(xres[s][:, :], xres[s][:, :], bob[0:T, :], ALU.add).then_inc(res_ready, 1)

                pool.wait_ge(scaled, 3)
                pipeline(pool, step, 2, 2, first=4)

            @block.vector
            def _(dve):
                def norm(b, s):
                    dve.wait_ge(x_loaded[s], landed(b, s))
                    ln.moments(dve, b, xin[s][:, :])
                    ln.newton(dve, b)
                    need(dve, ring_ready, (b - 2) * RING + 1)
                    ln.apply(dve, b, xhat[s][:, :], xin[s][:, :]).then_inc(xhat_ready, 1)

                def split(bank, parts, i, n, bias, at):
                    dve.tensor_scalar(parts[:, 0, i, :], bank, bias[:, i:i + 1], None, ALU.add).then_inc(high_ready, 1)
                    dve.wait_ge(high_ready, at)
                    return dve.scalar_tensor_tensor(out=parts[:, 1, i, :], in0=bank, scalar=bias[:, i:i + 1],
                                                    in1=parts[:, 0, i, :], op0=ALU.add, op1=ALU.subtract)

                def take_xT(b, s):
                    dve.wait_ge(ring_ready, b * RING + 1)
                    dve.tensor_copy(xT[s][:, :, :], ps_r[:, 0, 0:KC * T].rearrange("p (c t) -> p c t", c=KC)).then_inc(ring_free, 1)

                def take_q(b, s):
                    dve.wait_ge(ring_ready, b * RING + 2)
                    need(dve, q_saved, b * 32)
                    for i in range(KC):
                        last = split(ps_r[:, 1, i * T:(i + 1) * T], qparts, i, T, bqs, b * 4 + i + 1)
                    last.then_inc(ring_free, 1)

                def take_k(b, s, i):
                    dve.wait_ge(ring_ready, b * RING + 3 + i)
                    need(dve, k_saved, b * 32)
                    split(ps_r[:, i, 0:S], kparts, i, S, bks, b * 4 + 3 + i).then_inc(ring_free, 1)

                def take_v(b, s, js, item):
                    dve.wait_ge(ring_ready, b * RING + item + 1)
                    need(dve, vn_ready, b - 1)
                    for j in js:
                        r = CHUNKS[j][1]
                        last = dve.tensor_tensor(v[s][0:r, j, :], ps_r[0:r, item % 2, (j - js[0]) * D:(j - js[0] + 1) * D],
                                                 bvb[0:r, :], ALU.add)
                    last.then_inc(ring_free, 1)

                def maxima(b, s, u):
                    r = CHUNKS[u // 2][1]
                    dve.wait_ge(scores_ready, b * UNITS + u + 1)
                    need(dve, exp_done, b * UNITS + u - 1)
                    dve.tensor_reduce(negmax[u % 2][0:r, :].rearrange("p (k h) -> p k h", k=2),
                                      ps_s[0:r, 2 * (u % 2):2 * (u % 2) + 2, 0:HU // 2 * T].rearrange("p k (h t) -> p k h t", t=T),
                                      AX, ALU.max, negate=True).then_inc(negmax_ready, 1)

                def scale_v(b, s):
                    dve.wait_ge(exp_done, (b + 1) * UNITS)
                    need(dve, vn_ready, b)
                    dve.reciprocal(rden[:, :], den[s][:, :]).then_inc(rden_ready, 1)
                    dve.wait_ge(rden_ready, b + 1)
                    need(dve, pv_done, b - 1)
                    dve.wait_ge(ring_free, (b + 1) * RING)
                    dve.tensor_tensor(vn[s][:, :, :, 0:DH].rearrange("p j h d -> p (j h) d"),
                                      v[s][:, :, :].rearrange("p j (h d) -> p (j h) d", d=DH),
                                      rden[:, :].unsqueeze(2).to_broadcast([P, NJ * H, DH]), ALU.mult).then_inc(vn_ready, 1)

                def take_o(b):
                    dve.wait_ge(pv_done, b + 1)
                    need(dve, y_ready, b)
                    dve.tensor_copy(oT[:, :], ps_o[:, 0:HG * T]).then_inc(oT_ready, 1)

                def residual(b, s):
                    dve.wait_ge(y_ready, b + 1)
                    dve.wait_ge(res_ready, b + 1)
                    need(dve, x_stored[s], landed(b - 2, s))
                    dve.scalar_tensor_tensor(out=xout[s][:, :], in0=ps_y[0:T, 0:D], scalar=tanhg[0:T, 0:1],
                                             in1=xres[s][:, :], op0=ALU.mult, op1=ALU.add).then_inc(x_ready, 1)

                def step(b, s):
                    for u in range(UNITS):
                        if on(b):
                            maxima(b, s, u)
                        if u == 0 and on(b - 1):
                            scale_v(b - 1, 1 - s)
                        if u == 1 and on(b - 2):
                            residual(b - 2, s)
                        if on(b + 1):
                            if u == 0:
                                take_xT(b + 1, 1 - s)
                            if u == 1:
                                take_q(b + 1, 1 - s)
                            if u in (2, 3):
                                take_k(b + 1, 1 - s, u - 2)
                            if u == 4:
                                take_v(b + 1, 1 - s, (0, 1), 4)
                            if u == 5:
                                take_v(b + 1, 1 - s, (2,), 5)
                        if u == 5 and on(b - 1):
                            take_o(b - 1)
                        if u == 4 and on(b + 2):
                            norm(b + 2, s)

                dve.memset(wo[:, :, :], 0.0).then_inc(zeroed, 1)
                for i in range(2):
                    dve.memset(v[i][:, :, :], 0.0)
                    dve.memset(den[i][:, :], 1.0)
                    dve.memset(vn[i][:, :, :, :], 0.0).then_inc(zeroed, 1)
                dve.wait_ge(zeroed, 3)
                dve.wait_ge(w_loaded, 16 * NW)
                dve.tensor_scalar(wq[:, :, :], wq[:, :, :], DH ** -0.5, None, ALU.mult).then_inc(scaled, 1)
                dve.tensor_scalar(bqs[:, :], bqs[:, :], DH ** -0.5, None, ALU.mult).then_inc(scaled, 1)
                dve.tensor_scalar(bob[:, :], bob[:, :], tanhg[:, 0:1], None, ALU.mult).then_inc(scaled, 1)
                dve.wait_ge(scaled, 3)
                pipeline(dve, step, 2, 2, first=4)

            @block.scalar
            def _(act):
                def step(b, s):
                    if not on(b):
                        return
                    need(act, pv_done, b - 1)
                    for u in range(UNITS):
                        j, r = u // 2, CHUNKS[u // 2][1]
                        act.wait_ge(negmax_ready, b * UNITS + u + 1)
                        for hh in range(HU):
                            h = (u % 2) * HU + hh
                            last = act.activation(
                                probs[s][0:r, j, h * T:(h + 1) * T],
                                ps_s[0:r, 2 * (u % 2) + hh // 4, (hh % 4) * T:(hh % 4 + 1) * T], ACT.Exp,
                                bias=negmax[u % 2][0:r, hh:hh + 1], accum_out=den[s][0:r, j * H + h:j * H + h + 1])
                        last.then_inc(exp_done, 1)

                act.wait_ge(zeroed, 3)
                pipeline(act, step, 2, 2, first=4)

            @block.tensor
            def _(pe):
                def ring_slot(n):
                    need(pe, ring_free, n - 1)

                def transposes(b, s):
                    ring_slot(b * RING)
                    pe.wait_ge(xhat_ready, b + 1)
                    for c in range(KC):
                        last = pe.transpose(ps_r[:, 0, c * T:(c + 1) * T], xhat[s][:, c * P:(c + 1) * P], ident[0:T, 0:T])
                    last.then_inc(ring_ready, 1)

                def project_q(b, s):
                    pe.wait_ge(ring_free, b * RING + 1)
                    for i in range(KC):
                        for c in range(KC):
                            last = pe.matmul(ps_r[:, 1, i * T:(i + 1) * T], wq[:, c, i * P:(i + 1) * P], xT[s][:, c, :],
                                             start=(c == 0), stop=(c == KC - 1))
                    last.then_inc(ring_ready, 1)

                def project_k(b, s, i):
                    ring_slot(b * RING + 2 + i)
                    if i == 0:
                        pe.wait_ge(ctx_loaded[s], landed(b, s))
                    for c in range(KC):
                        last = pe.matmul(ps_r[:, i, 0:S], wk[:, c, i * P:(i + 1) * P], ctxt[s][:, c, :],
                                         start=(c == 0), stop=(c == KC - 1))
                    last.then_inc(ring_ready, 1)

                def project_v(b, s, js, item):
                    ring_slot(b * RING + item)
                    for j in js:
                        s0, r = CHUNKS[j]
                        for c in range(KC):
                            last = pe.matmul(ps_r[0:r, item % 2, (j - js[0]) * D:(j - js[0] + 1) * D],
                                             ctxt[s][:, c, s0:s0 + r], wv[:, c, :], start=(c == 0), stop=(c == KC - 1))
                    last.then_inc(ring_ready, 1)

                def scores(b, s, u):
                    s0, r = CHUNKS[u // 2]
                    if u == 0:
                        pe.wait_ge(q_stacked[s], landed(b, s, PARTS))
                        pe.wait_ge(k_stacked[s], landed(b, s, PARTS))
                    need(pe, exp_done, b * UNITS + u - 1)
                    for hh in range(HU):
                        h = (u % 2) * HU + hh
                        last = pe.matmul(ps_s[0:r, 2 * (u % 2) + hh // 4, (hh % 4) * T:(hh % 4 + 1) * T],
                                         kst[s][:, h, s0:s0 + r], qst[s][:, h, :], start=True, stop=True)
                    last.then_inc(scores_ready, 1)

                def values(b, s, g):
                    if g == 0:
                        pe.wait_ge(vn_ready, b + 1)
                        need(pe, oT_ready, b)
                    for j, (_, r) in enumerate(CHUNKS):
                        for c in range(CT):
                            h = g * CT + c
                            last = pe.matmul(ps_o[32 * c:32 * c + 32, g * T:(g + 1) * T], vn[s][0:r, j, h, :],
                                             probs[s][0:r, j, h * T:(h + 1) * T], start=(j == 0), stop=(j == NJ - 1))
                    if g == HG - 1:
                        last.then_inc(pv_done, 1)

                def project_o(b):
                    pe.wait_ge(oT_ready, b + 1)
                    need(pe, x_ready, b)
                    for g in range(HG):
                        last = pe.matmul(ps_y[0:T, 0:D], oT[:, g * T:(g + 1) * T], wo[:, g, :],
                                         start=(g == 0), stop=(g == HG - 1))
                    last.then_inc(y_ready, 1)

                def step(b, s):
                    for u in range(UNITS):
                        if on(b):
                            scores(b, s, u)
                        if on(b + 1):
                            if u == 0:
                                transposes(b + 1, 1 - s)
                            if u == 1:
                                project_q(b + 1, 1 - s)
                            if u in (2, 3):
                                project_k(b + 1, 1 - s, u - 2)
                            if u == 4:
                                project_v(b + 1, 1 - s, (0, 1), 4)
                            if u == 5:
                                project_v(b + 1, 1 - s, (2,), 5)
                        if u == 0 and on(b - 2):
                            project_o(b - 2)
                        if 1 <= u <= HG and on(b - 1):
                            values(b - 1, 1 - s, u - 1)

                pe.wait_ge(w_loaded, 16 * NW)
                pe.wait_ge(wo_loaded, 16 * H)
                pe.wait_ge(scaled, 3)
                pipeline(pe, step, 2, 2, first=4)


def clip(n):
    return min(max(n, 0), B) if isinstance(n, int) else n


RING1 = ((("norm_x", 1), ("turn_main", -3), ("key_aux0", 1), ("value_aux01", 0), ("turn_mix", -3)),
         (("turn_max", -1), ("query_key", 1), ("turn_aux", -3), ("key_aux1", 1), ("value_aux2", 0), ("out", -3)))


def ring1(t, name):
    for bank, order in enumerate(RING1):
        names = [n for n, _ in order]
        if name in names:
            before = clip(t + order[0][1])
            for _, off in order[1:]:
                before = before + clip(t + off)
            return bank, before + sum(on(t + off) for _, off in order[:names.index(name)])


def attend1(nc, consts, x_in, x_out, ctxT, Wqkv, bqkv, Wqkv_a, bqkv_a, Wo, bo, g):
    ident, mhalf, tanhg = consts
    with ExitStack() as ctx:
        m = Pool(nc, ctx, "at1")
        ctx.callback(m.close)
        N = 3
        KEYS = T + S
        UNITS = 8
        LAG = 3
        HU = H // 2
        AUGMENTED = STACK + 2
        TILES = [(0, T, 0)] + [(T + s0, r, 1) for s0, r in CHUNKS]
        CLAMP = 60000.0

        def slots(name, shape, dt=F32):
            return [m.sb(f"{name}{i}", shape, dt) for i in range(N)]

        w = m.sb("wqkv", [P, KC, 3 * D])
        wa = m.sb("wkv_aux", [P, KC, 2 * D])
        wo = m.sb("wo", [P, KC, D])
        bqk, bka = m.sb("bqk", [P, 2 * KC]), m.sb("bka", [P, KC])
        bvb, bvab, bob = m.sb("bv", [P, D]), m.sb("bv_aux", [P, D]), m.sb("bo", [P, D])
        gate, omgate, gexp = m.sb("gate", [P, H]), m.sb("omgate", [P, H]), m.sb("gexp", [P, H])
        ones = m.sb("ones", [1, H * S], F16)
        ctxt, xin, xres = slots("ctx", [P, KC, S]), slots("xin", [T, D]), slots("xres", [T, D])
        xout, xhat, xT = slots("xout", [T, D]), slots("xhat", [T, D]), slots("xT", [P, KC, T])
        qkparts = m.sb("qkparts", [P, 2, 2 * KC, T], F16)
        kaparts = m.sb("kaparts", [P, 2, KC, S], F16)
        qst, kst = slots("qst", [AUGMENTED, H, T], F16), slots("kst", [AUGMENTED, H, KEYS], F16)
        vm, va = slots("vm", [T, H, 32]), slots("va", [P, NJ, H, 32])
        negmax = slots("negmax", [T, 2 * H])
        shift = m.sb("shift", [2 * H, T], F16)
        probs = [m.sb(f"probs{i}", [P, HU * T]) for i in range(2)]
        osb = [slots("om", [P, HG * T]), slots("oa", [P, HG * T])]
        rden = m.sb("rden", [T, 2 * H])
        mixed = [m.sb(f"mixed{i}", [T, D]) for i in range(2)]
        mix, mixT = m.sb("mix", [T, D]), m.sb("mixT", [P, KC, T])
        qkd = nc.dram_tensor("at1_qkd", (N, 2, 2 * D, T), F16).ap()
        kad = nc.dram_tensor("at1_kad", (N, 2, D, S), F16).ap()
        ps_q = m.ps("by_query", [P, 2, 512])
        ps_k = m.ps("by_key", [P, 2, 512])
        ps_r = m.ps("ring", [P, 2, 512])
        ps_o = m.ps("o", [P, 2, 512])
        ln = Norm(m, mhalf)
        w_loaded, gexp_ready, scaled, filled, ones_set = (m.sem(n) for n in ("w_loaded", "gexp_ready", "scaled", "filled", "ones_set"))
        x_loaded, ctx_loaded, res_loaded, res_ready = (m.sem(n) for n in ("x_loaded", "ctx_loaded", "res_loaded", "res_ready"))
        xhat_ready = m.sem("xhat_ready")
        ring_ready = [m.sem(f"ring_ready{i}") for i in range(2)]
        ring_free = [m.sem(f"ring_free{i}") for i in range(2)]
        high_ready, qk_split, ka_split = m.sem("high_ready"), m.sem("qk_split"), m.sem("ka_split")
        qk_saved, ka_saved = m.sem("qk_saved"), m.sem("ka_saved")
        qk_stacked, ka_stacked = m.sem("qk_stacked"), m.sem("ka_stacked")
        by_query_ready, max_done = m.sem("by_query_ready"), m.sem("max_done")
        shift_ready, shift_stacked = m.sem("shift_ready"), m.sem("shift_stacked")
        by_key_ready, exp_done, pv_done = m.sem("by_key_ready"), m.sem("exp_done"), m.sem("pv_done")
        o_taken = [m.sem("om_taken"), m.sem("oa_taken")]
        rden_ready, mixed_ready, mix_ready = m.sem("rden_ready"), m.sem("mixed_ready"), m.sem("mix_ready")
        x_ready, x_stored, sp_turns = m.sem("x_ready"), m.sem("x_stored"), m.sem("sp_turns")
        NW = 9
        NF = 3 + 4

        def exp_unit(i):
            return (-1, i - LAG) if i >= LAG else (-2, i + UNITS - LAG)

        def sum_unit(i):
            return (-1, i - LAG - 1) if i > LAG else (-2, i + UNITS - LAG - 1)

        def slot_of(phase):
            return lambda off: (phase + off) % N

        with nc.Block() as block:
            @block.sync
            def _(sp):
                def hold(sem, value):
                    need(sp, sem, value)
                    sp.sem_inc(sp_turns, 1)

                def load_inputs(b, s):
                    hold(xhat_ready, b - 2)
                    hold(x_loaded, b * 16)
                    sp.dma_start(xin[s][:, :], x_in[b]).then_inc(x_loaded, 16)

                def load_context(b, s):
                    bank, n = ring1(b - 3, "value_aux2")
                    need_ring = n + 1 if not isinstance(b, int) or b >= 3 else 0
                    hold(ring_ready[bank], need_ring)
                    hold(ctx_loaded, b * 16)
                    sp.dma_start(ctxt[s][:, :, :], ctxT[b].rearrange("(c p) s -> p c s", p=P)).then_inc(ctx_loaded, 16)

                def stack(b, s):
                    hold(by_key_ready, (b - 2) * UNITS)
                    hold(qk_split, (b + 1) * 2 * KC)
                    sp.dma_start(qkd[s].rearrange("s (c p) n -> p s c n", p=P)[:, 0], qkparts[:, 0]).then_inc(qk_saved, 16)
                    sp.dma_start(qkd[s].rearrange("s (c p) n -> p s c n", p=P)[:, 1], qkparts[:, 1]).then_inc(qk_saved, 16)
                    hold(qk_saved, (b + 1) * 32)
                    hold(qk_stacked, b * 16 * 2 * PARTS)
                    rd = qkd[s].rearrange("s (w h d) n -> s w d h n", d=DH, w=2)
                    for r in range(PARTS):
                        rows = slice(r * DH, (r + 1) * DH)
                        sp.dma_start(qst[s][rows, :, :], rd[Q_PARTS[r], 0]).then_inc(qk_stacked, 16)
                        sp.dma_start(kst[s][rows, :, 0:T], rd[K_PARTS[r], 1]).then_inc(qk_stacked, 16)
                    hold(ka_split, (b + 1) * KC)
                    wr, rd = stack_views(kad, s)
                    for i in range(2):
                        sp.dma_start(wr[:, i], kaparts[:, i]).then_inc(ka_saved, 16)
                    hold(ka_saved, (b + 1) * 32)
                    hold(ka_stacked, b * 16 * PARTS)
                    for r in range(PARTS):
                        sp.dma_start(kst[s][r * DH:(r + 1) * DH, :, T:KEYS], rd[K_PARTS[r]]).then_inc(ka_stacked, 16)

                def stack_shift(b, s):
                    hold(shift_ready, b + 1)
                    hold(shift_stacked, b * 32)
                    for i in range(2):
                        sp.dma_start(qst[s][STACK + i:STACK + i + 1, :, :], shift[i * H:(i + 1) * H, :]).then_inc(shift_stacked, 16)

                def step(t, phase):
                    s = slot_of(phase)
                    if on(t - 1):
                        stack_shift(t - 1, s(-1))
                    if on(t - 2):
                        hold(x_ready, t - 4)
                        hold(res_loaded, (t - 2) * 16)
                        sp.dma_start(xres[s(-2)][:, :], x_in[t - 2]).then_inc(res_loaded, 16)
                    if on(t + 2):
                        load_inputs(t + 2, s(2))
                        load_context(t + 2, s(2))
                    if on(t + 1):
                        stack(t + 1, s(1))
                    if on(t - 4):
                        hold(x_ready, t - 3)
                        hold(x_stored, (t - 4) * 16)
                        sp.dma_start(x_out[t - 4], xout[s(-4)][:, :]).then_inc(x_stored, 16)

                sp.dma_start(w[:, :, :], Wqkv.rearrange("(c p) n -> p c n", p=P)).then_inc(w_loaded, 16)
                sp.dma_start(wa[:, :, :], Wqkv_a.rearrange("(c p) n -> p c n", p=P)[:, :, D:3 * D]).then_inc(w_loaded, 16)
                sp.dma_start(wo[:, :, :], Wo.rearrange("(c p) n -> p c n", p=P)).then_inc(w_loaded, 16)
                with nc.allow_non_contiguous_dma("one bias a partition"):
                    sp.dma_start(bqk[:, :], bqkv[0:2 * D].rearrange("(c p) -> p c", p=P)).then_inc(w_loaded, 16)
                    sp.dma_start(bka[:, :], bqkv_a[D:2 * D].rearrange("(c p) -> p c", p=P)).then_inc(w_loaded, 16)
                for tile, src in ((bvb, bqkv[2 * D:3 * D]), (bvab, bqkv_a[2 * D:3 * D]), (bob, bo), (gexp, g)):
                    sp.dma_start(tile[:, :], src.partition_broadcast(P)).then_inc(w_loaded, 16)
                sp.wait_ge(filled, NF)
                for i in range(N):
                    sp.dma_start(kst[i][STACK:STACK + 1, :, 0:T],
                                 ones[:, 0:H * T].rearrange("p (h k) -> p h k", h=H)).then_inc(ones_set, 16)
                    sp.dma_start(kst[i][STACK + 1:STACK + 2, :, T:KEYS],
                                 ones[:, :].rearrange("p (h k) -> p h k", h=H)).then_inc(ones_set, 16)
                pipeline(sp, step, 2, 4, N)
                sp.wait_ge(x_stored, 16 * B)

            @block.gpsimd
            def _(pool):
                def step(t, phase):
                    s = slot_of(phase)
                    if on(t + 2):
                        ln.power(pool, t + 2)
                    if on(t - 2):
                        b = t - 2
                        pool.wait_ge(res_loaded, (b + 1) * 16)
                        pool.tensor_tensor(xres[s(-2)][:, :], xres[s(-2)][:, :], bob[0:T, :], ALU.add).then_inc(res_ready, 1)

                pool.wait_ge(scaled, 9)
                pipeline(pool, step, 2, 4, N)

            @block.vector
            def _(dve):
                def take(t, name):
                    bank, n = ring1(t, name)
                    dve.wait_ge(ring_ready[bank], n + 1)
                    return ps_r[:, bank, :], ring_free[bank]

                def norm(b, s):
                    dve.wait_ge(x_loaded, (b + 1) * 16)
                    ln.moments(dve, b, xin[s][:, :])
                    ln.newton(dve, b)
                    if not isinstance(b, int) or b >= N:
                        bank, n = ring1(b - 1 - N, "norm_x")
                        dve.wait_ge(ring_ready[bank], n + 1)
                    ln.apply(dve, b, xhat[s][:, :], xin[s][:, :]).then_inc(xhat_ready, 1)

                def low(bank, parts, i, bias, at, done):
                    dve.wait_ge(high_ready, at)
                    return dve.scalar_tensor_tensor(out=parts[:, 1, i, :], in0=bank, scalar=bias[:, i:i + 1],
                                                    in1=parts[:, 0, i, :], op0=ALU.add, op1=ALU.subtract).then_inc(done, 1)

                def take_query_key(t):
                    b = t + 1
                    bank, free = take(t, "query_key")
                    for i in range(2 * KC):
                        low(bank[:, i * T:(i + 1) * T], qkparts, i, bqk, b * 6 + 2 * KC, qk_split)
                    dve.wait_ge(qk_split, (b + 1) * 2 * KC)
                    dve.sem_inc(free, 1)

                def take_key_aux(t, i):
                    b = t + 1
                    bank, free = take(t, f"key_aux{i}")
                    low(bank[:, 0:S], kaparts, i, bka, b * 6 + 5 + i, ka_split)
                    dve.wait_ge(ka_split, b * KC + i + 1)
                    dve.sem_inc(free, 1)

                def maxima(b, s, i):
                    dve.wait_ge(by_query_ready, b * UNITS + i + 1)
                    if i == 0 and (not isinstance(b, int) or b >= N):
                        bank, n = ring1(b - N + 1, "turn_max")
                        dve.wait_ge(ring_ready[bank], n + 1)
                    dve.tensor_reduce(negmax[s][:, 2 * i:2 * i + 2], ps_q[0:T, :, 0:T], AX, ALU.max, negate=True)
                    dve.tensor_reduce(negmax[s][:, H + 2 * i:H + 2 * i + 2], ps_q[0:T, :, T:KEYS], AX, ALU.max,
                                      negate=True).then_inc(max_done, 1)

                def take_max(t):
                    bank, free = take(t, "turn_max")
                    need(dve, shift_stacked, (t - 1) * 32)
                    dve.tensor_scalar(shift[:, :], bank[0:2 * H, 0:T], CLAMP, -CLAMP, ALU.min, ALU.max).then_inc(shift_ready, 1)
                    dve.wait_ge(shift_ready, t)
                    dve.sem_inc(free, 1)

                def take_values(t, s):
                    bank, free = take(t, "value_aux01")
                    need(dve, pv_done, (t - 2) * UNITS)
                    for j in (0, 1):
                        r = CHUNKS[j][1]
                        last = dve.tensor_tensor(va[s][0:r, j, :, 0:DH], heads(bank[0:r, j * D:(j + 1) * D]),
                                                 heads(bvab[0:r, :]), ALU.add)
                    last.then_inc(free, 1)

                def take_values2(t, s):
                    bank, free = take(t, "value_aux2")
                    r = CHUNKS[2][1]
                    dve.tensor_tensor(va[s][0:r, 2, :, 0:DH], heads(bank[0:r, 0:D]), heads(bvab[0:r, :]), ALU.add)
                    dve.tensor_tensor(vm[s][:, :, 0:DH], heads(bank[0:T, D:2 * D]), heads(bvb[0:T, :]), ALU.add).then_inc(free, 1)

                def normalize(t, i):
                    b = t - 3
                    bank, free = take(t, ("turn_main", "turn_aux")[i])
                    by_head = bank[0:T, :].rearrange("p (h e) -> p h e", e=32)
                    need(dve, mix_ready, b)
                    dve.reciprocal(rden[:, i * H:(i + 1) * H], by_head[:, :, DH]).then_inc(rden_ready, 1)
                    dve.wait_ge(rden_ready, b * 2 + i + 1)
                    dve.tensor_tensor(heads(mixed[i][:, :]), by_head[:, :, 0:DH],
                                      rden[:, i * H:(i + 1) * H].unsqueeze(2).to_broadcast([T, H, DH]), ALU.mult).then_inc(free, 1)
                    if i == 1:
                        dve.wait_ge(free, ring1(t, "turn_aux")[1] + 1)
                        if not isinstance(b, int) or b >= 1:
                            dve.wait_ge(ring_ready[0], ring1(t - 1, "turn_mix")[1] + 1)
                        dve.tensor_tensor(mix[:, :], mixed[0][:, :], mixed[1][:, :], ALU.add).then_inc(mix_ready, 1)

                def residual(t, s):
                    b = t - 3
                    bank, free = take(t, "out")
                    dve.wait_ge(res_ready, b + 1)
                    need(dve, x_stored, (b - 2) * 16)
                    dve.scalar_tensor_tensor(out=xout[s][:, :], in0=bank[0:T, 0:D], scalar=tanhg[0:T, 0:1],
                                             in1=xres[s][:, :], op0=ALU.mult, op1=ALU.add).then_inc(x_ready, 1)
                    dve.wait_ge(x_ready, b + 1)
                    dve.sem_inc(free, 1)

                def step(t, phase):
                    s = slot_of(phase)
                    for i in range(UNITS):
                        if i == 0 and on(t - 1):
                            take_max(t)
                        if on(t):
                            maxima(t, s(0), i)
                        if i == 1 and on(t - 3):
                            normalize(t, 0)
                        if i == 1 and on(t + 1):
                            take_query_key(t)
                        if i == 2 and on(t + 1):
                            take_key_aux(t, 0)
                        if i == 2 and on(t - 3):
                            normalize(t, 1)
                        if i == 3 and on(t + 1):
                            take_key_aux(t, 1)
                        if i == 4 and on(t):
                            take_values(t, s(0))
                        if i == 5 and on(t):
                            take_values2(t, s(0))
                        if i == 6 and on(t - 3):
                            residual(t, s(-3))
                        if i == 7 and on(t + 2):
                            norm(t + 2, s(2))

                dve.memset(ones[:, :], 1.0).then_inc(filled, 1)
                for i in range(N):
                    dve.memset(kst[i][STACK:AUGMENTED, :, :], 0.0).then_inc(filled, 1)
                    dve.memset(vm[i][:, :, DH:32], 0.0)
                    dve.memset(va[i][:, :, :, DH:32], 0.0)
                dve.memset(gate[:, :], 1.0).then_inc(filled, 1)
                dve.wait_ge(filled, 5)
                for i in range(N):
                    dve.memset(vm[i][:, :, DH:DH + 1], 1.0)
                    last = dve.memset(va[i][:, :, :, DH:DH + 1], 1.0)
                last.then_inc(filled, 2)
                dve.wait_ge(w_loaded, 16 * NW)
                dve.tensor_scalar(w[:, :, 0:D], w[:, :, 0:D], DH ** -0.5, None, ALU.mult).then_inc(scaled, 1)
                dve.tensor_scalar(bqk[:, 0:KC], bqk[:, 0:KC], DH ** -0.5, None, ALU.mult).then_inc(scaled, 1)
                dve.tensor_scalar(bob[:, :], bob[:, :], tanhg[:, 0:1], None, ALU.mult).then_inc(scaled, 1)
                dve.wait_ge(gexp_ready, 1)
                dve.tensor_scalar(omgate[:, :], gexp[:, :], 1.0, None, ALU.add).then_inc(scaled, 1)
                dve.wait_ge(scaled, 4)
                dve.reciprocal(gate[:, :], omgate[:, :]).then_inc(scaled, 1)
                dve.wait_ge(scaled, 5)
                dve.tensor_scalar(omgate[:, :], gate[:, :], -1.0, 1.0, ALU.mult, ALU.add)
                dve.tensor_tensor(heads(bvab[:, :]), heads(bvab[:, :]), gate[:, :].unsqueeze(2).to_broadcast([P, H, DH]),
                                  ALU.mult).then_inc(scaled, 1)
                dve.wait_ge(scaled, 6)
                dve.tensor_tensor(heads(bvb[:, :]), heads(bvb[:, :]), omgate[:, :].unsqueeze(2).to_broadcast([P, H, DH]),
                                  ALU.mult).then_inc(scaled, 1)
                for c in range(KC):
                    dve.tensor_tensor(heads(w[:, c, 2 * D:3 * D]), heads(w[:, c, 2 * D:3 * D]),
                                      omgate[:, :].unsqueeze(2).to_broadcast([P, H, DH]), ALU.mult)
                    last = dve.tensor_tensor(heads(wa[:, c, D:2 * D]), heads(wa[:, c, D:2 * D]),
                                             gate[:, :].unsqueeze(2).to_broadcast([P, H, DH]), ALU.mult)
                last.then_inc(scaled, 2)
                dve.wait_ge(scaled, 9)
                pipeline(dve, step, 2, 4, N)

            @block.scalar
            def _(act):
                def take(t, name):
                    bank, n = ring1(t, name)
                    act.wait_ge(ring_ready[bank], n + 1)
                    return ps_r[:, bank, :], ring_free[bank]

                def take_x(t, s):
                    bank, free = take(t, "norm_x")
                    act.activation(xT[s][:, :, :], bank[:, 0:KC * T].rearrange("p (c t) -> p c t", c=KC), ACT.Copy).then_inc(free, 1)

                def high(bank, parts, i, bias):
                    act.activation(parts[:, 0, i, :], bank, ACT.Identity, bias=bias[:, i:i + 1]).then_inc(high_ready, 1)

                def exponents(b, k, s):
                    n = b * UNITS + k
                    r = TILES[k // 2][1]
                    act.wait_ge(by_key_ready, n + 1)
                    need(act, pv_done, n - 1)
                    act.activation(probs[k % 2][0:r, :].rearrange("p (a n) -> p a n", a=2),
                                   ps_k[0:r, :, 0:HU // 2 * T], ACT.Exp).then_inc(exp_done, 1)

                def take_o(b, s, i):
                    act.wait_ge(pv_done, b * UNITS + (2, UNITS)[i])
                    if not isinstance(b, int) or b >= N:
                        bank, n = ring1(b, ("turn_main", "turn_aux")[i])
                        act.wait_ge(ring_ready[bank], n + 1)
                    act.activation(osb[i][s][:, :], ps_o[:, i, 0:HG * T], ACT.Copy).then_inc(o_taken[i], 1)

                def step(t, phase):
                    s = slot_of(phase)
                    for i in range(UNITS):
                        off, k = exp_unit(i)
                        b = t + off
                        if i == 4 and on(t - 2):
                            take_o(t - 2, s(-2), 1)
                        if i == 6 and on(t - 1):
                            take_o(t - 1, s(-1), 0)
                        if i == 0 and on(t + 1):
                            take_x(t, s(1))
                        if i == 1 and on(t + 1):
                            bank, _ = take(t, "query_key")
                            need(act, qk_saved, (t + 1) * 32)
                            for c in range(2 * KC):
                                high(bank[:, c * T:(c + 1) * T], qkparts, c, bqk)
                        if i in (2, 3) and on(t + 1):
                            bank, _ = take(t, f"key_aux{i - 2}")
                            need(act, ka_saved, (t + 1) * 32)
                            high(bank[:, 0:S], kaparts, i - 2, bka)
                        if i == 5 and on(t - 3):
                            bank, free = take(t, "turn_mix")
                            act.activation(mixT[:, :, :], bank[:, 0:KC * T].rearrange("p (c t) -> p c t", c=KC), ACT.Copy).then_inc(free, 1)
                        if on(b):
                            exponents(b, k, s)

                act.wait_ge(w_loaded, 16 * NW)
                act.activation(gexp[:, :], gexp[:, :], ACT.Exp, scale=-1.0).then_inc(gexp_ready, 1)
                pipeline(act, step, 2, 4, N)

            @block.tensor
            def _(pe):
                def into(t, name):
                    bank, n = ring1(t, name)
                    need(pe, ring_free[bank], n)
                    return ps_r[:, bank, :], ring_ready[bank]

                def turn_max(t, s):
                    bank, ready = into(t, "turn_max")
                    pe.wait_ge(max_done, t * UNITS)
                    pe.transpose(bank[0:2 * H, 0:T], negmax[s][:, :], ident[0:T, 0:T]).then_inc(ready, 1)

                def norm_x(t, s):
                    bank, ready = into(t, "norm_x")
                    pe.wait_ge(xhat_ready, t + 2)
                    for c in range(KC):
                        last = pe.transpose(bank[:, c * T:(c + 1) * T], xhat[s][:, c * P:(c + 1) * P], ident[0:T, 0:T])
                    last.then_inc(ready, 1)

                def query_key(t, s):
                    bank, ready = into(t, "query_key")
                    b0, n0 = ring1(t, "norm_x")
                    pe.wait_ge(ring_free[b0], n0 + 1)
                    for i in range(2 * KC):
                        for c in range(KC):
                            last = pe.matmul(bank[:, i * T:(i + 1) * T], w[:, c, i * P:(i + 1) * P], xT[s][:, c, :],
                                             start=(c == 0), stop=(c == KC - 1))
                    last.then_inc(ready, 1)

                def key_aux(t, s, i):
                    bank, ready = into(t, f"key_aux{i}")
                    if i == 0:
                        pe.wait_ge(ctx_loaded, (t + 2) * 16)
                    for c in range(KC):
                        last = pe.matmul(bank[:, 0:S], wa[:, c, i * P:(i + 1) * P], ctxt[s][:, c, :],
                                         start=(c == 0), stop=(c == KC - 1))
                    last.then_inc(ready, 1)

                def value(bank, at, r, lhs, rhs):
                    for c in range(KC):
                        last = pe.matmul(bank[0:r, at:at + D], lhs(c), rhs(c), start=(c == 0), stop=(c == KC - 1))
                    return last

                def values01(t, s):
                    bank, ready = into(t, "value_aux01")
                    for j in (0, 1):
                        s0, r = CHUNKS[j]
                        last = value(bank, j * D, r, lambda c: ctxt[s][:, c, s0:s0 + r], lambda c: wa[:, c, D:2 * D])
                    last.then_inc(ready, 1)

                def values2(t, s):
                    bank, ready = into(t, "value_aux2")
                    s0, r = CHUNKS[2]
                    value(bank, 0, r, lambda c: ctxt[s][:, c, s0:s0 + r], lambda c: wa[:, c, D:2 * D])
                    value(bank, D, T, lambda c: xT[s][:, c, :], lambda c: w[:, c, 2 * D:3 * D]).then_inc(ready, 1)

                def by_query(b, s, i):
                    if i == 0:
                        pe.wait_ge(qk_stacked, (b + 1) * 16 * 2 * PARTS)
                        pe.wait_ge(ka_stacked, (b + 1) * 16 * PARTS)
                    need(pe, max_done, b * UNITS + i)
                    for a in range(2):
                        h = 2 * i + a
                        last = pe.matmul(ps_q[0:T, a, 0:KEYS], qst[s][0:STACK, h, :], kst[s][0:STACK, h, :], start=True, stop=True)
                    last.then_inc(by_query_ready, 1)

                def by_key(b, s, k):
                    k0, r, _ = TILES[k // 2]
                    if k == 0:
                        pe.wait_ge(shift_stacked, (b + 1) * 32)
                    need(pe, exp_done, b * UNITS + k)
                    for hh in range(HU):
                        h = (k % 2) * HU + hh
                        last = pe.matmul(ps_k[0:r, hh // 4, (hh % 4) * T:(hh % 4 + 1) * T], kst[s][:, h, k0:k0 + r],
                                         qst[s][:, h, :], start=True, stop=True)
                    last.then_inc(by_key_ready, 1)

                def sum_up(b, s, k):
                    j, half = k // 2, k % 2
                    _, r, aux = TILES[j]
                    pe.wait_ge(exp_done, b * UNITS + k + 1)
                    if k in (0, 2):
                        need(pe, o_taken[aux], b)
                    for hh in range(HU):
                        h = half * HU + hh
                        g, c = h // CT, h % CT
                        vals = va[s][0:r, j - 1, h, :] if aux else vm[s][:, h, :]
                        last = pe.matmul(ps_o[32 * c:32 * c + 32, aux, g * T:(g + 1) * T], vals,
                                         probs[k % 2][0:r, hh * T:(hh + 1) * T],
                                         start=(j in (0, 1) and h < CT), stop=(j in (0, NJ)), skip_group_check=True)
                    last.then_inc(pv_done, 1)

                def turn_sums(t, s, i):
                    bank, ready = into(t, ("turn_main", "turn_aux")[i])
                    pe.wait_ge(o_taken[i], t - 2)
                    for g_ in range(HG):
                        last = pe.transpose(bank[0:T, g_ * P:(g_ + 1) * P], osb[i][s][:, g_ * T:(g_ + 1) * T], ident[:, :])
                    last.then_inc(ready, 1)

                def turn_mix(t):
                    bank, ready = into(t, "turn_mix")
                    pe.wait_ge(mix_ready, t - 2)
                    for c in range(KC):
                        last = pe.transpose(bank[:, c * T:(c + 1) * T], mix[:, c * P:(c + 1) * P], ident[0:T, 0:T])
                    last.then_inc(ready, 1)

                def project_out(t):
                    bank, ready = into(t, "out")
                    b0, n0 = ring1(t, "turn_mix")
                    pe.wait_ge(ring_free[b0], n0 + 1)
                    value(bank, 0, T, lambda c: mixT[:, c, :], lambda c: wo[:, c, :]).then_inc(ready, 1)

                def step(t, phase):
                    s = slot_of(phase)
                    for i in range(UNITS):
                        if i == 0 and on(t - 1):
                            turn_max(t, s(-1))
                        if on(t):
                            by_query(t, s(0), i)
                        off, k = exp_unit(i)
                        b = t + off
                        if on(b):
                            by_key(b, s(off), k)
                        off, k = sum_unit(i)
                        b = t + off
                        if on(b):
                            sum_up(b, s(off), k)
                        if i == 0 and on(t + 1):
                            norm_x(t, s(1))
                        if i == 1 and on(t - 3):
                            turn_sums(t, s(-3), 0)
                        if i == 1 and on(t + 1):
                            query_key(t, s(1))
                        if i == 2 and on(t + 1):
                            key_aux(t, s(1), 0)
                        if i == 2 and on(t - 3):
                            turn_sums(t, s(-3), 1)
                        if i == 3 and on(t + 1):
                            key_aux(t, s(1), 1)
                        if i == 4 and on(t):
                            values01(t, s(0))
                        if i == 5 and on(t):
                            values2(t, s(0))
                        if i == 5 and on(t - 3):
                            turn_mix(t)
                        if i == 6 and on(t - 3):
                            project_out(t)

                pe.wait_ge(scaled, 9)
                pe.wait_ge(filled, NF)
                pe.wait_ge(ones_set, 16 * 2 * N)
                pipeline(pe, step, 2, 4, N)


class Chain:

    def __init__(self, eng, sem):
        self.eng, self.sem, self.n = eng, sem, 0

    def __call__(self, instruction):
        instruction.then_inc(self.sem, 1)
        self.n += 1
        self.eng.wait_ge(self.sem, self.n)


def rounds(eng, step, lead, tail, count, n=3):
    def placed(phase, rnd):
        return lambda off: ((phase + off) % n, rnd + (phase + off) // n)

    lo, hi = -(-tail // n), (count - lead) // n
    for t in range(-lead, lo * n):
        step(t, placed(t % n, t // n))
    with eng.Fori(lo, hi) as rnd:
        for phase in range(n):
            step(rnd * n + phase, placed(phase, rnd))
    for t in range(hi * n, count + tail):
        step(t, placed(t % n, t // n))


def experts(nc, consts, name, x_in, x_out, router, router_b, pack1, pack2, b2, top, ff, shared):
    ident, mhalf, tanhg = consts
    with ExitStack() as ctx:
        m = Pool(nc, ctx, name)
        ctx.callback(m.close)
        N = 3
        E = router.shape[1]
        TOK = B * T
        TILES = (TOK * top + E * (P - 1)) // P
        ALL = -(-TOK // P)
        FIRST = 2 * ALL if shared else 0
        NT = FIRST + TILES
        WAYS = top + (2 if shared else 0)
        FC = ff // P
        UNIT = 4
        U = FC // UNIT
        B1 = KC * ff
        GB, NG = 4, B // 4
        CB = top * B
        AUX_ROW = TOK * top
        PAD_ROW = AUX_ROW + FIRST * P
        BIG = -3.0e38

        xs, xhat = m.sb("x", [T, B, D]), m.sb("xhat", [T, B, D])
        xhd = nc.dram_tensor(f"{name}_normed", (TOK, D), F32).ap()
        ways = nc.dram_tensor(f"{name}_results", (PAD_ROW + TILES * P, D), F32).ap()
        stats, mv = m.sb("stats", [T, B, 6]), m.sb("mv", [T, B, 2])
        var, r0, newt, rstd = (m.sb(n, [T, B]) for n in ("var", "r0", "newt", "rstd"))
        rw, rb = m.sb("router", [P, KC, E]), m.sb("router_b", [P, E])
        xTr = [m.sb(f"xTr{i}", [P, 2, KC, T]) for i in range(2)]
        tri, ones = m.sb("tri", [T, T]), m.sb("ones", [T, P])
        cols = m.sb("cols", [P, P])
        cols16 = m.sb("cols16", [P, P], F16)
        steps_of_p = m.sb("steps_of_p", [P, ALL])
        rev = m.sb("rev", [P, E])
        before = m.sb("before", [P, E, E])
        tok = m.sb("tok", [T, B])
        pad_row = m.sb("pad_row", [P, TILES])
        sel, key, mask = (m.sb(n, [T, B, E]) for n in ("sel", "key", "mask"))
        rowmax = m.sb("rowmax", [T, B])
        value = m.sb("value", [T, top, B])
        pick = m.sb("pick", [T, top, B, E])
        gates = m.sb("gates", [T, top, B])
        norm_sum, norm_rec = m.sb("norm_sum", [T, B]), m.sb("norm_rec", [T, B])
        picked = m.sb("picked", [T, top, B, E])
        rank, first = m.sb("rank", [T, CB]), m.sb("first", [T, CB])
        above = m.sb("above", [T, CB, ALL])
        tile_of, lane_of = m.sb("tile_of", [T, CB]), m.sb("lane_of", [T, CB])
        lane_of16 = m.sb("lane_of16", [T, CB], F16)
        full = m.sb("full", [P, E, ALL])
        tiles_of, start, end = (m.sb(n, [P, E]) for n in ("tiles_of", "start", "end"))
        below = m.sb("below", [P, E, E])
        in_tile = m.sb("in_tile", [T, CB, TILES], F16)
        tile_vals = m.sb("tile_vals", [T, CB, 2, TILES], F16)
        in_lane = m.sb("in_lane", [T, CB, P], F16)
        passed = m.sb("passed", [1, TILES, E])
        expert_f = m.sb("expert_f", [1, TILES])
        expert_of = m.sb("expert_of", [1, NT], I32)
        row_f, empty = m.sb("row_f", [P, TILES]), m.sb("empty", [P, TILES])
        aux_f = m.sb("aux_f", [P, max(FIRST, 1)])
        from_row, to_row = m.sb("from_row", [P, NT], U32), m.sb("to_row", [P, NT], U32)
        def slots(what, shape, dt=F32):
            return [m.sb(f"{what}{i}", shape, dt) for i in range(N)]

        w1, w2, b2t = slots("w1_", [P, B1 + FC]), slots("w2_", [P, FC * D]), slots("b2_", [P, D])
        gi, si = slots("from", [P, 1], U32), slots("to", [P, 1], U32)
        xt, xT, hT, yt = slots("xt", [P, D]), slots("xT", [P, KC, P]), slots("hT", [P, FC, P]), slots("yt", [P, D])
        parts = [m.sb(f"ways{i}", [T, GB, D]) for i in range(2)]
        ps_h = m.ps("h", [P, N, 512])
        ps_y = m.ps("y", [P, N, 512])
        ps_t = m.ps("t", [P, 2, 512])

        x_in_done = [m.sem(f"x_loaded{g}") for g in range(NG)]
        w_loaded, consts_set, half_set = m.sem("w_loaded"), m.sem("consts_set"), m.sem("half_set")
        stats_ready, root_ready, newton_step = m.sem("stats_ready"), m.sem("root_ready"), m.sem("newton_step")
        xhat_ready, xhat_saved = m.sem("xhat_ready"), m.sem("xhat_saved")
        turned, turned_taken, logits_ready = m.sem("turned"), m.sem("turned_taken"), m.sem("logits_ready")
        route_step, exp_in, exp_out = m.sem("route_step"), m.sem("exp_in"), m.sem("exp_out")
        mask_ready, ranks_ready, onehots_ready, table_ready = (m.sem(n) for n in ("mask_ready", "ranks_ready", "onehots_ready", "table_ready"))
        expert_ready, rows_ready = m.sem("expert_ready"), m.sem("rows_ready")
        w1_in, w2_in = [m.sem(f"w1_in{i}") for i in range(N)], [m.sem(f"w2_in{i}") for i in range(N)]
        gathered, scattered = [m.sem(f"gathered{i}") for i in range(N)], [m.sem(f"scattered{i}") for i in range(N)]
        from_ready, to_ready = m.sem("from_ready"), m.sem("to_ready")
        xT_ready, xT_taken, h_ready, h_taken = (m.sem(n) for n in ("xT_ready", "xT_taken", "h_ready", "h_taken"))
        y_ready, y_taken = m.sem("y_ready"), m.sem("y_taken")
        sp_turns, pool_turns, dve_turns = m.sem("sp_turns"), m.sem("pool_turns"), m.sem("dve_turns")
        ways_in = [m.sem(f"ways_in{i}") for i in range(2)]
        added, x_stored = m.sem("added"), m.sem("x_stored")

        def col(t):
            return slice(t, t + 1) if isinstance(t, int) else bass.ds(t, 1)

        def live(t):
            return not isinstance(t, int) or 0 <= t < NT

        with nc.Block() as block:
            @block.sync
            def _(sp):
                def hold(sem, value):
                    need(sp, sem, value)
                    sp.sem_inc(sp_turns, 1)

                def expert(t):
                    return sp.value_load(expert_of[0:1, col(t)], min_val=0, max_val=pack1.shape[0] - 1)

                def load_in(t, s, rnd):
                    hold(h_ready, (t - N + 1) * U)
                    hold(h_taken, (t - N + 1) * U)
                    sp.dma_start(w1[s][:, :], pack1[bass.ds(expert(t), 1)].rearrange("o p n -> p (o n)")).then_inc(w1_in[s], 16)

                def load_out(t, s, rnd):
                    hold(y_ready, t - N + 1)
                    hold(y_taken, t - N + 1)
                    e = expert(t)
                    sp.dma_start(w2[s][:, :], pack2[bass.ds(e, 1)].rearrange("o p n -> p (o n)")).then_inc(w2_in[s], 16)
                    sp.dma_start(b2t[s][:, :], b2[bass.ds(e, 1)].rearrange("o d -> (o d)").partition_broadcast(P)).then_inc(w2_in[s], 16)

                def step(t, at):
                    if live(t + 3):
                        load_in(t + 3, *at(3))
                    if live(t + 2):
                        load_out(t + 2, *at(2))

                def store(g):
                    sp.wait_ge(added, (g + 1) * WAYS * GB)
                    sp.dma_start(x_out[g * GB:(g + 1) * GB].rearrange("b t d -> t b d"),
                                 xs[:, g * GB:(g + 1) * GB, :]).then_inc(x_stored, 16)

                for g in range(NG):
                    sp.dma_start(xs[:, g * GB:(g + 1) * GB, :],
                                 x_in[g * GB:(g + 1) * GB].rearrange("b t d -> t b d")).then_inc(x_in_done[g], 16)
                sp.dma_start(rw[:, :, :], router.rearrange("(c p) e -> p c e", p=P)).then_inc(w_loaded, 16)
                if router_b is not None:
                    sp.dma_start(rb[:, :], router_b.partition_broadcast(P)).then_inc(w_loaded, 16)
                for g in range(NG):
                    sp.wait_ge(xhat_ready, (g + 1) * GB)
                    sp.dma_start(xhd[g * GB * T:(g + 1) * GB * T].rearrange("(b t) d -> t b d", t=T),
                                 xhat[:, g * GB:(g + 1) * GB, :]).then_inc(xhat_saved, 16)
                sp.wait_ge(expert_ready, 1)
                rounds(sp, step, 3, 1, NT)
                for s in range(N):
                    sp.wait_ge(scattered[s], 16 * len(range(s, NT, N)))
                for i in range(NG * WAYS):
                    g, way = i // WAYS, i % WAYS
                    row = way * TOK if way < top else AUX_ROW + (way - top) * ALL * P
                    need(sp, added, (i - 1) * GB)
                    sp.dma_start(parts[i % 2][:, :, :],
                                 ways[row + g * GB * T:row + (g + 1) * GB * T].rearrange("(b t) d -> t b d", t=T)).then_inc(ways_in[i % 2], 16)
                    if way == WAYS - 1 and g > 0:
                        store(g - 1)
                store(NG - 1)
                sp.wait_ge(x_stored, 16 * NG)

            @block.gpsimd
            def _(pool):
                def hold(sem, value):
                    need(pool, sem, value)
                    pool.sem_inc(pool_turns, 1)

                def gather(t, s, rnd):
                    hold(xT_ready, t - N + 1)
                    hold(from_ready, t + 1)
                    pool.indirect_dma_start(xt[s][:, :], None, xhd, bass.IndirectOffsetOnAxis(gi[s][:, :], 0)).then_inc(gathered[s], 16)

                def scatter(t, s, rnd):
                    hold(y_taken, t + 1)
                    hold(to_ready, t + 1)
                    pool.indirect_dma_start(ways, bass.IndirectOffsetOnAxis(si[s][:, :], 0), yt[s][:, :], None).then_inc(scattered[s], 16)

                def step(t, at):
                    if live(t + 3):
                        gather(t + 3, *at(3))
                    if live(t - 1):
                        scatter(t - 1, *at(-1))

                iota = pool.iota
                imprecise = dict(allow_small_or_imprecise_dtypes=True)
                pool.memset(ones[:, :], 1.0).then_inc(half_set, 1)
                pool.memset(before[:, :, :], 1.0).then_inc(half_set, 1)
                iota(cols[:, :], pattern=[[1, P]], base=0, channel_multiplier=0, **imprecise).then_inc(consts_set, 1)
                iota(cols16[:, :], pattern=[[1, P]], base=0, channel_multiplier=0, **imprecise).then_inc(consts_set, 1)
                iota(steps_of_p[:, :], pattern=[[P, ALL]], base=0, channel_multiplier=0, **imprecise).then_inc(consts_set, 1)
                iota(rev[:, :], pattern=[[-1, E]], base=E, channel_multiplier=0, **imprecise).then_inc(consts_set, 1)
                iota(tok[:, :], pattern=[[T, B]], base=0, channel_multiplier=1, **imprecise).then_inc(consts_set, 1)
                iota(pad_row[:, :], pattern=[[P, TILES]], base=PAD_ROW + TOK, channel_multiplier=1, **imprecise).then_inc(consts_set, 1)
                pool.wait_ge(half_set, 2)
                pool.affine_select(out=tri[:, :], in_=ones[:, 0:T], compare_op=ALU.is_gt, fill=0.0, base=0,
                                   pattern=[[1, T]], channel_multiplier=-1).then_inc(consts_set, 1)
                pool.affine_select(out=before[:, :, :], in_=before[:, :, :], compare_op=ALU.is_gt, fill=0.0, base=0,
                                   pattern=[[1, E], [-1, E]], channel_multiplier=0).then_inc(consts_set, 1)
                if shared:
                    iota(aux_f[:, :].rearrange("p (h t) -> p h t", h=2), pattern=[[0, 2], [P, ALL]], base=0, channel_multiplier=1,
                         **imprecise).then_inc(half_set, 1)
                    iota(to_row[:, 0:FIRST], pattern=[[P, FIRST]], base=AUX_ROW, channel_multiplier=1).then_inc(consts_set, 1)
                    pool.memset(expert_of[:, 0:ALL], E).then_inc(consts_set, 1)
                    pool.memset(expert_of[:, ALL:FIRST], E + 1).then_inc(consts_set, 1)
                for g in range(NG):
                    at = slice(g * GB, (g + 1) * GB)
                    pool.wait_ge(stats_ready, (g + 1))
                    pool.tensor_tensor(r0[:, at], var[:, at], mhalf[0:T, :].to_broadcast([T, GB]), ALU.pow).then_inc(root_ready, 1)
                pool.wait_ge(xhat_saved, 16 * NG)
                rounds(pool, step, 3, 1, NT)

            @block.vector
            def _(dve):
                def moments(g):
                    dve.wait_ge(x_in_done[g], 16)
                    chain = Chain(dve, newton_step)
                    chain.n = g * 6
                    for b in range(g * GB, (g + 1) * GB):
                        last = dve.bn_stats(stats[:, b, :], xs[:, b, :])
                    chain(last)
                    for b in range(g * GB, (g + 1) * GB):
                        last = dve.bn_aggr(mv[:, b, :], stats[:, b, :])
                    chain(last)
                    at = slice(g * GB, (g + 1) * GB)
                    dve.tensor_scalar(var[:, at], mv[:, at, 1], EPS, None, ALU.add).then_inc(stats_ready, 1)
                    dve.wait_ge(stats_ready, g + 1)
                    dve.wait_ge(root_ready, g + 1)
                    chain(dve.tensor_tensor(newt[:, at], r0[:, at], r0[:, at], ALU.mult))
                    chain(dve.tensor_tensor(newt[:, at], newt[:, at], var[:, at], ALU.mult))
                    chain(dve.tensor_scalar(newt[:, at], newt[:, at], -0.5, 1.5, ALU.mult, ALU.add))
                    chain(dve.tensor_tensor(rstd[:, at], r0[:, at], newt[:, at], ALU.mult))
                    for b in range(g * GB, (g + 1) * GB):
                        dve.tensor_scalar(xhat[:, b, :], xs[:, b, :], mv[:, b, 0:1], rstd[:, b:b + 1],
                                          ALU.subtract, ALU.mult).then_inc(xhat_ready, 1)

                def per_expert(ap):
                    return ap.unsqueeze(2).to_broadcast([T, B, E])

                def per_batch(ap):
                    return ap.unsqueeze(1).to_broadcast([T, B, E])

                def route():
                    then = Chain(dve, route_step)
                    dve.wait_ge(consts_set, 8 + (3 if shared else 0))
                    dve.wait_ge(logits_ready, 1)
                    logits = ps_y[0:T, 0, 0:B * E].rearrange("p (b e) -> p b e", e=E)
                    if router_b is None:
                        then(dve.tensor_copy(sel[:, :, :], logits))
                    else:
                        then(dve.tensor_tensor(key[:, :, :], logits, per_batch(rb[0:T, :]), ALU.add))
                        then(dve.tensor_reduce(rowmax[:, :], key[:, :, :], AX, ALU.max))
                        dve.tensor_tensor(key[:, :, :], key[:, :, :], per_expert(rowmax[:, :]), ALU.subtract).then_inc(exp_in, 1)
                        dve.wait_ge(exp_out, 1)
                        then(dve.tensor_reduce(norm_sum[:, :], sel[:, :, :], AX, ALU.add))
                        then(dve.reciprocal(norm_rec[:, :], norm_sum[:, :]))
                        then(dve.tensor_tensor(sel[:, :, :], sel[:, :, :], per_expert(norm_rec[:, :]), ALU.mult))
                    for k in range(top):
                        then(dve.tensor_reduce(value[:, k, :], sel[:, :, :], AX, ALU.max))
                        then(dve.tensor_tensor(key[:, :, :], sel[:, :, :], per_expert(value[:, k, :]), ALU.is_equal))
                        then(dve.tensor_tensor(key[:, :, :], key[:, :, :], per_batch(rev[0:T, :]), ALU.mult))
                        then(dve.tensor_reduce(rowmax[:, :], key[:, :, :], AX, ALU.max))
                        then(dve.tensor_tensor(pick[:, k], key[:, :, :], per_expert(rowmax[:, :]), ALU.is_equal))
                        if k < top - 1:
                            then(dve.scalar_tensor_tensor(out=sel[:, :, :], in0=pick[:, k], scalar=BIG, in1=sel[:, :, :],
                                                          op0=ALU.mult, op1=ALU.add))
                    then(dve.tensor_tensor(mask[:, :, :], pick[:, 0], pick[:, 1], ALU.add))
                    for k in range(2, top):
                        then(dve.tensor_tensor(mask[:, :, :], mask[:, :, :], pick[:, k], ALU.add))
                    dve.sem_inc(mask_ready, 1)
                    if router_b is None:
                        dve.tensor_tensor(norm_sum[:, :], value[:, 1, :], value[:, 0, :], ALU.subtract).then_inc(exp_in, 1)
                        dve.wait_ge(exp_out, 1)
                        then(dve.tensor_scalar(norm_sum[:, :], norm_rec[:, :], 1.0, None, ALU.add))
                        then(dve.reciprocal(value[:, 0, :], norm_sum[:, :]))
                        then(dve.tensor_tensor(value[:, 1, :], value[:, 0, :], norm_rec[:, :], ALU.mult))
                    then(dve.tensor_scalar(gates[:, :, :], value[:, :, :], tanhg[0:T, 0:1], None, ALU.mult))
                    dve.wait_ge(ranks_ready, 1)
                    ranks = ps_y[0:T, 1, 0:B * E].rearrange("p (b e) -> p b e", e=E)
                    counts = ps_y[:, 2, 0:E]
                    then(dve.tensor_tensor(full[:, :, :], counts.unsqueeze(2).to_broadcast([P, E, ALL]),
                                           steps_of_p[:, :].unsqueeze(1).to_broadcast([P, E, ALL]), ALU.is_gt))
                    then(dve.tensor_reduce(tiles_of[:, :], full[:, :, :], AX, ALU.add))
                    then(dve.tensor_tensor(below[:, :, :], before[:, :, :], tiles_of[:, :].unsqueeze(1).to_broadcast([P, E, E]), ALU.mult))
                    then(dve.tensor_reduce(start[:, :], below[:, :, :], AX, ALU.add))
                    then(dve.tensor_tensor(end[:, :], start[:, :], tiles_of[:, :], ALU.add))
                    then(dve.tensor_tensor(passed[:, :, :], cols[0:1, 0:TILES].unsqueeze(2).to_broadcast([1, TILES, E]),
                                           end[0:1, :].unsqueeze(1).to_broadcast([1, TILES, E]), ALU.is_ge))
                    then(dve.tensor_reduce(expert_f[:, :], passed[:, :, :], AX, ALU.add))
                    dve.tensor_scalar(expert_of[:, FIRST:NT], expert_f[:, :], float(E - 1), None, ALU.min).then_inc(expert_ready, 1)
                    for k in range(top):
                        then(dve.tensor_tensor(picked[:, k], pick[:, k], ranks, ALU.mult))
                    by_choice = picked[:, :, :, :].rearrange("p k b e -> p (k b) e")
                    then(dve.tensor_reduce(rank[:, :], by_choice, AX, ALU.add))
                    then(dve.tensor_tensor(by_choice, pick[:, :, :, :].rearrange("p k b e -> p (k b) e"),
                                           start[0:T, :].unsqueeze(1).to_broadcast([T, CB, E]), ALU.mult))
                    then(dve.tensor_reduce(first[:, :], by_choice, AX, ALU.add))
                    then(dve.tensor_tensor(above[:, :, 1:ALL], rank[:, :].unsqueeze(2).to_broadcast([T, CB, ALL - 1]),
                                           steps_of_p[0:T, 1:ALL].unsqueeze(1).to_broadcast([T, CB, ALL - 1]), ALU.is_ge))
                    then(dve.tensor_reduce(tile_of[:, :], above[:, :, 1:ALL], AX, ALU.add))
                    then(dve.scalar_tensor_tensor(out=lane_of[:, :], in0=tile_of[:, :], scalar=-float(P), in1=rank[:, :],
                                                  op0=ALU.mult, op1=ALU.add))
                    then(dve.tensor_tensor(tile_of[:, :], tile_of[:, :], first[:, :], ALU.add))
                    then(dve.tensor_tensor(in_tile[:, :, :], tile_of[:, :].unsqueeze(2).to_broadcast([T, CB, TILES]),
                                           cols[0:T, 0:TILES].unsqueeze(1).to_broadcast([T, CB, TILES]), ALU.is_equal))
                    for k in range(top):
                        of_k = slice(k * B, (k + 1) * B)
                        dve.tensor_tensor(tile_vals[:, of_k, 0, :], in_tile[:, of_k, :],
                                          tok[:, :].unsqueeze(2).to_broadcast([T, B, TILES]), ALU.mult)
                        then(dve.tensor_scalar(tile_vals[:, of_k, 1, :], in_tile[:, of_k, :], float(k + 1), None, ALU.mult))
                        dve.tensor_tensor(in_lane[:, of_k, :], lane_of[:, of_k].unsqueeze(2).to_broadcast([T, B, P]),
                                          cols[0:T, :].unsqueeze(1).to_broadcast([T, B, P]), ALU.is_equal).then_inc(onehots_ready, 1)
                    dve.wait_ge(table_ready, 1)
                    token, choice = ps_y[:, 0, 0:TILES], ps_y[:, 0, TILES:2 * TILES]
                    then(dve.tensor_scalar(empty[:, :], choice, 0.0, None, ALU.is_equal))
                    then(dve.tensor_tensor(empty[:, :], empty[:, :], pad_row[:, :], ALU.mult))
                    then(dve.tensor_scalar(row_f[:, :], choice, float(TOK), -float(TOK), ALU.mult, ALU.add))
                    then(dve.tensor_tensor(row_f[:, :], row_f[:, :], token, ALU.add))
                    then(dve.tensor_copy(from_row[:, FIRST:NT], token))
                    then(dve.tensor_tensor(to_row[:, FIRST:NT], row_f[:, :], empty[:, :], ALU.add))

                def index_from(t, s, rnd):
                    need(dve, gathered[s], rnd * 16)
                    dve.sem_inc(dve_turns, 1)
                    dve.tensor_copy(gi[s][:, :], from_row[:, col(t)]).then_inc(from_ready, 1)

                def index_to(t, s, rnd):
                    need(dve, scattered[s], rnd * 16)
                    dve.sem_inc(dve_turns, 1)
                    dve.tensor_copy(si[s][:, :], to_row[:, col(t)]).then_inc(to_ready, 1)

                def take_xT(t, s, rnd):
                    dve.wait_ge(xT_ready, t + 1)
                    need(dve, h_ready, (t - N + 1) * U)
                    dve.tensor_copy(xT[s][:, :, :], ps_t[:, 0, 0:D].rearrange("p (c t) -> p c t", c=KC)).then_inc(xT_taken, 1)

                def take_y(t, s, rnd):
                    dve.wait_ge(y_ready, t + 1)
                    need(dve, scattered[s], rnd * 16)
                    dve.wait_ge(w2_in[s], (rnd + 1) * 32)
                    dve.tensor_tensor(yt[s][:, :], ps_y[:, s, 0:D], b2t[s][:, :], ALU.add).then_inc(y_taken, 1)

                def step(t, at):
                    if live(t + 3):
                        index_from(t + 3, *at(3))
                    if live(t + 1):
                        take_xT(t + 1, *at(1))
                    if live(t):
                        index_to(t, *at(0))
                    if live(t - 1):
                        take_y(t - 1, *at(-1))

                for g in range(NG):
                    moments(g)
                if shared:
                    dve.wait_ge(half_set, 3)
                    dve.tensor_scalar(from_row[:, 0:FIRST], aux_f[:, :], float(TOK - 1), None, ALU.min).then_inc(rows_ready, 1)
                route()
                if shared:
                    dve.wait_ge(rows_ready, 1)
                rounds(dve, step, 3, 1, NT)
                if shared:
                    for b in range(B):
                        last = dve.scalar_tensor_tensor(out=xs[:, b, :], in0=xhat[:, b, :], scalar=tanhg[0:T, 0:1], in1=xs[:, b, :],
                                                        op0=ALU.mult, op1=ALU.add)
                    last.then_inc(rows_ready, 1)
                    dve.wait_ge(rows_ready, 2)
                for i in range(NG * WAYS):
                    g, way = i // WAYS, i % WAYS
                    dve.wait_ge(ways_in[i % 2], 16 * (i // 2 + 1))
                    need(dve, added, i * GB if way else 0)
                    for j in range(GB):
                        b = g * GB + j
                        gate = gates[:, way, b:b + 1] if way < top else tanhg[0:T, 0:1]
                        dve.scalar_tensor_tensor(out=xs[:, b, :], in0=parts[i % 2][:, j, :], scalar=gate, in1=xs[:, b, :],
                                                 op0=ALU.mult, op1=ALU.add).then_inc(added, 1)

            @block.scalar
            def _(act):
                def step(t, at):
                    if live(t):
                        s, _ = at(0)
                        for u in range(U):
                            act.wait_ge(h_ready, t * U + u + 1)
                            if u == 0:
                                need(act, y_ready, t - N + 1)
                            bank = (s * U + u) % N
                            for i in range(UNIT):
                                c = u * UNIT + i
                                last = act.activation(hT[s][:, c, :], ps_h[:, bank, i * P:(i + 1) * P], ACT.Gelu,
                                                      bias=w1[s][:, B1 + c:B1 + c + 1])
                            last.then_inc(h_taken, 1)

                for i in range(B // 2):
                    act.wait_ge(turned, i + 1)
                    act.activation(xTr[i % 2][:, :, :, :], ps_t[:, i % 2, 0:2 * KC * T].rearrange("p (b c t) -> p b c t", b=2, c=KC),
                                   ACT.Copy).then_inc(turned_taken, 1)
                act.wait_ge(exp_in, 1)
                if router_b is None:
                    act.activation(norm_rec[:, :], norm_sum[:, :], ACT.Exp).then_inc(exp_out, 1)
                else:
                    act.activation(sel[:, :, :], key[:, :, :], ACT.Exp).then_inc(exp_out, 1)
                rounds(act, step, 0, 1, NT)

            @block.tensor
            def _(pe):
                def turn(t, s, rnd):
                    pe.wait_ge(gathered[s], (rnd + 1) * 16)
                    need(pe, xT_taken, t)
                    for c in range(KC):
                        last = pe.transpose(ps_t[:, 0, c * P:(c + 1) * P], xt[s][:, c * P:(c + 1) * P], ident[:, :])
                    last.then_inc(xT_ready, 1)

                def hidden(t, s, rnd):
                    pe.wait_ge(w1_in[s], (rnd + 1) * 16)
                    pe.wait_ge(xT_taken, t + 1)
                    for u in range(U):
                        need(pe, h_taken, t * U + u - N + 1)
                        bank = (s * U + u) % N
                        for i in range(UNIT):
                            f = (u * UNIT + i) * P
                            for c in range(KC):
                                last = pe.matmul(ps_h[:, bank, i * P:(i + 1) * P], w1[s][:, c * ff + f:c * ff + f + P], xT[s][:, c, :],
                                                 start=(c == 0), stop=(c == KC - 1))
                        last.then_inc(h_ready, 1)

                def result(t, s, rnd):
                    pe.wait_ge(h_taken, (t + 1) * U)
                    need(pe, y_taken, t - N + 1)
                    pe.wait_ge(w2_in[s], (rnd + 1) * 32)
                    for c in range(FC):
                        last = pe.matmul(ps_y[:, s, 0:D], hT[s][:, c, :], w2[s][:, c * D:(c + 1) * D], start=(c == 0), stop=(c == FC - 1))
                    last.then_inc(y_ready, 1)

                def step(t, at):
                    if live(t + 1):
                        turn(t + 1, *at(1))
                    if live(t):
                        hidden(t, *at(0))
                    if live(t - 1):
                        result(t - 1, *at(-1))

                pe.wait_ge(w_loaded, 16 if router_b is None else 32)
                for i in range(B // 2 + 1):
                    if i < B // 2:
                        need(pe, turned_taken, i - 1)
                        pe.wait_ge(xhat_ready, 2 * i + 2)
                        for j in range(2):
                            for c in range(KC):
                                last = pe.transpose(ps_t[:, i % 2, (j * KC + c) * T:(j * KC + c + 1) * T],
                                                    xhat[:, 2 * i + j, c * P:(c + 1) * P], ident[0:T, 0:T])
                        last.then_inc(turned, 1)
                    if i > 0:
                        pe.wait_ge(turned_taken, i)
                        for j in range(2):
                            b = 2 * (i - 1) + j
                            for c in range(KC):
                                last = pe.matmul(ps_y[0:T, 0, b * E:(b + 1) * E], xTr[(i - 1) % 2][:, j, c, :], rw[:, c, :],
                                                 start=(c == 0), stop=(c == KC - 1))
                last.then_inc(logits_ready, 1)
                pe.wait_ge(consts_set, 8 + (3 if shared else 0))
                pe.wait_ge(mask_ready, 1)
                by_lane = mask[:, :, :].rearrange("p b e -> p (b e)")
                pe.matmul(ps_y[0:T, 1, 0:B * E], tri[:, :], by_lane, start=True, stop=True)
                for d in range(1, B):
                    pe.matmul(ps_y[0:T, 1, d * E:B * E], ones[:, 0:T], by_lane[:, 0:(B - d) * E], start=False, stop=True,
                              skip_group_check=True)
                for b in range(B):
                    last = pe.matmul(ps_y[:, 2, 0:E], ones[:, :], mask[:, b, :], start=(b == 0), stop=(b == B - 1))
                last.then_inc(ranks_ready, 1)
                for k in range(top):
                    pe.wait_ge(onehots_ready, k + 1)
                    for b in range(B):
                        c = k * B + b
                        last = pe.matmul(ps_y[:, 0, 0:2 * TILES], in_lane[:, c, :], tile_vals[:, c, :, :].rearrange("p v t -> p (v t)"),
                                         start=(c == 0), stop=(c == CB - 1))
                last.then_inc(table_ready, 1)
                rounds(pe, step, 1, 1, NT)


def build(nc, a, out):
    with ExitStack() as ctx:
        ident, mhalf, g_att, g_ffn = constants(nc, ctx, a["g_xattn"], a["g_ffn"])
        x1, x2, x3 = (nc.dram_tensor(f"x{i}", (B, T, D), F32).ap() for i in (1, 2, 3))
        attend0(nc, (ident, mhalf, g_att[:, 0:1]), a["x"], x1, a["ctxT"], *(a[f"L0_xattn_{n}"] for n in
                ("Wq", "bq", "Wk", "bk", "Wv", "bv", "Wo", "bo")))
        experts(nc, (ident, mhalf, g_ffn[:, 0:1]), "ex0", x1, x2, a["router0"], None, a["pack0_in"], a["pack0_out"], a["L0_ffn_b2"], 2, 1024, False)
        attend1(nc, (ident, mhalf, g_att[:, 1:2]), x2, x3, a["ctxT"], *(a[f"L1_xattn_{n}"] for n in
                ("Wqkv", "bqkv", "Wqkv_aux", "bqkv_aux", "Wo", "bo", "g")))
        experts(nc, (ident, mhalf, g_ffn[:, 1:2]), "ex1", x3, out, a["L1_ffn_gW"], a["L1_ffn_gb"], a["pack1_in"], a["pack1_out"], a["b2_1"], 3, 512, True)


def packed(np, w1, w2, b1):
    e, _, f = w1.shape
    return (np.concatenate([w1.reshape(e, KC, P, f).transpose(0, 2, 1, 3).reshape(e, P, KC * f),
                            b1.reshape(e, f // P, P).transpose(0, 2, 1)], axis=2),
            w2.reshape(e, f // P, P, D).transpose(0, 2, 1, 3).reshape(e, P, f // P * D))


def kernel(**inputs):
    import numpy as np
    import concourse.bacc as bacc
    from concourse.bass_utils import run_bass_kernel_spmd as run

    a = {k: np.asarray(v) for k, v in inputs.items()}
    laid = {k: v for k, v in a.items() if k.startswith(("x", "g_", "L0_xattn", "L1_xattn"))}
    laid.update({k: a[k] for k in ("L0_ffn_b2", "L1_ffn_gW", "L1_ffn_gb")})
    laid["ctxT"] = a["ctx_1024"].transpose(0, 2, 1)
    laid["router0"] = a["L0_ffn_router_w"].T
    laid["pack0_in"], laid["pack0_out"] = packed(np, a["L0_ffn_w1"].transpose(0, 2, 1), a["L0_ffn_w2"].transpose(0, 2, 1), a["L0_ffn_b1"])
    f = a["L1_ffn_rb1"].shape[1]
    w1, w2, b1 = a["L1_ffn_sW1"][0], a["L1_ffn_sW2"][0], a["L1_ffn_sb1"][0]
    laid["pack1_in"], laid["pack1_out"] = packed(np, np.concatenate([a["L1_ffn_rW1"], np.stack([w1[:, :f], w1[:, f:]])]),
                           np.concatenate([a["L1_ffn_rW2"], np.stack([w2[:f], w2[f:]])]),
                           np.concatenate([a["L1_ffn_rb1"], np.stack([b1[:f], b1[f:]])]))
    laid["b2_1"] = np.concatenate([a["L1_ffn_rb2"], a["L1_ffn_sb2"], np.zeros_like(a["L1_ffn_sb2"])])
    nc = bacc.Bacc("TRN2", target_bir_lowering=False, num_devices=1)
    arrays, handles = {}, {}
    for name, arr in laid.items():
        arrays[f"in_{name}"] = np.ascontiguousarray(arr)
        handles[name] = nc.dram_tensor(f"in_{name}", arr.shape, mybir.dt.from_np(arr.dtype), kind="ExternalInput").ap()
    out = nc.dram_tensor("out_x", (B, T, D), F32, kind="ExternalOutput").ap()
    build(nc, handles, out)
    return run(nc, [arrays], core_ids=[0]).results[0]["out_x"]
```

```python
from contextlib import ExitStack

import concourse.bass as bass
from concourse import mybir

F32 = mybir.dt.float32
F16 = mybir.dt.float16
I32 = mybir.dt.int32
U32 = mybir.dt.uint32
ACT = mybir.ActivationFunctionType
ALU = mybir.AluOpType
AX = mybir.AxisListType.X

P = 128
B, T, D = 16, 100, 256
S = 361
H, DH = 16, 16
KC = D // P
CHUNKS = [(0, 121), (121, 120), (241, 120)]
NJ = len(CHUNKS)
CT = 4
HG = H // CT
PARTS = 4
STACK = PARTS * DH
EPS = 1e-5
Q_PARTS = (0, 1, 0, 1)
K_PARTS = (0, 0, 1, 1)


def on(b):
    return not isinstance(b, int) or 0 <= b < B


def need(eng, sem, value):
    if not isinstance(value, int) or value > 0:
        eng.wait_ge(sem, value)


def landed(b, slot, dmas=1):
    return (b - slot) * (8 * dmas) + 16 * dmas


def pipeline(eng, step, lead, tail, n=2, first=0):
    lo = -(-max(tail, first) // n) * n
    hi = lo + (B - lead - lo) // n * n
    for b in range(-lead, lo):
        step(b, b % n)
    with eng.Fori(lo, hi - n + 1, n) as b:
        for i in range(n):
            step(b + i, i)
    for b in range(hi, B + tail):
        step(b, b % n)


def flat(ap):
    return ap.rearrange("p h n -> p (h n)")


def heads(ap):
    return ap.rearrange("p (h d) -> p h d", d=DH)


class Pool:

    def __init__(self, nc, ctx, stage):
        self.nc, self.ctx, self.stage = nc, ctx, stage
        self.allocated = []

    def close(self):
        self.nc.clear_and_free_semaphores(self.allocated)
        self.nc.all_engine_barrier()

    def sb(self, name, shape, dt=F32):
        return self.ctx.enter_context(self.nc.sbuf_tensor(f"{self.stage}_{name}", shape, dt))

    def ps(self, name, shape, dt=F32):
        return self.ctx.enter_context(self.nc.psum_tensor(f"{self.stage}_{name}", shape, dt))

    def sem(self, name):
        self.allocated.append(self.nc.alloc_semaphore(f"{self.stage}_{name}"))
        return self.allocated[-1]

    def sems(self, name):
        return [self.sem(f"{name}{i}") for i in range(2)]


def constants(nc, ctx, g_xattn, g_ffn):
    m = Pool(nc, ctx, "const")
    ident = m.sb("ident", [P, P])
    gates = m.sb("gates", [P, 4])
    tanhs = m.sb("tanhs", [P, 4])
    mhalf = m.sb("mhalf", [P, 1])
    zeroed, built, loaded, squashed = (m.sem(n) for n in ("zeroed", "built", "loaded", "squashed"))
    with nc.Block() as block:
        @block.gpsimd
        def _(pool):
            pool.memset(ident[:, :], 0.0).then_inc(zeroed, 1)
            pool.wait_ge(zeroed, 1)
            pool.affine_select(out=ident[:, :], in_=ident[:, :], compare_op=ALU.not_equal, fill=1.0,
                               base=0, pattern=[[-1, P]], channel_multiplier=1).then_inc(built, 1)
            pool.memset(mhalf[:, :], -0.5).then_inc(built, 1)
            pool.wait_ge(built, 2)

        @block.sync
        def _(sp):
            sp.dma_start(gates[:, 0:2], g_xattn.partition_broadcast(P)).then_inc(loaded, 16)
            sp.dma_start(gates[:, 2:4], g_ffn.partition_broadcast(P)).then_inc(loaded, 16)

        @block.scalar
        def _(act):
            act.wait_ge(loaded, 32)
            act.activation(tanhs[:, :], gates[:, :], ACT.Tanh).then_inc(squashed, 1)
            act.wait_ge(squashed, 1)
    return ident, mhalf, tanhs[:, 0:2], tanhs[:, 2:4]


class Norm:

    OPS = 6

    def __init__(self, m, mhalf):
        self.mhalf = mhalf
        self.stats, self.mv = m.sb("ln_stats", [T, 6]), m.sb("ln_mv", [T, 2])
        self.var, self.r0 = m.sb("ln_var", [T, 1]), m.sb("ln_r0", [T, 1])
        self.turn = m.sb("ln_turn", [T, 1])
        self.t, self.rstd = m.sb("ln_t", [T, 1]), m.sb("ln_rstd", [T, 1])
        self.step = m.sem("ln_step")
        self.root = m.sem("ln_root")

    def moments(self, dve, b, x):
        at = b * self.OPS
        need(dve, self.step, at)
        dve.bn_stats(self.stats[:, :], x).then_inc(self.step, 1)
        dve.wait_ge(self.step, at + 1)
        dve.memset(self.turn[:, :], 0.0)
        dve.bn_aggr(self.mv[:, :], self.stats[:, :]).then_inc(self.step, 1)
        dve.wait_ge(self.step, at + 2)
        dve.tensor_scalar(self.var[:, :], self.mv[:, 1:2], EPS, None, ALU.add).then_inc(self.step, 1)

    def power(self, pool, b):
        pool.wait_ge(self.step, b * self.OPS + 3)
        pool.tensor_tensor(self.r0[:, :], self.var[:, :], self.mhalf[0:T, :], ALU.pow).then_inc(self.root, 1)

    def newton(self, dve, b):
        at = b * self.OPS
        dve.wait_ge(self.root, b + 1)
        dve.scalar_tensor_tensor(out=self.t[:, :], in0=self.r0[:, :], scalar=self.var[:, 0:1], in1=self.r0[:, :],
                                 op0=ALU.mult, op1=ALU.mult).then_inc(self.step, 1)
        dve.wait_ge(self.step, at + 4)
        dve.tensor_scalar(self.t[:, :], self.t[:, :], -0.5, 1.5, ALU.mult, ALU.add).then_inc(self.step, 1)
        dve.wait_ge(self.step, at + 5)
        dve.tensor_tensor(self.rstd[:, :], self.r0[:, :], self.t[:, :], ALU.mult).then_inc(self.step, 1)

    def apply(self, dve, b, out, x):
        dve.wait_ge(self.step, (b + 1) * self.OPS)
        return dve.tensor_scalar(out, x, self.mv[:, 0:1], self.rstd[:, 0:1], ALU.subtract, ALU.mult)


def twice(rows):
    return rows.unsqueeze(0).to_broadcast([2] + list(rows.shape))


def part_tile(parts):
    return parts.rearrange("p s c n -> p s (c n)")


def part_save(scratch):
    return scratch.rearrange("s p m -> p s m")


def part_rows(scratch):
    return scratch.rearrange("s (d i) m -> s d (i m)", d=DH)


def attend0(nc, consts, x_in, x_out, ctxT, Wq, bq, Wk, bk, Wv, bv, Wo, bo):
    ident, mhalf, tanhg = consts
    with ExitStack() as ctx:
        m = Pool(nc, ctx, "at0")
        ctx.callback(m.close)
        RING = 6
        KEY, NORMED, QUERY, VALUE01, VALUE2 = 0, 2, 3, 4, 5
        UNITS = 2 * NJ
        HU = H // 2
        wq, wk, wv = (m.sb(n, [P, KC, D]) for n in ("wq", "wk", "wv"))
        wo = m.sb("wo", [P, HG, D])
        bqs, bks = m.sb("bq", [P, KC]), m.sb("bk", [P, KC])
        bvb, bob = m.sb("bv", [P, D]), m.sb("bo", [P, D])
        ctxt = [m.sb(f"ctx{i}", [P, KC, S]) for i in range(2)]
        xin = [m.sb(f"xin{i}", [T, D]) for i in range(2)]
        xres = [m.sb(f"xres{i}", [T, D]) for i in range(2)]
        xout = [m.sb(f"xout{i}", [T, D]) for i in range(2)]
        xhat = [m.sb(f"xhat{i}", [T, D]) for i in range(2)]
        xT = [m.sb(f"xT{i}", [P, KC, T]) for i in range(2)]
        qfull, kfull = m.sb("qfull", [P, KC, T]), m.sb("kfull", [P, KC, S])
        qparts = m.sb("qparts", [P, 2, KC, T], F16)
        kparts = m.sb("kparts", [P, 2, KC, S], F16)
        qst = [m.sb(f"qst{i}", [STACK, H, T], F16) for i in range(2)]
        kst = [m.sb(f"kst{i}", [STACK, H, S], F16) for i in range(2)]
        v = [m.sb(f"v{i}", [P, NJ, D]) for i in range(2)]
        vn = [m.sb(f"vn{i}", [P, NJ, H, 32]) for i in range(2)]
        probs = [m.sb(f"probs{i}", [P, NJ, H * T]) for i in range(2)]
        den = [m.sb(f"den{i}", [P, NJ * H]) for i in range(2)]
        rden = m.sb("rden", [P, NJ * H])
        negmax = [m.sb(f"negmax{i}", [P, HU]) for i in range(2)]
        oT = m.sb("oT", [P, HG * T])
        qd = nc.dram_tensor("at0_qd", (2, 2, P, KC * T), F16).ap()
        kd = nc.dram_tensor("at0_kd", (2, 2, P, KC * S), F16).ap()
        ps_s = m.ps("scores", [P, 4, 512])
        ps_r = m.ps("ring", [P, 2, 512])
        ps_o = m.ps("o", [P, 512])
        ps_y = m.ps("y", [P, 512])
        ln = Norm(m, mhalf)
        w_loaded, zeroed, wo_loaded = m.sem("w_loaded"), m.sem("zeroed"), m.sem("wo_loaded")
        scaled = m.sem("scaled")
        x_loaded, ctx_loaded, res_loaded = m.sems("x_loaded"), m.sems("ctx_loaded"), m.sems("res_loaded")
        xhat_ready, ring_ready, ring_free = m.sem("xhat_ready"), m.sem("ring_ready"), m.sem("ring_free")
        q_full, q_high, q_split = m.sem("q_full"), m.sem("q_high"), m.sem("q_split")
        k_full, k_high, k_split = m.sem("k_full"), m.sem("k_high"), m.sem("k_split")
        q_saved, k_saved = m.sem("q_saved"), m.sem("k_saved")
        q_stacked, k_stacked = m.sems("q_stacked"), m.sems("k_stacked")
        scores_ready, negmax_ready, exp_done = m.sem("scores_ready"), m.sem("negmax_ready"), m.sem("exp_done")
        rden_ready, vn_ready, pv_done = m.sem("rden_ready"), m.sem("vn_ready"), m.sem("pv_done")
        oT_ready, y_ready, x_ready = m.sem("oT_ready"), m.sem("y_ready"), m.sem("x_ready")
        res_ready, x_stored, sp_turns = m.sem("res_ready"), m.sems("x_stored"), m.sem("sp_turns")
        pool_turns = m.sem("pool_turns")
        NW = 7

        with nc.Block() as block:
            @block.sync
            def _(sp):
                def hold(sem, value):
                    need(sp, sem, value)
                    sp.sem_inc(sp_turns, 1)

                def load_inputs(b, s):
                    hold(xhat_ready, b - 1)
                    sp.dma_start(xin[s][:, :], x_in[b]).then_inc(x_loaded[s], 16)
                    hold(ring_ready, (b - 1) * RING)
                    sp.dma_start(ctxt[s][:, :, :], ctxT[b].rearrange("(c p) s -> p c s", p=P)).then_inc(ctx_loaded[s], 16)

                def save_keys(b, s):
                    hold(k_split, (b + 1) * KC)
                    sp.dma_start(part_save(kd[s]), part_tile(kparts[:, :, :, :])).then_inc(k_saved, 16)

                def stack_keys(b, s):
                    hold(scores_ready, (b - 1) * UNITS)
                    hold(k_saved, (b + 1) * 16)
                    for r in range(2):
                        sp.dma_start(flat(kst[s][r * 2 * DH:(r + 1) * 2 * DH, :, :]), twice(part_rows(kd[s])[r])).then_inc(k_stacked[s], 16)

                def stack_queries(b, s):
                    hold(q_split, b + 1)
                    sp.dma_start(part_save(qd[s]), part_tile(qparts[:, :, :, :])).then_inc(q_saved, 16)
                    hold(q_saved, (b + 1) * 16)
                    sp.dma_start(flat(qst[s][:, :, :]), twice(part_rows(qd[s]).rearrange("s d m -> (s d) m"))).then_inc(q_stacked[s], 16)

                def step(b, s):
                    if on(b + 2):
                        load_inputs(b + 2, s)
                    if on(b + 1):
                        save_keys(b + 1, 1 - s)
                    if on(b + 1):
                        stack_keys(b + 1, 1 - s)
                    if on(b - 2):
                        hold(x_ready, b - 1)
                        sp.dma_start(x_out[b - 2], xout[s][:, :]).then_inc(x_stored[s], 16)
                    if on(b):
                        sp.dma_start(xres[s][:, :], x_in[b]).then_inc(res_loaded[s], 16)
                    if on(b + 1):
                        stack_queries(b + 1, 1 - s)

                for w, src in ((wq, Wq), (wk, Wk), (wv, Wv)):
                    sp.dma_start(w[:, :, :], src.rearrange("(c p) n -> p c n", p=P)).then_inc(w_loaded, 16)
                for t, src in ((bqs, bq), (bks, bk)):
                    with nc.allow_non_contiguous_dma("one bias a partition"):
                        sp.dma_start(t[:, :], src.rearrange("(c p) -> p c", p=P)).then_inc(w_loaded, 16)
                for t, src in ((bvb, bv), (bob, bo)):
                    sp.dma_start(t[:, :], src.partition_broadcast(P)).then_inc(w_loaded, 16)
                sp.dma_start(wo[:, :, :], Wo.rearrange("g p n -> p g n")).then_inc(wo_loaded, 16)
                pipeline(sp, step, 2, 2, first=4)
                for s in range(2):
                    sp.wait_ge(x_stored[s], landed(B - 2 + s, s))

            @block.gpsimd
            def _(pool):
                def step(b, s):
                    if on(b + 1):
                        pool.wait_ge(q_full, b + 2)
                        need(pool, q_saved, (b + 1) * 16)
                        pool.sem_inc(pool_turns, 1)
                        pool.tensor_copy(qparts[:, 0], qfull[:, :, :]).then_inc(q_high, 1)
                        pool.wait_ge(q_high, b + 2)
                        pool.tensor_tensor(qparts[:, 1], qfull[:, :, :], qparts[:, 0], ALU.subtract).then_inc(q_split, 1)
                    if on(b + 2):
                        ln.power(pool, b + 2)
                    if on(b):
                        pool.wait_ge(res_loaded[s], landed(b, s))
                        pool.tensor_tensor(xres[s][:, :], xres[s][:, :], bob[0:T, :], ALU.add).then_inc(res_ready, 1)
                    if on(b + 2):
                        for i in range(KC):
                            n = (b + 2) * KC + i
                            pool.wait_ge(k_full, n + 1)
                            need(pool, k_saved, (b + 2) * 16)
                            pool.sem_inc(pool_turns, 1)
                            pool.tensor_copy(kparts[:, 0, i, :], kfull[:, i, :]).then_inc(k_high, 1)
                            pool.wait_ge(k_high, n + 1)
                            pool.tensor_tensor(kparts[:, 1, i, :], kfull[:, i, :], kparts[:, 0, i, :], ALU.subtract).then_inc(k_split, 1)

                for i in range(2):
                    pool.memset(den[i][:, :], 1.0).then_inc(zeroed, 1)
                    pool.memset(v[i][:, :, :], 0.0).then_inc(zeroed, 1)
                    pool.memset(vn[i][:, :, :, :], 0.0).then_inc(zeroed, 1)
                pool.wait_ge(scaled, 3)
                pipeline(pool, step, 2, 2, first=4)

            @block.vector
            def _(dve):
                def norm(b, s):
                    dve.wait_ge(x_loaded[s], landed(b, s))
                    ln.moments(dve, b, xin[s][:, :])

                def normed(b, s):
                    ln.newton(dve, b)
                    need(dve, ring_ready, (b - 2) * RING + NORMED + 1)
                    ln.apply(dve, b, xhat[s][:, :], xin[s][:, :]).then_inc(xhat_ready, 1)

                def take_xT(b, s):
                    dve.wait_ge(ring_ready, b * RING + NORMED + 1)
                    dve.tensor_copy(xT[s][:, :, :], ps_r[:, NORMED % 2, 0:KC * T].rearrange("p (c t) -> p c t", c=KC)).then_inc(ring_free, 1)

                def take_q(b, s):
                    dve.wait_ge(ring_ready, b * RING + QUERY + 1)
                    need(dve, q_split, b)
                    dve.tensor_tensor(qfull[:, :, :], ps_r[:, QUERY % 2, 0:KC * T].rearrange("p (c t) -> p c t", c=KC),
                                      bqs[:, :].unsqueeze(2).to_broadcast([P, KC, T]), ALU.add).then_inc(q_full, 1)
                    dve.wait_ge(q_full, b + 1)
                    dve.sem_inc(ring_free, 1)

                def take_k(b, i):
                    dve.wait_ge(ring_ready, b * RING + KEY + i + 1)
                    need(dve, k_split, (b - 1) * KC + i + 1)
                    dve.tensor_scalar(kfull[:, i, :], ps_r[:, (KEY + i) % 2, 0:S], bks[:, i:i + 1], None, ALU.add).then_inc(k_full, 1)
                    dve.wait_ge(k_full, b * KC + i + 1)
                    dve.sem_inc(ring_free, 1)

                def take_v(b, s, js, item):
                    dve.wait_ge(ring_ready, b * RING + item + 1)
                    need(dve, vn_ready, b - 1)
                    for j in js:
                        r = CHUNKS[j][1]
                        last = dve.tensor_tensor(v[s][0:r, j, :], ps_r[0:r, item % 2, (j - js[0]) * D:(j - js[0] + 1) * D],
                                                 bvb[0:r, :], ALU.add)
                    last.then_inc(ring_free, 1)

                def maxima(b, s, u):
                    r = CHUNKS[u // 2][1]
                    dve.wait_ge(scores_ready, b * UNITS + u + 1)
                    need(dve, exp_done, b * UNITS + u - 1)
                    dve.tensor_reduce(negmax[u % 2][0:r, :].rearrange("p (k h) -> p k h", k=2),
                                      ps_s[0:r, 2 * (u % 2):2 * (u % 2) + 2, 0:HU // 2 * T].rearrange("p k (h t) -> p k h t", t=T),
                                      AX, ALU.max, negate=True).then_inc(negmax_ready, 1)

                def scale_v(b, s):
                    dve.wait_ge(exp_done, (b + 1) * UNITS)
                    need(dve, vn_ready, b)
                    dve.reciprocal(rden[:, :], den[s][:, :]).then_inc(rden_ready, 1)
                    dve.wait_ge(rden_ready, b + 1)
                    need(dve, pv_done, b - 1)
                    dve.wait_ge(ring_free, (b + 1) * RING)
                    dve.tensor_tensor(vn[s][:, :, :, 0:DH].rearrange("p j h d -> p (j h) d"),
                                      v[s][:, :, :].rearrange("p j (h d) -> p (j h) d", d=DH),
                                      rden[:, :].unsqueeze(2).to_broadcast([P, NJ * H, DH]), ALU.mult).then_inc(vn_ready, 1)

                def take_o(b):
                    dve.wait_ge(pv_done, b + 1)
                    need(dve, y_ready, b)
                    dve.tensor_copy(oT[:, :], ps_o[:, 0:HG * T]).then_inc(oT_ready, 1)

                def residual(b, s):
                    dve.wait_ge(y_ready, b + 1)
                    dve.wait_ge(res_ready, b + 1)
                    need(dve, x_stored[s], landed(b - 2, s))
                    dve.scalar_tensor_tensor(out=xout[s][:, :], in0=ps_y[0:T, 0:D], scalar=tanhg[0:T, 0:1],
                                             in1=xres[s][:, :], op0=ALU.mult, op1=ALU.add).then_inc(x_ready, 1)

                def step(b, s):
                    for u in range(UNITS):
                        if on(b):
                            maxima(b, s, u)
                        if u == 0 and on(b - 1):
                            scale_v(b - 1, 1 - s)
                        if u == 1 and on(b - 2):
                            residual(b - 2, s)
                        if on(b + 1):
                            if u == 0:
                                take_xT(b + 1, 1 - s)
                            if u == 1:
                                take_q(b + 1, 1 - s)
                            if u == 2:
                                take_v(b + 1, 1 - s, (0, 1), VALUE01)
                            if u == 3:
                                take_v(b + 1, 1 - s, (2,), VALUE2)
                        if u in (4, 5) and on(b + 2):
                            take_k(b + 2, u - 4)
                        if u == 5 and on(b - 1):
                            take_o(b - 1)
                        if u == 3 and on(b + 2):
                            norm(b + 2, s)
                        if u == 4 and on(b + 2):
                            normed(b + 2, s)

                dve.wait_ge(w_loaded, 16 * NW)
                dve.tensor_scalar(wq[:, :, :], wq[:, :, :], DH ** -0.5, None, ALU.mult).then_inc(scaled, 1)
                dve.tensor_scalar(bqs[:, :], bqs[:, :], DH ** -0.5, None, ALU.mult).then_inc(scaled, 1)
                dve.tensor_scalar(bob[:, :], bob[:, :], tanhg[:, 0:1], None, ALU.mult).then_inc(scaled, 1)
                dve.wait_ge(scaled, 3)
                dve.wait_ge(zeroed, 6)
                pipeline(dve, step, 2, 2, first=4)

            @block.scalar
            def _(act):
                def step(b, s):
                    if not on(b):
                        return
                    need(act, pv_done, b - 1)
                    for u in range(UNITS):
                        j, r = u // 2, CHUNKS[u // 2][1]
                        act.wait_ge(negmax_ready, b * UNITS + u + 1)
                        for hh in range(HU):
                            h = (u % 2) * HU + hh
                            last = act.activation(
                                probs[s][0:r, j, h * T:(h + 1) * T],
                                ps_s[0:r, 2 * (u % 2) + hh // 4, (hh % 4) * T:(hh % 4 + 1) * T], ACT.Exp,
                                bias=negmax[u % 2][0:r, hh:hh + 1], accum_out=den[s][0:r, j * H + h:j * H + h + 1])
                        last.then_inc(exp_done, 1)

                act.wait_ge(zeroed, 6)
                pipeline(act, step, 2, 2, first=4)

            @block.tensor
            def _(pe):
                def ring_slot(n):
                    need(pe, ring_free, n - 1)

                def transposes(b, s):
                    ring_slot(b * RING + NORMED)
                    pe.wait_ge(xhat_ready, b + 1)
                    for c in range(KC):
                        last = pe.transpose(ps_r[:, NORMED % 2, c * T:(c + 1) * T], xhat[s][:, c * P:(c + 1) * P], ident[0:T, 0:T])
                    last.then_inc(ring_ready, 1)

                def project_q(b, s):
                    pe.wait_ge(ring_free, b * RING + NORMED + 1)
                    for i in range(KC):
                        for c in range(KC):
                            last = pe.matmul(ps_r[:, QUERY % 2, i * T:(i + 1) * T], wq[:, c, i * P:(i + 1) * P], xT[s][:, c, :],
                                             start=(c == 0), stop=(c == KC - 1))
                    last.then_inc(ring_ready, 1)

                def project_k(b, s, i):
                    ring_slot(b * RING + KEY + i)
                    if i == 0:
                        pe.wait_ge(ctx_loaded[s], landed(b, s))
                    for c in range(KC):
                        last = pe.matmul(ps_r[:, (KEY + i) % 2, 0:S], wk[:, c, i * P:(i + 1) * P], ctxt[s][:, c, :],
                                         start=(c == 0), stop=(c == KC - 1))
                    last.then_inc(ring_ready, 1)

                def project_v(b, s, js, item):
                    ring_slot(b * RING + item)
                    for j in js:
                        s0, r = CHUNKS[j]
                        for c in range(KC):
                            last = pe.matmul(ps_r[0:r, item % 2, (j - js[0]) * D:(j - js[0] + 1) * D],
                                             ctxt[s][:, c, s0:s0 + r], wv[:, c, :], start=(c == 0), stop=(c == KC - 1))
                    last.then_inc(ring_ready, 1)

                def scores(b, s, u):
                    s0, r = CHUNKS[u // 2]
                    if u == 0:
                        pe.wait_ge(q_stacked[s], landed(b, s))
                        pe.wait_ge(k_stacked[s], landed(b, s, 2))
                    need(pe, exp_done, b * UNITS + u - 1)
                    for hh in range(HU):
                        h = (u % 2) * HU + hh
                        last = pe.matmul(ps_s[0:r, 2 * (u % 2) + hh // 4, (hh % 4) * T:(hh % 4 + 1) * T],
                                         kst[s][:, h, s0:s0 + r], qst[s][:, h, :], start=True, stop=True)
                    last.then_inc(scores_ready, 1)

                def values(b, s, g):
                    if g == 0:
                        pe.wait_ge(vn_ready, b + 1)
                        need(pe, oT_ready, b)
                    for j, (_, r) in enumerate(CHUNKS):
                        for c in range(CT):
                            h = g * CT + c
                            last = pe.matmul(ps_o[32 * c:32 * c + 32, g * T:(g + 1) * T], vn[s][0:r, j, h, :],
                                             probs[s][0:r, j, h * T:(h + 1) * T], start=(j == 0), stop=(j == NJ - 1))
                    if g == HG - 1:
                        last.then_inc(pv_done, 1)

                def project_o(b):
                    pe.wait_ge(oT_ready, b + 1)
                    need(pe, x_ready, b)
                    for g in range(HG):
                        last = pe.matmul(ps_y[0:T, 0:D], oT[:, g * T:(g + 1) * T], wo[:, g, :],
                                         start=(g == 0), stop=(g == HG - 1))
                    last.then_inc(y_ready, 1)

                def step(b, s):
                    for u in range(UNITS):
                        if on(b):
                            scores(b, s, u)
                        if on(b + 1):
                            if u == 0:
                                transposes(b + 1, 1 - s)
                            if u == 1:
                                project_q(b + 1, 1 - s)
                            if u == 2:
                                project_v(b + 1, 1 - s, (0, 1), VALUE01)
                            if u == 3:
                                project_v(b + 1, 1 - s, (2,), VALUE2)
                        if u in (4, 5) and on(b + 2):
                            project_k(b + 2, s, u - 4)
                        if u == 0 and on(b - 2):
                            project_o(b - 2)
                        if 1 <= u <= HG and on(b - 1):
                            values(b - 1, 1 - s, u - 1)

                pe.wait_ge(w_loaded, 16 * NW)
                pe.wait_ge(wo_loaded, 16)
                pe.wait_ge(scaled, 3)
                pipeline(pe, step, 2, 2, first=4)


def clip(n):
    return min(max(n, 0), B) if isinstance(n, int) else n


RING1 = ((("norm_x", 1), ("turn_main", -3), ("turn_aux", -3), ("turn_mix", -3), ("value_own", 0), ("value_aux2", 0)),
         (("turn_max", -1), ("query_key", 1), ("value_aux01", 0), ("key_aux0", 2), ("key_aux1", 2), ("out", -3)))


def ring1(t, name):
    for bank, order in enumerate(RING1):
        names = [n for n, _ in order]
        if name in names:
            before = clip(t + order[0][1])
            for _, off in order[1:]:
                before = before + clip(t + off)
            return bank, before + sum(on(t + off) for _, off in order[:names.index(name)])


def attend1(nc, consts, x_in, x_out, ctxT, Wqkv, bqkv, Wqkv_a, bqkv_a, Wo, bo, g):
    ident, mhalf, tanhg = consts
    with ExitStack() as ctx:
        m = Pool(nc, ctx, "at1")
        ctx.callback(m.close)
        N = 3
        KEYS = T + S
        UNITS = 8
        LAG = 3
        HU = H // 2
        AUGMENTED = STACK + 2
        TILES = [(0, T, 0)] + [(T + s0, r, 1) for s0, r in CHUNKS]
        CLAMP = 60000.0

        def slots(name, shape, dt=F32):
            return [m.sb(f"{name}{i}", shape, dt) for i in range(N)]

        w = m.sb("wqkv", [P, KC, 3 * D])
        wa = m.sb("wkv_aux", [P, KC, 2 * D])
        wo = m.sb("wo", [P, KC, D])
        bqk, bka = m.sb("bqk", [P, 2 * KC]), m.sb("bka", [P, KC])
        bvb, bvab, bob = m.sb("bv", [P, D]), m.sb("bv_aux", [P, D]), m.sb("bo", [P, D])
        gate, omgate, gexp = m.sb("gate", [P, H]), m.sb("omgate", [P, H]), m.sb("gexp", [P, H])
        ones, zeros = m.sb("ones", [1, H * S], F16), m.sb("zeros", [1, H * S], F16)
        ctxt, xin, xres = slots("ctx", [P, KC, S]), slots("xin", [T, D]), slots("xres", [T, D])
        xout, xhat, xT = slots("xout", [T, D]), slots("xhat", [T, D]), slots("xT", [P, KC, T])
        qkfull, kafull = m.sb("qkfull", [P, 2 * KC, T]), m.sb("kafull", [P, KC, S])
        qkparts = m.sb("qkparts", [P, 2, 2 * KC, T], F16)
        kaparts = m.sb("kaparts", [P, 2, KC, S], F16)
        qst, kst = slots("qst", [AUGMENTED, H, T], F16), slots("kst", [AUGMENTED, H, KEYS], F16)
        vm, va = slots("vm", [T, H, 32]), slots("va", [P, NJ, H, 32])
        negmax = slots("negmax", [T, 2 * H])
        shift = m.sb("shift", [2 * H, T], F16)
        probs = [m.sb(f"probs{i}", [P, HU * T]) for i in range(2)]
        osb = [slots("om", [P, HG * T]), slots("oa", [P, HG * T])]
        rden = m.sb("rden", [T, 2 * H])
        mixed = [m.sb(f"mixed{i}", [T, D]) for i in range(2)]
        mix, mixT = m.sb("mix", [T, D]), m.sb("mixT", [P, KC, T])
        qd, kd = (nc.dram_tensor(f"at1_{n}d", (N, 2, P, KC * T), F16).ap() for n in "qk")
        kad = nc.dram_tensor("at1_kad", (N, 2, P, KC * S), F16).ap()
        ps_q = m.ps("by_query", [P, 2, 512])
        ps_k = m.ps("by_key", [P, 2, 512])
        ps_r = m.ps("ring", [P, 2, 512])
        ps_o = m.ps("o", [P, 2, 512])
        ln = Norm(m, mhalf)
        w_loaded, gexp_ready, scaled, filled, ones_set = (m.sem(n) for n in ("w_loaded", "gexp_ready", "scaled", "filled", "ones_set"))
        rows_set = m.sem("rows_set")
        x_loaded, ctx_loaded, res_loaded, res_ready = (m.sem(n) for n in ("x_loaded", "ctx_loaded", "res_loaded", "res_ready"))
        xhat_ready = m.sem("xhat_ready")
        ring_ready = [m.sem(f"ring_ready{i}") for i in range(2)]
        ring_free = [m.sem(f"ring_free{i}") for i in range(2)]
        qk_full, qk_high, qk_split = m.sem("qk_full"), m.sem("qk_high"), m.sem("qk_split")
        ka_full, ka_high, ka_split = m.sem("ka_full"), m.sem("ka_high"), m.sem("ka_split")
        qk_saved, ka_saved = m.sem("qk_saved"), m.sem("ka_saved")
        qk_stacked, ka_stacked = m.sem("qk_stacked"), m.sem("ka_stacked")
        by_query_ready, max_done = m.sem("by_query_ready"), m.sem("max_done")
        shift_ready, shift_stacked = m.sem("shift_ready"), m.sem("shift_stacked")
        by_key_ready, exp_done, pv_done = m.sem("by_key_ready"), m.sem("exp_done"), m.sem("pv_done")
        o_taken = [m.sem("om_taken"), m.sem("oa_taken")]
        rden_ready, mixed_ready, mix_ready = m.sem("rden_ready"), m.sem("mixed_ready"), m.sem("mix_ready")
        x_ready, x_stored, sp_turns = m.sem("x_ready"), m.sem("x_stored"), m.sem("sp_turns")
        NW = 9

        def exp_unit(i):
            return (-1, i - LAG) if i >= LAG else (-2, i + UNITS - LAG)

        def sum_unit(i):
            return (-1, i - LAG - 1) if i > LAG else (-2, i + UNITS - LAG - 1)

        def slot_of(phase):
            return lambda off: (phase + off) % N

        with nc.Block() as block:
            @block.sync
            def _(sp):
                def hold(sem, value):
                    need(sp, sem, value)
                    sp.sem_inc(sp_turns, 1)

                def load_inputs(b, s):
                    hold(xhat_ready, b - 2)
                    hold(x_loaded, b * 16)
                    sp.dma_start(xin[s][:, :], x_in[b]).then_inc(x_loaded, 16)

                def load_context(b, s):
                    bank, n = ring1(b - 3, "value_aux2")
                    need_ring = n + 1 if not isinstance(b, int) or b >= 3 else 0
                    hold(ring_ready[bank], need_ring)
                    hold(ctx_loaded, b * 16)
                    sp.dma_start(ctxt[s][:, :, :], ctxT[b].rearrange("(c p) s -> p c s", p=P)).then_inc(ctx_loaded, 16)

                def save_context_keys(b, s):
                    hold(ka_split, (b + 1) * KC)
                    sp.dma_start(part_save(kad[s]), part_tile(kaparts[:, :, :, :])).then_inc(ka_saved, 16)

                def stack_context_keys(b, s):
                    hold(by_key_ready, (b - 2) * UNITS)
                    hold(ka_saved, (b + 1) * 16)
                    hold(ka_stacked, b * 64)
                    for r in range(2):
                        key_rows(kst[s], r, T, KEYS, kad[s], ka_stacked)

                def stack_own(b, s):
                    hold(qk_split, b + 1)
                    for i, scratch in enumerate((qd, kd)):
                        sp.dma_start(part_save(scratch[s]), part_tile(qkparts[:, :, i * KC:(i + 1) * KC, :])).then_inc(qk_saved, 16)
                    hold(qk_saved, (b + 1) * 32)
                    hold(qk_stacked, b * 80)
                    sp.dma_start(flat(qst[s][0:STACK, :, :]), twice(part_rows(qd[s]).rearrange("s d m -> (s d) m"))).then_inc(qk_stacked, 16)
                    for r in range(2):
                        key_rows(kst[s], r, 0, T, kd[s], qk_stacked)

                def key_rows(stack, r, lo, hi, scratch, stacked):
                    for i in range(2):
                        sp.dma_start(stack[(2 * r + i) * DH:(2 * r + i + 1) * DH, :, lo:hi],
                                     part_rows(scratch)[r].rearrange("d (h n) -> d h n", h=H)).then_inc(stacked, 16)

                def stack_shift(b, s):
                    hold(shift_ready, b + 1)
                    hold(shift_stacked, b * 32)
                    for i in range(2):
                        sp.dma_start(qst[s][STACK + i:STACK + i + 1, :, :], shift[i * H:(i + 1) * H, :]).then_inc(shift_stacked, 16)

                def step(t, phase):
                    s = slot_of(phase)
                    if on(t + 1):
                        save_context_keys(t + 1, s(1))
                    if on(t - 1):
                        stack_shift(t - 1, s(-1))
                    if on(t + 3):
                        load_inputs(t + 3, s(3))
                    if on(t + 2):
                        load_context(t + 2, s(2))
                    if on(t - 2):
                        hold(x_ready, t - 4)
                        hold(res_loaded, (t - 2) * 16)
                        sp.dma_start(xres[s(-2)][:, :], x_in[t - 2]).then_inc(res_loaded, 16)
                    if on(t + 1):
                        stack_context_keys(t + 1, s(1))
                        stack_own(t + 1, s(1))
                    if on(t - 4):
                        hold(x_ready, t - 3)
                        hold(x_stored, (t - 4) * 16)
                        sp.dma_start(x_out[t - 4], xout[s(-4)][:, :]).then_inc(x_stored, 16)

                sp.dma_start(w[:, :, :], Wqkv.rearrange("(c p) n -> p c n", p=P)).then_inc(w_loaded, 16)
                sp.dma_start(wa[:, :, :], Wqkv_a.rearrange("(c p) n -> p c n", p=P)[:, :, D:3 * D]).then_inc(w_loaded, 16)
                sp.dma_start(wo[:, :, :], Wo.rearrange("(c p) n -> p c n", p=P)).then_inc(w_loaded, 16)
                with nc.allow_non_contiguous_dma("one bias a partition"):
                    sp.dma_start(bqk[:, :], bqkv[0:2 * D].rearrange("(c p) -> p c", p=P)).then_inc(w_loaded, 16)
                    sp.dma_start(bka[:, :], bqkv_a[D:2 * D].rearrange("(c p) -> p c", p=P)).then_inc(w_loaded, 16)
                for tile, src in ((bvb, bqkv[2 * D:3 * D]), (bvab, bqkv_a[2 * D:3 * D]), (bob, bo), (gexp, g)):
                    sp.dma_start(tile[:, :], src.partition_broadcast(P)).then_inc(w_loaded, 16)
                pipeline(sp, step, 3, 4, N, first=6)
                sp.wait_ge(x_stored, 16 * B)

            @block.gpsimd
            def _(pool):
                def step(t, phase):
                    s = slot_of(phase)
                    if on(t + 1):
                        pool.wait_ge(qk_high, t + 2)
                        pool.tensor_tensor(qkparts[:, 1], qkfull[:, :, :], qkparts[:, 0], ALU.subtract).then_inc(qk_split, 1)
                    if on(t + 2):
                        ln.power(pool, t + 2)
                    if on(t - 2):
                        pool.wait_ge(res_loaded, (t - 1) * 16)
                        pool.tensor_tensor(xres[s(-2)][:, :], xres[s(-2)][:, :], bob[0:T, :], ALU.add).then_inc(res_ready, 1)
                    if on(t + 2):
                        for j in range(KC):
                            pool.wait_ge(ka_high, (t + 2) * KC + j + 1)
                            pool.tensor_tensor(kaparts[:, 1, j, :], kafull[:, j, :], kaparts[:, 0, j, :], ALU.subtract).then_inc(ka_split, 1)

                pool.memset(ones[:, :], 1.0).then_inc(rows_set, 1)
                pool.memset(zeros[:, :], 0.0).then_inc(rows_set, 1)
                pool.wait_ge(scaled, 9)
                pipeline(pool, step, 2, 4, N)

            @block.vector
            def _(dve):
                def take(t, name):
                    bank, n = ring1(t, name)
                    dve.wait_ge(ring_ready[bank], n + 1)
                    return ps_r[:, bank, :], ring_free[bank]

                def norm(b, s):
                    dve.wait_ge(x_loaded, (b + 1) * 16)
                    ln.moments(dve, b, xin[s][:, :])

                def normed(b, s):
                    ln.newton(dve, b)
                    if not isinstance(b, int) or b >= N:
                        bank, n = ring1(b - 1 - N, "norm_x")
                        dve.wait_ge(ring_ready[bank], n + 1)
                    ln.apply(dve, b, xhat[s][:, :], xin[s][:, :]).then_inc(xhat_ready, 1)

                def take_query_key(t):
                    b = t + 1
                    bank, free = take(t, "query_key")
                    need(dve, qk_split, b)
                    dve.tensor_tensor(qkfull[:, :, :], bank[:, 0:2 * KC * T].rearrange("p (c t) -> p c t", t=T),
                                      bqk[:, :].unsqueeze(2).to_broadcast([P, 2 * KC, T]), ALU.add).then_inc(qk_full, 1)
                    dve.wait_ge(qk_full, b + 1)
                    dve.sem_inc(free, 1)

                def maxima(b, s, i):
                    dve.wait_ge(by_query_ready, b * UNITS + i + 1)
                    if i == 0 and (not isinstance(b, int) or b >= N):
                        bank, n = ring1(b - N + 1, "turn_max")
                        dve.wait_ge(ring_ready[bank], n + 1)
                    dve.tensor_reduce(negmax[s][:, 2 * i:2 * i + 2], ps_q[0:T, :, 0:T], AX, ALU.max, negate=True)
                    dve.tensor_reduce(negmax[s][:, H + 2 * i:H + 2 * i + 2], ps_q[0:T, :, T:KEYS], AX, ALU.max,
                                      negate=True).then_inc(max_done, 1)

                def take_max(t):
                    bank, free = take(t, "turn_max")
                    need(dve, shift_stacked, (t - 1) * 32)
                    dve.tensor_scalar(shift[:, :], bank[0:2 * H, 0:T], CLAMP, -CLAMP, ALU.min, ALU.max).then_inc(shift_ready, 1)
                    dve.wait_ge(shift_ready, t)
                    dve.sem_inc(free, 1)

                def take_values(t, s):
                    bank, free = take(t, "value_aux01")
                    need(dve, pv_done, (t - 2) * UNITS)
                    for j in (0, 1):
                        r = CHUNKS[j][1]
                        last = dve.tensor_tensor(va[s][0:r, j, :, 0:DH], heads(bank[0:r, j * D:(j + 1) * D]),
                                                 heads(bvab[0:r, :]), ALU.add)
                    last.then_inc(free, 1)

                def take_values2(t, s):
                    bank, free = take(t, "value_aux2")
                    r = CHUNKS[2][1]
                    dve.tensor_tensor(va[s][0:r, 2, :, 0:DH], heads(bank[0:r, 0:D]), heads(bvab[0:r, :]), ALU.add).then_inc(free, 1)

                def take_values_own(t, s):
                    bank, free = take(t, "value_own")
                    need(dve, pv_done, (t - 2) * UNITS)
                    dve.tensor_tensor(vm[s][:, :, 0:DH], heads(bank[0:T, 0:D]), heads(bvb[0:T, :]), ALU.add).then_inc(free, 1)

                def normalize(t, i):
                    b = t - 3
                    bank, free = take(t, ("turn_main", "turn_aux")[i])
                    by_head = bank[0:T, :].rearrange("p (h e) -> p h e", e=32)
                    need(dve, mix_ready, b)
                    dve.reciprocal(rden[:, i * H:(i + 1) * H], by_head[:, :, DH]).then_inc(rden_ready, 1)
                    dve.wait_ge(rden_ready, b * 2 + i + 1)
                    dve.tensor_tensor(heads(mixed[i][:, :]), by_head[:, :, 0:DH],
                                      rden[:, i * H:(i + 1) * H].unsqueeze(2).to_broadcast([T, H, DH]), ALU.mult).then_inc(free, 1)
                    if i == 1:
                        dve.wait_ge(free, ring1(t, "turn_aux")[1] + 1)
                        if not isinstance(b, int) or b >= 1:
                            bank1, n1 = ring1(t - 1, "turn_mix")
                            dve.wait_ge(ring_ready[bank1], n1 + 1)
                        dve.tensor_tensor(mix[:, :], mixed[0][:, :], mixed[1][:, :], ALU.add).then_inc(mix_ready, 1)

                def residual(t, s):
                    b = t - 3
                    bank, free = take(t, "out")
                    dve.wait_ge(res_ready, b + 1)
                    need(dve, x_stored, (b - 2) * 16)
                    dve.scalar_tensor_tensor(out=xout[s][:, :], in0=bank[0:T, 0:D], scalar=tanhg[0:T, 0:1],
                                             in1=xres[s][:, :], op0=ALU.mult, op1=ALU.add).then_inc(x_ready, 1)
                    dve.wait_ge(x_ready, b + 1)
                    dve.sem_inc(free, 1)

                def step(t, phase):
                    s = slot_of(phase)
                    for i in range(UNITS):
                        if on(t):
                            maxima(t, s(0), i)
                        if i == 0 and on(t - 1):
                            take_max(t)
                        if i == 1 and on(t - 3):
                            normalize(t, 0)
                        if i == 1 and on(t + 2):
                            norm(t + 2, s(2))
                        if i == 2 and on(t + 1):
                            take_query_key(t)
                        if i == 3 and on(t - 3):
                            normalize(t, 1)
                        if i == 4 and on(t):
                            take_values(t, s(0))
                        if i == 5 and on(t + 2):
                            normed(t + 2, s(2))
                        if i == 6 and on(t):
                            take_values_own(t, s(0))
                        if i == 7 and on(t):
                            take_values2(t, s(0))
                        if i == 7 and on(t - 3):
                            residual(t, s(-3))

                dve.wait_ge(w_loaded, 16 * NW)
                dve.tensor_scalar(w[:, :, 0:D], w[:, :, 0:D], DH ** -0.5, None, ALU.mult).then_inc(scaled, 1)
                dve.tensor_scalar(bqk[:, 0:KC], bqk[:, 0:KC], DH ** -0.5, None, ALU.mult).then_inc(scaled, 1)
                dve.tensor_scalar(bob[:, :], bob[:, :], tanhg[:, 0:1], None, ALU.mult).then_inc(scaled, 1)
                dve.wait_ge(gexp_ready, 1)
                dve.tensor_scalar(omgate[:, :], gexp[:, :], 1.0, None, ALU.add).then_inc(scaled, 1)
                dve.wait_ge(scaled, 4)
                dve.reciprocal(gate[:, :], omgate[:, :]).then_inc(scaled, 1)
                dve.wait_ge(scaled, 5)
                dve.tensor_scalar(omgate[:, :], gate[:, :], -1.0, 1.0, ALU.mult, ALU.add)
                dve.tensor_tensor(heads(bvab[:, :]), heads(bvab[:, :]), gate[:, :].unsqueeze(2).to_broadcast([P, H, DH]),
                                  ALU.mult).then_inc(scaled, 1)
                dve.wait_ge(scaled, 6)
                dve.tensor_tensor(heads(bvb[:, :]), heads(bvb[:, :]), omgate[:, :].unsqueeze(2).to_broadcast([P, H, DH]),
                                  ALU.mult).then_inc(scaled, 1)
                for c in range(KC):
                    dve.tensor_tensor(heads(w[:, c, 2 * D:3 * D]), heads(w[:, c, 2 * D:3 * D]),
                                      omgate[:, :].unsqueeze(2).to_broadcast([P, H, DH]), ALU.mult)
                    last = dve.tensor_tensor(heads(wa[:, c, D:2 * D]), heads(wa[:, c, D:2 * D]),
                                             gate[:, :].unsqueeze(2).to_broadcast([P, H, DH]), ALU.mult)
                last.then_inc(scaled, 2)
                for i in range(N):
                    dve.memset(vm[i][:, :, DH:32], 0.0)
                    last = dve.memset(va[i][:, :, :, DH:32], 0.0)
                last.then_inc(filled, 1)
                dve.wait_ge(filled, 1)
                for i in range(N):
                    dve.memset(vm[i][:, :, DH:DH + 1], 1.0)
                    last = dve.memset(va[i][:, :, :, DH:DH + 1], 1.0)
                last.then_inc(filled, 1)
                dve.wait_ge(scaled, 9)
                pipeline(dve, step, 2, 4, N)

            @block.scalar
            def _(act):
                def take(t, name):
                    bank, n = ring1(t, name)
                    act.wait_ge(ring_ready[bank], n + 1)
                    return ps_r[:, bank, :], ring_free[bank]

                def take_x(t, s):
                    bank, free = take(t, "norm_x")
                    act.activation(xT[s][:, :, :], bank[:, 0:KC * T].rearrange("p (c t) -> p c t", c=KC), ACT.Copy).then_inc(free, 1)

                def exponents(b, k, s):
                    n = b * UNITS + k
                    r = TILES[k // 2][1]
                    act.wait_ge(by_key_ready, n + 1)
                    need(act, pv_done, n - 1)
                    act.activation(probs[k % 2][0:r, :].rearrange("p (a n) -> p a n", a=2),
                                   ps_k[0:r, :, 0:HU // 2 * T], ACT.Exp).then_inc(exp_done, 1)

                def take_o(b, s, i):
                    act.wait_ge(pv_done, b * UNITS + (2, UNITS)[i])
                    if not isinstance(b, int) or b >= N:
                        bank, n = ring1(b, ("turn_main", "turn_aux")[i])
                        act.wait_ge(ring_ready[bank], n + 1)
                    act.activation(osb[i][s][:, :], ps_o[:, i, 0:HG * T], ACT.Copy).then_inc(o_taken[i], 1)

                def step(t, phase):
                    s = slot_of(phase)
                    for i in range(UNITS):
                        off, k = exp_unit(i)
                        b = t + off
                        if on(b):
                            exponents(b, k, s)
                        if i == 0 and on(t + 1):
                            take_x(t, s(1))
                        if i == 2 and on(t + 1):
                            act.wait_ge(qk_full, t + 2)
                            need(act, qk_saved, (t + 1) * 32)
                            act.activation(qkparts[:, 0], qkfull[:, :, :], ACT.Copy).then_inc(qk_high, 1)
                        if i == 4 and on(t - 3):
                            bank, free = take(t, "turn_mix")
                            act.activation(mixT[:, :, :], bank[:, 0:KC * T].rearrange("p (c t) -> p c t", c=KC), ACT.Copy).then_inc(free, 1)
                        if i == 4 and on(t - 2):
                            take_o(t - 2, s(-2), 1)
                        if i in (5, 6) and on(t + 2):
                            j = i - 5
                            n = (t + 2) * KC + j
                            bank, free = take(t, f"key_aux{j}")
                            need(act, ka_split, n - 1)
                            act.activation(kafull[:, j, :], bank[:, 0:S], ACT.Identity, bias=bka[:, j:j + 1]).then_inc(ka_full, 1)
                            need(act, ka_saved, (t + 2) * 16)
                            act.wait_ge(ka_full, n + 1)
                            act.sem_inc(free, 1)
                            act.activation(kaparts[:, 0, j, :], kafull[:, j, :], ACT.Copy).then_inc(ka_high, 1)
                        if i == 6 and on(t - 1):
                            take_o(t - 1, s(-1), 0)

                act.wait_ge(w_loaded, 16 * NW)
                act.activation(gexp[:, :], gexp[:, :], ACT.Exp, scale=-1.0).then_inc(gexp_ready, 1)
                act.wait_ge(rows_set, 2)
                for i in range(N):
                    for row, own, context in ((STACK, ones, zeros), (STACK + 1, zeros, ones)):
                        act.dma_start(kst[i][row:row + 1, :, 0:T], own[:, 0:H * T].rearrange("p (h k) -> p h k", h=H)).then_inc(ones_set, 16)
                        act.dma_start(kst[i][row:row + 1, :, T:KEYS], context[:, :].rearrange("p (h k) -> p h k", h=H)).then_inc(ones_set, 16)
                pipeline(act, step, 2, 4, N)

            @block.tensor
            def _(pe):
                def into(t, name):
                    bank, n = ring1(t, name)
                    need(pe, ring_free[bank], n)
                    return ps_r[:, bank, :], ring_ready[bank]

                def turn_max(t, s):
                    bank, ready = into(t, "turn_max")
                    pe.wait_ge(max_done, t * UNITS)
                    pe.transpose(bank[0:2 * H, 0:T], negmax[s][:, :], ident[0:T, 0:T]).then_inc(ready, 1)

                def norm_x(t, s):
                    bank, ready = into(t, "norm_x")
                    pe.wait_ge(xhat_ready, t + 2)
                    for c in range(KC):
                        last = pe.transpose(bank[:, c * T:(c + 1) * T], xhat[s][:, c * P:(c + 1) * P], ident[0:T, 0:T])
                    last.then_inc(ready, 1)

                def query_key(t, s):
                    bank, ready = into(t, "query_key")
                    b0, n0 = ring1(t, "norm_x")
                    pe.wait_ge(ring_free[b0], n0 + 1)
                    for i in range(2 * KC):
                        for c in range(KC):
                            last = pe.matmul(bank[:, i * T:(i + 1) * T], w[:, c, i * P:(i + 1) * P], xT[s][:, c, :],
                                             start=(c == 0), stop=(c == KC - 1))
                    last.then_inc(ready, 1)

                def key_aux(t, s, i):
                    bank, ready = into(t, f"key_aux{i}")
                    if i == 0:
                        pe.wait_ge(ctx_loaded, (t + 3) * 16)
                    for c in range(KC):
                        last = pe.matmul(bank[:, 0:S], wa[:, c, i * P:(i + 1) * P], ctxt[s][:, c, :],
                                         start=(c == 0), stop=(c == KC - 1))
                    last.then_inc(ready, 1)

                def value(bank, at, r, lhs, rhs):
                    for c in range(KC):
                        last = pe.matmul(bank[0:r, at:at + D], lhs(c), rhs(c), start=(c == 0), stop=(c == KC - 1))
                    return last

                def values01(t, s):
                    bank, ready = into(t, "value_aux01")
                    for j in (0, 1):
                        s0, r = CHUNKS[j]
                        last = value(bank, j * D, r, lambda c: ctxt[s][:, c, s0:s0 + r], lambda c: wa[:, c, D:2 * D])
                    last.then_inc(ready, 1)

                def values2(t, s):
                    bank, ready = into(t, "value_aux2")
                    s0, r = CHUNKS[2]
                    value(bank, 0, r, lambda c: ctxt[s][:, c, s0:s0 + r], lambda c: wa[:, c, D:2 * D]).then_inc(ready, 1)

                def values_own(t, s):
                    bank, ready = into(t, "value_own")
                    value(bank, 0, T, lambda c: xT[s][:, c, :], lambda c: w[:, c, 2 * D:3 * D]).then_inc(ready, 1)

                def by_query(b, s, i):
                    if i == 0:
                        pe.wait_ge(qk_stacked, (b + 1) * 80)
                        pe.wait_ge(ka_stacked, (b + 1) * 64)
                    need(pe, max_done, b * UNITS + i)
                    for a in range(2):
                        h = 2 * i + a
                        last = pe.matmul(ps_q[0:T, a, 0:KEYS], qst[s][0:STACK, h, :], kst[s][0:STACK, h, :], start=True, stop=True)
                    last.then_inc(by_query_ready, 1)

                def by_key(b, s, k):
                    k0, r, _ = TILES[k // 2]
                    if k == 0:
                        pe.wait_ge(ones_set, 16 * 4 * N)
                        pe.wait_ge(shift_stacked, (b + 1) * 32)
                    need(pe, exp_done, b * UNITS + k)
                    for hh in range(HU):
                        h = (k % 2) * HU + hh
                        last = pe.matmul(ps_k[0:r, hh // 4, (hh % 4) * T:(hh % 4 + 1) * T], kst[s][:, h, k0:k0 + r],
                                         qst[s][:, h, :], start=True, stop=True)
                    last.then_inc(by_key_ready, 1)

                def sum_up(b, s, k):
                    j, half = k // 2, k % 2
                    _, r, aux = TILES[j]
                    pe.wait_ge(exp_done, b * UNITS + k + 1)
                    if k == 0:
                        pe.wait_ge(filled, 2)
                    if k in (0, 2):
                        need(pe, o_taken[aux], b)
                    for hh in range(HU):
                        h = half * HU + hh
                        g, c = h // CT, h % CT
                        vals = va[s][0:r, j - 1, h, :] if aux else vm[s][:, h, :]
                        last = pe.matmul(ps_o[32 * c:32 * c + 32, aux, g * T:(g + 1) * T], vals,
                                         probs[k % 2][0:r, hh * T:(hh + 1) * T],
                                         start=(j in (0, 1) and h < CT), stop=(j in (0, NJ)), skip_group_check=True)
                    last.then_inc(pv_done, 1)

                def turn_sums(t, s, i):
                    bank, ready = into(t, ("turn_main", "turn_aux")[i])
                    pe.wait_ge(o_taken[i], t - 2)
                    for g_ in range(HG):
                        last = pe.transpose(bank[0:T, g_ * P:(g_ + 1) * P], osb[i][s][:, g_ * T:(g_ + 1) * T], ident[:, :])
                    last.then_inc(ready, 1)

                def turn_mix(t):
                    bank, ready = into(t, "turn_mix")
                    pe.wait_ge(mix_ready, t - 2)
                    for c in range(KC):
                        last = pe.transpose(bank[:, c * T:(c + 1) * T], mix[:, c * P:(c + 1) * P], ident[0:T, 0:T])
                    last.then_inc(ready, 1)

                def project_out(t):
                    bank, ready = into(t, "out")
                    b0, n0 = ring1(t, "turn_mix")
                    pe.wait_ge(ring_free[b0], n0 + 1)
                    value(bank, 0, T, lambda c: mixT[:, c, :], lambda c: wo[:, c, :]).then_inc(ready, 1)

                def step(t, phase):
                    s = slot_of(phase)
                    for i in range(UNITS):
                        if on(t):
                            by_query(t, s(0), i)
                        off, k = exp_unit(i)
                        b = t + off
                        if on(b):
                            by_key(b, s(off), k)
                        off, k = sum_unit(i)
                        b = t + off
                        if on(b):
                            sum_up(b, s(off), k)
                        if i == 0 and on(t + 1):
                            norm_x(t, s(1))
                        if i == 0 and on(t - 1):
                            turn_max(t, s(-1))
                        if i == 0 and on(t - 3):
                            turn_sums(t, s(-3), 0)
                        if i == 1 and on(t + 1):
                            query_key(t, s(1))
                        if i == 2 and on(t - 3):
                            turn_sums(t, s(-3), 1)
                        if i == 3 and on(t):
                            values01(t, s(0))
                        if i == 4 and on(t - 3):
                            turn_mix(t)
                        if i == 5 and on(t):
                            values_own(t, s(0))
                        if i in (5, 6) and on(t + 2):
                            key_aux(t, s(2), i - 5)
                        if i == 7 and on(t):
                            values2(t, s(0))
                        if i == 7 and on(t - 3):
                            project_out(t)

                pe.wait_ge(scaled, 9)
                pipeline(pe, step, 2, 4, N)


class Chain:

    def __init__(self, eng, sem):
        self.eng, self.sem, self.n = eng, sem, 0

    def __call__(self, instruction):
        instruction.then_inc(self.sem, 1)
        self.n += 1
        self.eng.wait_ge(self.sem, self.n)


def rounds(eng, step, lead, tail, count, n=3):
    def placed(phase, rnd):
        return lambda off: ((phase + off) % n, rnd + (phase + off) // n)

    lo, hi = -(-tail // n), (count - lead) // n
    for t in range(-lead, lo * n):
        step(t, placed(t % n, t // n))
    with eng.Fori(lo, hi) as rnd:
        for phase in range(n):
            step(rnd * n + phase, placed(phase, rnd))
    for t in range(hi * n, count + tail):
        step(t, placed(t % n, t // n))


def experts(nc, consts, name, x_in, x_out, router, router_b, pack1, pack2, b2, top, ff, shared):
    ident, mhalf, tanhg = consts
    with ExitStack() as ctx:
        m = Pool(nc, ctx, name)
        ctx.callback(m.close)
        N = 3
        E = router.shape[1]
        TOK = B * T
        TILES = (TOK * top + E * (P - 1)) // P
        ALL = -(-TOK // P)
        NT = TILES
        FC = ff // P
        UNIT = 4
        U = FC // UNIT
        B1 = KC * ff
        GB, NG = 4, B // 4
        CB = top * B
        PAD_ROW = TOK * top
        BIG = -3.0e38

        xs, xhat = m.sb("x", [T, B, D]), m.sb("xhat", [T, B, D])
        xhd = nc.dram_tensor(f"{name}_normed", (TOK, D), F32).ap()
        ways = nc.dram_tensor(f"{name}_results", (PAD_ROW + TILES * P, D), F32).ap()
        stats, mv = m.sb("stats", [T, B, 6]), m.sb("mv", [T, B, 2])
        var, r0, newt, rstd = (m.sb(n, [T, B]) for n in ("var", "r0", "newt", "rstd"))
        rw, rb = m.sb("router", [P, KC, E]), m.sb("router_b", [P, E])
        xTr = None if shared else [m.sb(f"xTr{i}", [P, KC, 2 * T]) for i in range(2)]
        tri, ones = m.sb("tri", [T, T]), m.sb("ones", [T, P])
        cols = m.sb("cols", [P, P])
        cols16 = m.sb("cols16", [P, P], F16)
        steps_of_p = m.sb("steps_of_p", [P, ALL])
        rev = m.sb("rev", [P, E])
        before = m.sb("before", [P, E, E])
        tok = m.sb("tok", [T, B])
        pad_row = m.sb("pad_row", [P, TILES])
        sel, key, mask = (m.sb(n, [T, B, E]) for n in ("sel", "key", "mask"))
        rowmax = m.sb("rowmax", [T, B])
        value = m.sb("value", [T, top, B])
        pick = m.sb("pick", [T, top, B, E])
        gates = m.sb("gates", [T, top, B])
        norm_sum, norm_rec = m.sb("norm_sum", [T, B]), m.sb("norm_rec", [T, B])
        picked = m.sb("picked", [T, top, B, E])
        rank, first = m.sb("rank", [T, CB]), m.sb("first", [T, CB])
        above = m.sb("above", [T, CB, ALL])
        tile_of, lane_of = m.sb("tile_of", [T, CB]), m.sb("lane_of", [T, CB])
        lane_of16 = m.sb("lane_of16", [T, CB], F16)
        full = m.sb("full", [T, E, ALL])
        tiles_of, start, end = (m.sb(n, [T, E]) for n in ("tiles_of", "start", "end"))
        below = m.sb("below", [T, E, E])
        ranks = m.sb("ranks", [T, B, E])
        running = [m.sb(f"running{i}", [T, B, E]) for i in range(2)]
        in_tile = m.sb("in_tile", [T, CB, TILES], F16)
        tile_vals = m.sb("tile_vals", [T, CB, 2, TILES], F16)
        in_lane = m.sb("in_lane", [T, CB, P], F16)
        passed = m.sb("passed", [1, TILES, E])
        expert_f = m.sb("expert_f", [1, TILES])
        expert_of = m.sb("expert_of", [1, NT], I32)
        row_f, empty = m.sb("row_f", [P, TILES]), m.sb("empty", [P, TILES])
        from_row, to_row = m.sb("from_row", [P, NT], U32), m.sb("to_row", [P, NT], U32)
        def slots(what, shape, dt=F32):
            return [m.sb(f"{what}{i}", shape, dt) for i in range(N)]

        w1, w2 = slots("w1_", [P, B1 + FC]), slots("w2_", [P, FC * D])
        gi, si = slots("from", [P, 1], U32), slots("to", [P, 1], U32)
        xt, xT, hT, yt = slots("xt", [P, D]), slots("xT", [P, KC, P]), slots("hT", [P, FC, P]), slots("yt", [P, D])
        PARTS_N = 4
        if not shared:
            parts = [m.sb(f"ways{i}", [T, GB, D])[:, :, :] for i in range(PARTS_N)]
            b2all = m.sb("b2", [P, E, D])[:, :, :]
        else:
            sw1_in, sb1_in, sw2_in, sb2_in = shared
            FS = sw1_in.shape[1] // P
            GT = GB * T
            sw = m.sb("sw", [P, KC * FS * P + FS * D])
            sw1 = sw[:, 0:KC * FS * P].rearrange("p (c f) -> p c f", c=KC)
            sw2 = sw[:, KC * FS * P:].rearrange("p (c d) -> p c d", d=D)
            b2all = sw[:, 0:E * D].rearrange("p (e d) -> p e d", d=D)
            sb1, sb2 = m.sb("sb1", [P, FS]), m.sb("sb2", [P, D])
            sxT = m.sb("sxT", [P, KC, TOK])
            shT = [m.sb(f"shT{i}", [P, FS, GT]) for i in range(2)]
            parts = [shT[i // 2][0:T, :, :].rearrange("p f g -> p (f g)")[:, i % 2 * GB * D:(i % 2 + 1) * GB * D]
                     .rearrange("p (b d) -> p b d", d=D) for i in range(PARTS_N)]
            addend = m.sb("addend", [T, B, D])
        ps_h = m.ps("h", [P, N, 512])
        ps_y = m.ps("y", [P, N, 512])
        ps_t = m.ps("t", [P, 2, 512])

        x_in_done = [m.sem(f"x_loaded{g}") for g in range(NG)]
        w_loaded, consts_set, half_set = m.sem("w_loaded"), m.sem("consts_set"), m.sem("half_set")
        stats_ready, root_ready, newton_step = m.sem("stats_ready"), m.sem("root_ready"), m.sem("newton_step")
        xhat_ready, xhat_saved = m.sem("xhat_ready"), m.sem("xhat_saved")
        turned, turned_taken, logits_ready = m.sem("turned"), m.sem("turned_taken"), m.sem("logits_ready")
        route_step, exp_in, exp_out = m.sem("route_step"), m.sem("exp_in"), m.sem("exp_out")
        mask_ready, ranks_ready, onehots_ready, table_ready = (m.sem(n) for n in ("mask_ready", "ranks_ready", "onehots_ready", "table_ready"))
        expert_ready, rows_ready = m.sem("expert_ready"), m.sem("rows_ready")
        w1_in, w2_in = [m.sem(f"w1_in{i}") for i in range(N)], [m.sem(f"w2_in{i}") for i in range(N)]
        gathered, scattered = [m.sem(f"gathered{i}") for i in range(N)], [m.sem(f"scattered{i}") for i in range(N)]
        from_ready, to_ready = m.sem("from_ready"), m.sem("to_ready")
        xT_ready, xT_taken, h_ready, h_taken = (m.sem(n) for n in ("xT_ready", "xT_taken", "h_ready", "h_taken"))
        y_ready, y_taken = m.sem("y_ready"), m.sem("y_taken")
        sp_turns, pool_turns, dve_turns = m.sem("sp_turns"), m.sem("pool_turns"), m.sem("dve_turns")
        ways_in = [m.sem(f"ways_in{i}") for i in range(PARTS_N)]
        b2_loaded = m.sem("b2_loaded")
        sw_loaded, sh_ready, sh_taken, sy_ready, sy_taken, sx_ready, base_step, sb2_ready = (
            m.sem(n) for n in ("sw_loaded", "sh_ready", "sh_taken", "sy_ready", "sy_taken", "sx_ready", "base_step", "sb2_ready"))
        added, x_stored = m.sem("added"), m.sem("x_stored")
        weighted, last_added = m.sem("weighted"), m.sem("last_added")
        weighted_row = [m.sb(f"weighted{i}", [T, D]) for i in range(2)]

        def turned_in(i):
            return sxT[:, :, i * 2 * T:(i + 1) * 2 * T] if shared else xTr[i % 2][:, :, :]

        def shared_bank(n):
            return (ps_h[0:T, 2, 0:D], ps_t[0:T, 1, 0:D])[n % 2]

        def col(t):
            return slice(t, t + 1) if isinstance(t, int) else bass.ds(t, 1)

        def live(t):
            return not isinstance(t, int) or 0 <= t < NT

        with nc.Block() as block:
            @block.sync
            def _(sp):
                def hold(sem, value):
                    need(sp, sem, value)
                    sp.sem_inc(sp_turns, 1)

                def expert(t):
                    return sp.value_load(expert_of[0:1, col(t)], min_val=0, max_val=pack1.shape[0] - 1)

                def load_in(t, s, rnd):
                    hold(h_ready, (t - N + 1) * U)
                    hold(h_taken, (t - N + 1) * U)
                    sp.dma_start(w1[s][:, :], pack1[bass.ds(expert(t), 1)].rearrange("o p n -> p (o n)")).then_inc(w1_in[s], 16)

                def load_out(t, s, rnd):
                    hold(y_ready, t - N + 1)
                    sp.dma_start(w2[s][:, :], pack2[bass.ds(expert(t), 1)].rearrange("o p n -> p (o n)")).then_inc(w2_in[s], 16)

                def step(t, at):
                    if live(t + 3):
                        load_in(t + 3, *at(3))
                    if live(t + 2):
                        load_out(t + 2, *at(2))

                def store(g):
                    sp.wait_ge(added, (g + 1) * top * (GB - 1))
                    sp.wait_ge(last_added, (g + 1) * top)
                    sp.dma_start(x_out[g * GB:(g + 1) * GB].rearrange("b t d -> t b d"),
                                 xs[:, g * GB:(g + 1) * GB, :]).then_inc(x_stored, 16)

                for g in range(NG):
                    sp.dma_start(xs[:, g * GB:(g + 1) * GB, :],
                                 x_in[g * GB:(g + 1) * GB].rearrange("b t d -> t b d")).then_inc(x_in_done[g], 16)
                sp.dma_start(rw[:, :, :], router.rearrange("(c p) e -> p c e", p=P)).then_inc(w_loaded, 16)
                if router_b is not None:
                    sp.dma_start(rb[:, :], router_b.partition_broadcast(P)).then_inc(w_loaded, 16)
                if shared:
                    sp.dma_start(sw1[:, :, :], sw1_in.rearrange("(c p) f -> p c f", p=P)).then_inc(sw_loaded, 16)
                    with nc.allow_non_contiguous_dma("one bias a partition"):
                        sp.dma_start(sb1[:, :], sb1_in.rearrange("(c p) -> p c", p=P)).then_inc(sw_loaded, 16)
                    sp.dma_start(sw2[:, :, :], sw2_in.rearrange("(c p) d -> p c d", p=P)).then_inc(sw_loaded, 16)
                    sp.dma_start(sb2[:, :], sb2_in.partition_broadcast(P)).then_inc(sw_loaded, 16)
                else:
                    sp.dma_start(b2all, b2.partition_broadcast(P)).then_inc(b2_loaded, 16)
                for g in range(NG):
                    sp.wait_ge(xhat_ready, (g + 1) * GB)
                    sp.dma_start(xhd[g * GB * T:(g + 1) * GB * T].rearrange("(b t) d -> t b d", t=T),
                                 xhat[:, g * GB:(g + 1) * GB, :]).then_inc(xhat_saved, 16)
                sp.wait_ge(expert_ready, 1)
                rounds(sp, step, 3, 1, NT)
                for s in range(N):
                    sp.wait_ge(scattered[s], 16 * len(range(s, NT, N)))
                if shared:
                    sp.wait_ge(sy_ready, B)
                for i in range(NG * top):
                    g, way = i // top, i % top
                    need(sp, added, (i - PARTS_N + 1) * (GB - 1))
                    need(sp, weighted, i - PARTS_N + 1)
                    row = way * TOK + g * GB * T
                    sp.dma_start(parts[i % PARTS_N][:, :, :],
                                 ways[row:row + GB * T].rearrange("(b t) d -> t b d", t=T)).then_inc(ways_in[i % PARTS_N], 16)
                    if way == top - 1 and g > 0:
                        store(g - 1)
                store(NG - 1)
                sp.wait_ge(x_stored, 16 * NG)

            @block.gpsimd
            def _(pool):
                def hold(sem, value):
                    need(pool, sem, value)
                    pool.sem_inc(pool_turns, 1)

                def gather(t, s, rnd):
                    hold(xT_ready, t - N + 1)
                    hold(from_ready, t + 1)
                    pool.indirect_dma_start(xt[s][:, :], None, xhd, bass.IndirectOffsetOnAxis(gi[s][:, :], 0)).then_inc(gathered[s], 16)

                def scatter(t, s, rnd):
                    hold(y_taken, t + 1)
                    hold(to_ready, t + 1)
                    pool.indirect_dma_start(ways, bass.IndirectOffsetOnAxis(si[s][:, :], 0), yt[s][:, :], None).then_inc(scattered[s], 16)

                def step(t, at):
                    if live(t + 3):
                        gather(t + 3, *at(3))
                    if live(t - 1):
                        scatter(t - 1, *at(-1))

                iota = pool.iota
                imprecise = dict(allow_small_or_imprecise_dtypes=True)
                pool.memset(ones[:, :], 1.0).then_inc(half_set, 1)
                pool.memset(before[:, :, :], 1.0).then_inc(half_set, 1)
                iota(cols[:, :], pattern=[[1, P]], base=0, channel_multiplier=0, **imprecise).then_inc(consts_set, 1)
                iota(cols16[:, :], pattern=[[1, P]], base=0, channel_multiplier=0, **imprecise).then_inc(consts_set, 1)
                iota(steps_of_p[:, :], pattern=[[P, ALL]], base=0, channel_multiplier=0, **imprecise).then_inc(consts_set, 1)
                iota(rev[:, :], pattern=[[-1, E]], base=E, channel_multiplier=0, **imprecise).then_inc(consts_set, 1)
                iota(tok[:, :], pattern=[[T, B]], base=0, channel_multiplier=1, **imprecise).then_inc(consts_set, 1)
                iota(pad_row[:, :], pattern=[[P, TILES]], base=PAD_ROW + TOK, channel_multiplier=1, **imprecise).then_inc(consts_set, 1)
                pool.wait_ge(half_set, 2)
                pool.affine_select(out=tri[:, :], in_=ones[:, 0:T], compare_op=ALU.is_gt, fill=0.0, base=0,
                                   pattern=[[1, T]], channel_multiplier=-1).then_inc(consts_set, 1)
                pool.affine_select(out=before[:, :, :], in_=before[:, :, :], compare_op=ALU.is_gt, fill=0.0, base=0,
                                   pattern=[[1, E], [-1, E]], channel_multiplier=0).then_inc(consts_set, 1)
                for g in range(NG):
                    at = slice(g * GB, (g + 1) * GB)
                    pool.wait_ge(stats_ready, (g + 1))
                    pool.tensor_tensor(r0[:, at], var[:, at], mhalf[0:T, :].to_broadcast([T, GB]), ALU.pow).then_inc(root_ready, 1)
                def add_shared(n):
                    pool.wait_ge(sy_taken, n + 1)
                    pool.tensor_tensor(xs[:, n, :], xs[:, n, :], addend[:, n, :], ALU.add).then_inc(base_step, 1)

                if shared:
                    pool.wait_ge(sb2_ready, 1)
                    for n in range(B):
                        pool.wait_ge(sx_ready, n + 1)
                        pool.tensor_tensor(xs[:, n, :], xs[:, n, :], addend[:, n, :], ALU.add).then_inc(base_step, 1)
                    for n in range(B):
                        pool.wait_ge(base_step, B)
                        pool.tensor_tensor(xs[:, n, :], xs[:, n, :], sb2[0:T, :], ALU.add).then_inc(base_step, 1)
                    pool.wait_ge(base_step, 2 * B)
                    for n in range(B - GB):
                        add_shared(n)
                pool.wait_ge(xhat_saved, 16 * NG)
                rounds(pool, step, 3, 1, NT)
                if shared:
                    for n in range(B - GB, B):
                        add_shared(n)
                    pool.wait_ge(base_step, 3 * B)
                for i in range(NG * top):
                    b = i // top * GB + GB - 1
                    pool.wait_ge(weighted, i + 1)
                    need(pool, last_added, i if i % top else 0)
                    pool.tensor_tensor(xs[:, b, :], xs[:, b, :], weighted_row[i % 2][:, :], ALU.add).then_inc(last_added, 1)

            @block.vector
            def _(dve):
                norm_then = Chain(dve, newton_step)

                def moments(g):
                    dve.wait_ge(x_in_done[g], 16)
                    for b in range(g * GB, (g + 1) * GB):
                        last = dve.bn_stats(stats[:, b, :], xs[:, b, :])
                    norm_then(last)
                    for b in range(g * GB, (g + 1) * GB):
                        last = dve.bn_aggr(mv[:, b, :], stats[:, b, :])
                    norm_then(last)
                    at = slice(g * GB, (g + 1) * GB)
                    dve.tensor_scalar(var[:, at], mv[:, at, 1], EPS, None, ALU.add).then_inc(stats_ready, 1)

                def normed(g):
                    at = slice(g * GB, (g + 1) * GB)
                    dve.wait_ge(stats_ready, g + 1)
                    dve.wait_ge(root_ready, g + 1)
                    norm_then(dve.tensor_tensor(newt[:, at], r0[:, at], r0[:, at], ALU.mult))
                    norm_then(dve.tensor_tensor(newt[:, at], newt[:, at], var[:, at], ALU.mult))
                    norm_then(dve.tensor_scalar(newt[:, at], newt[:, at], -0.5, 1.5, ALU.mult, ALU.add))
                    norm_then(dve.tensor_tensor(rstd[:, at], r0[:, at], newt[:, at], ALU.mult))
                    for b in range(g * GB, (g + 1) * GB):
                        dve.tensor_scalar(xhat[:, b, :], xs[:, b, :], mv[:, b, 0:1], rstd[:, b:b + 1],
                                          ALU.subtract, ALU.mult).then_inc(xhat_ready, 1)

                def per_expert(ap):
                    return ap.unsqueeze(2).to_broadcast([T, B, E])

                def per_batch(ap):
                    return ap.unsqueeze(1).to_broadcast([T, B, E])

                def route():
                    then = Chain(dve, route_step)
                    dve.wait_ge(consts_set, 8)
                    dve.wait_ge(logits_ready, 1)
                    logits = ps_y[0:T, 0, 0:B * E].rearrange("p (b e) -> p b e", e=E)
                    if router_b is None:
                        then(dve.tensor_copy(sel[:, :, :], logits))
                    else:
                        then(dve.tensor_tensor(key[:, :, :], logits, per_batch(rb[0:T, :]), ALU.add))
                        then(dve.tensor_reduce(rowmax[:, :], key[:, :, :], AX, ALU.max))
                        dve.tensor_tensor(key[:, :, :], key[:, :, :], per_expert(rowmax[:, :]), ALU.subtract).then_inc(exp_in, 1)
                        dve.wait_ge(exp_out, 1)
                        then(dve.tensor_reduce(norm_sum[:, :], sel[:, :, :], AX, ALU.add))
                        then(dve.reciprocal(norm_rec[:, :], norm_sum[:, :]))
                        then(dve.tensor_tensor(sel[:, :, :], sel[:, :, :], per_expert(norm_rec[:, :]), ALU.mult))
                    for k in range(top):
                        then(dve.tensor_reduce(value[:, k, :], sel[:, :, :], AX, ALU.max))
                        then(dve.tensor_tensor(key[:, :, :], sel[:, :, :], per_expert(value[:, k, :]), ALU.is_equal))
                        then(dve.tensor_tensor(key[:, :, :], key[:, :, :], per_batch(rev[0:T, :]), ALU.mult))
                        then(dve.tensor_reduce(rowmax[:, :], key[:, :, :], AX, ALU.max))
                        then(dve.tensor_tensor(pick[:, k], key[:, :, :], per_expert(rowmax[:, :]), ALU.is_equal))
                        if k < top - 1:
                            then(dve.scalar_tensor_tensor(out=sel[:, :, :], in0=pick[:, k], scalar=BIG, in1=sel[:, :, :],
                                                          op0=ALU.mult, op1=ALU.add))
                    then(dve.tensor_tensor(mask[:, :, :], pick[:, 0], pick[:, 1], ALU.add))
                    for k in range(2, top):
                        then(dve.tensor_tensor(mask[:, :, :], mask[:, :, :], pick[:, k], ALU.add))
                    dve.sem_inc(mask_ready, 1)
                    if router_b is None:
                        dve.tensor_tensor(norm_sum[:, :], value[:, 1, :], value[:, 0, :], ALU.subtract).then_inc(exp_in, 1)
                        dve.wait_ge(exp_out, 1)
                        then(dve.tensor_scalar(norm_sum[:, :], norm_rec[:, :], 1.0, None, ALU.add))
                        then(dve.reciprocal(value[:, 0, :], norm_sum[:, :]))
                        then(dve.tensor_tensor(value[:, 1, :], value[:, 0, :], norm_rec[:, :], ALU.mult))
                    then(dve.tensor_scalar(gates[:, :, :], value[:, :, :], tanhg[0:T, 0:1], None, ALU.mult))
                    dve.wait_ge(ranks_ready, 1)
                    in_batch = ps_y[0:T, 1, 0:B * E].rearrange("p (b e) -> p b e", e=E)
                    total = ps_y[0:T, 2, 0:B * E].rearrange("p (b e) -> p b e", e=E)
                    then(dve.tensor_copy(running[0][:, :, :], total))
                    upto, d = running[0][:, :, :], 1
                    while d < B:
                        nxt = running[d.bit_length() % 2]
                        dve.tensor_copy(nxt[:, 0:d, :], upto[:, 0:d, :])
                        then(dve.tensor_tensor(nxt[:, d:B, :], upto[:, d:B, :], upto[:, 0:B - d, :], ALU.add))
                        upto, d = nxt[:, :, :], 2 * d
                    dve.tensor_copy(ranks[:, 0:1, :], in_batch[:, 0:1, :])
                    then(dve.tensor_tensor(ranks[:, 1:B, :], in_batch[:, 1:B, :], upto[:, 0:B - 1, :], ALU.add))
                    counts = upto[:, B - 1, :]
                    then(dve.tensor_tensor(full[:, :, :], counts.unsqueeze(2).to_broadcast([T, E, ALL]),
                                           steps_of_p[0:T, :].unsqueeze(1).to_broadcast([T, E, ALL]), ALU.is_gt))
                    then(dve.tensor_reduce(tiles_of[:, :], full[:, :, :], AX, ALU.add))
                    then(dve.tensor_tensor(below[:, :, :], before[0:T, :, :], tiles_of[:, :].unsqueeze(1).to_broadcast([T, E, E]), ALU.mult))
                    then(dve.tensor_reduce(start[:, :], below[:, :, :], AX, ALU.add))
                    then(dve.tensor_tensor(end[:, :], start[:, :], tiles_of[:, :], ALU.add))
                    then(dve.tensor_tensor(passed[:, :, :], cols[0:1, 0:TILES].unsqueeze(2).to_broadcast([1, TILES, E]),
                                           end[0:1, :].unsqueeze(1).to_broadcast([1, TILES, E]), ALU.is_ge))
                    then(dve.tensor_reduce(expert_f[:, :], passed[:, :, :], AX, ALU.add))
                    dve.tensor_scalar(expert_of[:, 0:NT], expert_f[:, :], float(E - 1), None, ALU.min).then_inc(expert_ready, 1)
                    for k in range(top):
                        then(dve.tensor_tensor(picked[:, k], pick[:, k], ranks[:, :, :], ALU.mult))
                    by_choice = picked[:, :, :, :].rearrange("p k b e -> p (k b) e")
                    then(dve.tensor_reduce(rank[:, :], by_choice, AX, ALU.add))
                    then(dve.tensor_tensor(by_choice, pick[:, :, :, :].rearrange("p k b e -> p (k b) e"),
                                           start[0:T, :].unsqueeze(1).to_broadcast([T, CB, E]), ALU.mult))
                    then(dve.tensor_reduce(first[:, :], by_choice, AX, ALU.add))
                    then(dve.tensor_tensor(above[:, :, 1:ALL], rank[:, :].unsqueeze(2).to_broadcast([T, CB, ALL - 1]),
                                           steps_of_p[0:T, 1:ALL].unsqueeze(1).to_broadcast([T, CB, ALL - 1]), ALU.is_ge))
                    then(dve.tensor_reduce(tile_of[:, :], above[:, :, 1:ALL], AX, ALU.add))
                    then(dve.scalar_tensor_tensor(out=lane_of[:, :], in0=tile_of[:, :], scalar=-float(P), in1=rank[:, :],
                                                  op0=ALU.mult, op1=ALU.add))
                    then(dve.tensor_tensor(tile_of[:, :], tile_of[:, :], first[:, :], ALU.add))
                    then(dve.tensor_tensor(in_tile[:, :, :], tile_of[:, :].unsqueeze(2).to_broadcast([T, CB, TILES]),
                                           cols[0:T, 0:TILES].unsqueeze(1).to_broadcast([T, CB, TILES]), ALU.is_equal))
                    for k in range(top):
                        of_k = slice(k * B, (k + 1) * B)
                        dve.tensor_tensor(tile_vals[:, of_k, 0, :], in_tile[:, of_k, :],
                                          tok[:, :].unsqueeze(2).to_broadcast([T, B, TILES]), ALU.mult)
                        then(dve.tensor_scalar(tile_vals[:, of_k, 1, :], in_tile[:, of_k, :], float(k + 1), None, ALU.mult))
                        dve.tensor_tensor(in_lane[:, of_k, :], lane_of[:, of_k].unsqueeze(2).to_broadcast([T, B, P]),
                                          cols[0:T, :].unsqueeze(1).to_broadcast([T, B, P]), ALU.is_equal).then_inc(onehots_ready, 1)
                    dve.wait_ge(table_ready, 1)
                    token, choice = ps_y[:, 0, 0:TILES], ps_y[:, 0, TILES:2 * TILES]
                    then(dve.tensor_scalar(empty[:, :], choice, 0.0, None, ALU.is_equal))
                    then(dve.tensor_tensor(empty[:, :], empty[:, :], pad_row[:, :], ALU.mult))
                    then(dve.tensor_scalar(row_f[:, :], choice, float(TOK), -float(TOK), ALU.mult, ALU.add))
                    then(dve.tensor_tensor(row_f[:, :], row_f[:, :], token, ALU.add))
                    then(dve.tensor_copy(from_row[:, 0:NT], token))
                    then(dve.tensor_tensor(to_row[:, 0:NT], row_f[:, :], empty[:, :], ALU.add))

                def index_from(t, s, rnd):
                    need(dve, gathered[s], rnd * 16)
                    dve.sem_inc(dve_turns, 1)
                    dve.tensor_copy(gi[s][:, :], from_row[:, col(t)]).then_inc(from_ready, 1)

                def index_to(t, s, rnd):
                    need(dve, scattered[s], rnd * 16)
                    dve.sem_inc(dve_turns, 1)
                    dve.tensor_copy(si[s][:, :], to_row[:, col(t)]).then_inc(to_ready, 1)

                def take_xT(t, s, rnd):
                    dve.wait_ge(xT_ready, t + 1)
                    need(dve, h_ready, (t - N + 1) * U)
                    dve.tensor_copy(xT[s][:, :, :], ps_t[:, 0, 0:D].rearrange("p (c t) -> p c t", c=KC)).then_inc(xT_taken, 1)

                def take_y(t, s, rnd):
                    dve.wait_ge(b2_loaded, 16)
                    e = dve.value_load(expert_of[0:1, col(t)], min_val=0, max_val=E - 1)
                    dve.wait_ge(y_ready, t + 1)
                    need(dve, scattered[s], rnd * 16)
                    dve.sem_inc(dve_turns, 1)
                    dve.tensor_tensor(yt[s][:, :], ps_y[:, s, 0:D], b2all[:, bass.ds(e, 1), :].rearrange("p o d -> p (o d)"),
                                      ALU.add).then_inc(y_taken, 1)

                def step(t, at):
                    if live(t + 3):
                        index_from(t + 3, *at(3))
                    if live(t + 1):
                        take_xT(t + 1, *at(1))
                    if live(t):
                        index_to(t, *at(0))
                    if live(t - 1):
                        take_y(t - 1, *at(-1))

                for g in range(NG):
                    moments(g)
                    if g > 0:
                        normed(g - 1)
                normed(NG - 1)
                route()
                dve.wait_ge(expert_ready, 1)
                rounds(dve, step, 3, 1, NT)
                if shared:
                    dve.wait_ge(base_step, 3 * B)
                for i in range(NG * top):
                    g, way = i // top, i % top
                    dve.wait_ge(ways_in[i % PARTS_N], 16 * (i // PARTS_N + 1))
                    need(dve, added, i * (GB - 1) if way else 0)
                    for j in range(GB - 1):
                        b = g * GB + j
                        dve.scalar_tensor_tensor(out=xs[:, b, :], in0=parts[i % PARTS_N][:, j, :], scalar=gates[:, way, b:b + 1], in1=xs[:, b, :],
                                                 op0=ALU.mult, op1=ALU.add).then_inc(added, 1)

            @block.scalar
            def _(act):
                def step(t, at):
                    if live(t):
                        s, _ = at(0)
                        for u in range(U):
                            act.wait_ge(h_ready, t * U + u + 1)
                            if u == 0:
                                need(act, y_ready, t - N + 1)
                            bank = (s * U + u) % N
                            for i in range(UNIT):
                                c = u * UNIT + i
                                last = act.activation(hT[s][:, c, :], ps_h[:, bank, i * P:(i + 1) * P], ACT.Gelu,
                                                      bias=w1[s][:, B1 + c:B1 + c + 1])
                            last.then_inc(h_taken, 1)

                for i in range(B // 2):
                    act.wait_ge(turned, i + 1)
                    act.activation(turned_in(i).rearrange("p c (b t) -> p b c t", b=2),
                                   ps_t[:, i % 2, 0:2 * KC * T].rearrange("p (b c t) -> p b c t", b=2, c=KC), ACT.Copy).then_inc(turned_taken, 1)
                def shared_gelu(g):
                    for f in range(FS):
                        act.wait_ge(sh_ready, g * FS + f + 1)
                        if f == 0:
                            need(act, sy_ready, (g - 1) * GB)
                        act.activation(shT[g % 2][:, f, :], ps_h[:, f % 2, 0:GT], ACT.Gelu, bias=sb1[:, f:f + 1]).then_inc(sh_taken, 1)

                def shared_take(g):
                    for n in range(g * GB, (g + 1) * GB):
                        act.wait_ge(sy_ready, n + 1)
                        act.wait_ge(base_step, B)
                        act.activation(addend[:, n, :], shared_bank(n), ACT.Copy, scale=tanhg[0:T, 0:1]).then_inc(sy_taken, 1)

                if shared:
                    for n in range(B):
                        act.wait_ge(xhat_ready, n + 1)
                        act.activation(addend[:, n, :], xhat[:, n, :], ACT.Copy, scale=tanhg[0:T, 0:1]).then_inc(sx_ready, 1)
                    act.wait_ge(sw_loaded, 64)
                    act.activation(sb2[:, :], sb2[:, :], ACT.Copy, scale=tanhg[:, 0:1]).then_inc(sb2_ready, 1)
                act.wait_ge(exp_in, 1)
                if router_b is None:
                    act.activation(norm_rec[:, :], norm_sum[:, :], ACT.Exp).then_inc(exp_out, 1)
                else:
                    act.activation(sel[:, :, :], key[:, :, :], ACT.Exp).then_inc(exp_out, 1)
                if shared:
                    shared_gelu(0)
                    shared_gelu(1)
                    shared_take(0)
                    shared_gelu(2)
                    shared_take(1)
                    shared_gelu(3)
                    shared_take(2)
                    shared_take(3)
                    act.wait_ge(sy_ready, B)
                    act.dma_start(b2all, b2.partition_broadcast(P)).then_inc(b2_loaded, 16)
                rounds(act, step, 0, 1, NT)
                for i in range(NG * top):
                    b = i // top * GB + GB - 1
                    act.wait_ge(ways_in[i % PARTS_N], 16 * (i // PARTS_N + 1))
                    need(act, last_added, i - 1)
                    act.activation(weighted_row[i % 2][:, :], parts[i % PARTS_N][:, GB - 1, :], ACT.Copy,
                                   scale=gates[:, i % top, b:b + 1]).then_inc(weighted, 1)

            @block.tensor
            def _(pe):
                def turn(t, s, rnd):
                    pe.wait_ge(gathered[s], (rnd + 1) * 16)
                    need(pe, xT_taken, t)
                    for c in range(KC):
                        last = pe.transpose(ps_t[:, 0, c * P:(c + 1) * P], xt[s][:, c * P:(c + 1) * P], ident[:, :])
                    last.then_inc(xT_ready, 1)

                def hidden(t, s, rnd):
                    pe.wait_ge(w1_in[s], (rnd + 1) * 16)
                    pe.wait_ge(xT_taken, t + 1)
                    for u in range(U):
                        need(pe, h_taken, t * U + u - N + 1)
                        bank = (s * U + u) % N
                        for i in range(UNIT):
                            f = (u * UNIT + i) * P
                            for c in range(KC):
                                last = pe.matmul(ps_h[:, bank, i * P:(i + 1) * P], w1[s][:, c * ff + f:c * ff + f + P], xT[s][:, c, :],
                                                 start=(c == 0), stop=(c == KC - 1))
                        last.then_inc(h_ready, 1)

                def result(t, s, rnd):
                    pe.wait_ge(h_taken, (t + 1) * U)
                    need(pe, y_taken, t - N + 1)
                    pe.wait_ge(w2_in[s], (rnd + 1) * 16)
                    for c in range(FC):
                        last = pe.matmul(ps_y[:, s, 0:D], hT[s][:, c, :], w2[s][:, c * D:(c + 1) * D], start=(c == 0), stop=(c == FC - 1))
                    last.then_inc(y_ready, 1)

                def step(t, at):
                    if live(t + 1):
                        turn(t + 1, *at(1))
                    if live(t):
                        hidden(t, *at(0))
                    if live(t - 1):
                        result(t - 1, *at(-1))

                pe.wait_ge(w_loaded, 16 if router_b is None else 32)
                for i in range(B // 2 + 1):
                    if i < B // 2:
                        need(pe, turned_taken, i - 1)
                        pe.wait_ge(xhat_ready, 2 * i + 2)
                        for j in range(2):
                            for c in range(KC):
                                last = pe.transpose(ps_t[:, i % 2, (j * KC + c) * T:(j * KC + c + 1) * T],
                                                    xhat[:, 2 * i + j, c * P:(c + 1) * P], ident[0:T, 0:T])
                        last.then_inc(turned, 1)
                    if i > 0:
                        pe.wait_ge(turned_taken, i)
                        for j in range(2):
                            b = 2 * (i - 1) + j
                            for c in range(KC):
                                last = pe.matmul(ps_y[0:T, 0, b * E:(b + 1) * E], turned_in(i - 1)[:, c, j * T:(j + 1) * T], rw[:, c, :],
                                                 start=(c == 0), stop=(c == KC - 1))
                last.then_inc(logits_ready, 1)
                def rank():
                    pe.wait_ge(consts_set, 8)
                    pe.wait_ge(mask_ready, 1)
                    by_lane = mask[:, :, :].rearrange("p b e -> p (b e)")
                    pe.matmul(ps_y[0:T, 1, 0:B * E], tri[:, :], by_lane, start=True, stop=True)
                    pe.matmul(ps_y[0:T, 2, 0:B * E], ones[:, 0:T], by_lane, start=True, stop=True).then_inc(ranks_ready, 1)

                def shared_hidden(g):
                    pe.wait_ge(sw_loaded, 64)
                    pe.wait_ge(turned_taken, (g + 1) * GB // 2)
                    for f in range(FS):
                        need(pe, sh_taken, g * FS + f - 1)
                        for c in range(KC):
                            last = pe.matmul(ps_h[:, f % 2, 0:GT], sw1[:, c, f * P:(f + 1) * P], sxT[:, c, g * GT:(g + 1) * GT],
                                             start=(c == 0), stop=(c == KC - 1))
                        last.then_inc(sh_ready, 1)

                def shared_result(g):
                    pe.wait_ge(sh_taken, (g + 1) * FS)
                    for n in range(g * GB, (g + 1) * GB):
                        need(pe, sy_taken, n - 1)
                        for c in range(FS):
                            last = pe.matmul(shared_bank(n), shT[g % 2][:, c, n % GB * T:(n % GB + 1) * T], sw2[:, c, :],
                                             start=(c == 0), stop=(c == FS - 1))
                        last.then_inc(sy_ready, 1)

                def table():
                    for k in range(top):
                        pe.wait_ge(onehots_ready, k + 1)
                        for b in range(B):
                            c = k * B + b
                            last = pe.matmul(ps_y[:, 0, 0:2 * TILES], in_lane[:, c, :], tile_vals[:, c, :, :].rearrange("p v t -> p (v t)"),
                                             start=(c == 0), stop=(c == CB - 1))
                    last.then_inc(table_ready, 1)

                if shared:
                    shared_hidden(0)
                    shared_hidden(1)
                    shared_result(0)
                rank()
                if shared:
                    shared_hidden(2)
                    shared_result(1)
                    shared_hidden(3)
                    shared_result(2)
                table()
                if shared:
                    shared_result(3)
                rounds(pe, step, 1, 1, NT)


def build(nc, a, out):
    with ExitStack() as ctx:
        ident, mhalf, g_att, g_ffn = constants(nc, ctx, a["g_xattn"], a["g_ffn"])
        x1, x2, x3 = (nc.dram_tensor(f"x{i}", (B, T, D), F32).ap() for i in (1, 2, 3))
        attend0(nc, (ident, mhalf, g_att[:, 0:1]), a["x"], x1, a["ctxT"], *(a[f"L0_xattn_{n}"] for n in
                ("Wq", "bq", "Wk", "bk", "Wv", "bv", "Wo", "bo")))
        experts(nc, (ident, mhalf, g_ffn[:, 0:1]), "ex0", x1, x2, a["router0"], None, a["pack0_in"], a["pack0_out"], a["L0_ffn_b2"], 2, 1024, None)
        attend1(nc, (ident, mhalf, g_att[:, 1:2]), x2, x3, a["ctxT"], *(a[f"L1_xattn_{n}"] for n in
                ("Wqkv", "bqkv", "Wqkv_aux", "bqkv_aux", "Wo", "bo", "g")))
        experts(nc, (ident, mhalf, g_ffn[:, 1:2]), "ex1", x3, out, a["L1_ffn_gW"], a["L1_ffn_gb"], a["pack1_in"], a["pack1_out"], a["L1_ffn_rb2"], 3, 512,
                [a[f"L1_ffn_{n}"] for n in ("sW1", "sb1", "sW2", "sb2")])


def packed(np, w1, w2, b1):
    e, _, f = w1.shape
    return (np.concatenate([w1.reshape(e, KC, P, f).transpose(0, 2, 1, 3).reshape(e, P, KC * f),
                            b1.reshape(e, f // P, P).transpose(0, 2, 1)], axis=2),
            w2.reshape(e, f // P, P, D).transpose(0, 2, 1, 3).reshape(e, P, f // P * D))


def by_dimension(w):
    lead = w.shape[:-1]
    n = len(lead)
    return w.reshape(*lead, H // KC, KC, DH).transpose(*range(n), n + 1, n + 2, n).reshape(*lead, D)


def kernel(**inputs):
    import numpy as np
    import concourse.bacc as bacc
    from concourse.bass_utils import run_bass_kernel_spmd as run

    a = {k: np.asarray(v) for k, v in inputs.items()}
    laid = {k: v for k, v in a.items() if k.startswith(("x", "g_", "L0_xattn", "L1_xattn"))}
    laid.update({k: a[k] for k in ("L0_ffn_b2", "L1_ffn_gW", "L1_ffn_gb")})
    laid["ctxT"] = a["ctx_1024"].transpose(0, 2, 1)
    laid["router0"] = a["L0_ffn_router_w"].T
    laid["pack0_in"], laid["pack0_out"] = packed(np, a["L0_ffn_w1"].transpose(0, 2, 1), a["L0_ffn_w2"].transpose(0, 2, 1), a["L0_ffn_b1"])
    for name in ("L0_xattn_Wq", "L0_xattn_bq", "L0_xattn_Wk", "L0_xattn_bk"):
        laid[name] = by_dimension(laid[name])
    for name in ("L1_xattn_Wqkv", "L1_xattn_bqkv", "L1_xattn_Wqkv_aux", "L1_xattn_bqkv_aux"):
        laid[name] = np.concatenate([by_dimension(part) if i < 2 else part
                                     for i, part in enumerate(np.split(laid[name], 3, axis=-1))], axis=-1)
    laid["L0_xattn_Wo"] = np.pad(a["L0_xattn_Wo"].reshape(HG, CT, DH, D), ((0, 0), (0, 0), (0, 32 - DH), (0, 0))).reshape(HG, P, D)
    laid["pack1_in"], laid["pack1_out"] = packed(np, a["L1_ffn_rW1"], a["L1_ffn_rW2"], a["L1_ffn_rb1"])
    laid["L1_ffn_rb2"] = a["L1_ffn_rb2"]
    laid.update({f"L1_ffn_{n}": a[f"L1_ffn_{n}"][0] for n in ("sW1", "sb1", "sW2", "sb2")})
    nc = bacc.Bacc("TRN2", target_bir_lowering=False, num_devices=1)
    arrays, handles = {}, {}
    for name, arr in laid.items():
        arrays[f"in_{name}"] = np.ascontiguousarray(arr)
        handles[name] = nc.dram_tensor(f"in_{name}", arr.shape, mybir.dt.from_np(arr.dtype), kind="ExternalInput").ap()
    out = nc.dram_tensor("out_x", (B, T, D), F32, kind="ExternalOutput").ap()
    build(nc, handles, out)
    return run(nc, [arrays], core_ids=[0]).results[0]["out_x"]
```

```python
from contextlib import ExitStack

import concourse.bass as bass
from concourse import mybir

F32 = mybir.dt.float32
F16 = mybir.dt.float16
I32 = mybir.dt.int32
U32 = mybir.dt.uint32
ACT = mybir.ActivationFunctionType
ALU = mybir.AluOpType
AX = mybir.AxisListType.X

P = 128
B, T, D = 16, 100, 256
S = 361
H, DH = 16, 16
KC = D // P
CHUNKS = [(0, 121), (121, 120), (241, 120)]
NJ = len(CHUNKS)
CT = 4
HG = H // CT
PARTS = 4
STACK = PARTS * DH
EPS = 1e-5


def on(b):
    return not isinstance(b, int) or 0 <= b < B


def need(eng, sem, value):
    if not isinstance(value, int) or value > 0:
        eng.wait_ge(sem, value)


def landed(b, slot, dmas=1):
    return (b - slot) * (8 * dmas) + 16 * dmas


def pipeline(eng, step, lead, tail, n=2, first=0):
    lo = -(-max(tail, first) // n) * n
    hi = lo + (B - lead - lo) // n * n
    for b in range(-lead, lo):
        step(b, b % n)
    with eng.Fori(lo, hi - n + 1, n) as b:
        for i in range(n):
            step(b + i, i)
    for b in range(hi, B + tail):
        step(b, b % n)


def flat(ap):
    return ap.rearrange("p h n -> p (h n)")


def heads(ap):
    return ap.rearrange("p (h d) -> p h d", d=DH)


class Pool:

    def __init__(self, nc, ctx, stage):
        self.nc, self.ctx, self.stage = nc, ctx, stage
        self.allocated = []

    def close(self):
        self.nc.clear_and_free_semaphores(self.allocated)
        self.nc.all_engine_barrier()

    def sb(self, name, shape, dt=F32):
        return self.ctx.enter_context(self.nc.sbuf_tensor(f"{self.stage}_{name}", shape, dt))

    def ps(self, name, shape, dt=F32):
        return self.ctx.enter_context(self.nc.psum_tensor(f"{self.stage}_{name}", shape, dt))

    def sem(self, name):
        self.allocated.append(self.nc.alloc_semaphore(f"{self.stage}_{name}"))
        return self.allocated[-1]

    def sems(self, name):
        return [self.sem(f"{name}{i}") for i in range(2)]


def constants(nc, ctx, g_xattn, g_ffn):
    m = Pool(nc, ctx, "const")
    ident = m.sb("ident", [P, P])
    gates = m.sb("gates", [P, 4])
    tanhs = m.sb("tanhs", [P, 4])
    mhalf = m.sb("mhalf", [P, 1])
    zeroed, built, loaded, squashed = (m.sem(n) for n in ("zeroed", "built", "loaded", "squashed"))
    with nc.Block() as block:
        @block.gpsimd
        def _(pool):
            pool.memset(ident[:, :], 0.0).then_inc(zeroed, 1)
            pool.wait_ge(zeroed, 1)
            pool.affine_select(out=ident[:, :], in_=ident[:, :], compare_op=ALU.not_equal, fill=1.0,
                               base=0, pattern=[[-1, P]], channel_multiplier=1).then_inc(built, 1)
            pool.memset(mhalf[:, :], -0.5).then_inc(built, 1)
            pool.wait_ge(built, 2)

        @block.sync
        def _(sp):
            sp.dma_start(gates[:, 0:2], g_xattn.partition_broadcast(P)).then_inc(loaded, 16)
            sp.dma_start(gates[:, 2:4], g_ffn.partition_broadcast(P)).then_inc(loaded, 16)

        @block.scalar
        def _(act):
            act.wait_ge(loaded, 32)
            act.activation(tanhs[:, :], gates[:, :], ACT.Tanh).then_inc(squashed, 1)
            act.wait_ge(squashed, 1)
    return ident, mhalf, tanhs[:, 0:2], tanhs[:, 2:4]


class Norm:

    OPS = 6

    def __init__(self, m, mhalf):
        self.mhalf = mhalf
        self.stats, self.mv = m.sb("ln_stats", [T, 6]), m.sb("ln_mv", [T, 2])
        self.var, self.r0 = m.sb("ln_var", [T, 1]), m.sb("ln_r0", [T, 1])
        self.turn = m.sb("ln_turn", [T, 1])
        self.t, self.rstd = m.sb("ln_t", [T, 1]), m.sb("ln_rstd", [T, 1])
        self.step = m.sem("ln_step")
        self.root = m.sem("ln_root")

    def moments(self, dve, b, x):
        at = b * self.OPS
        need(dve, self.step, at)
        dve.bn_stats(self.stats[:, :], x).then_inc(self.step, 1)
        dve.wait_ge(self.step, at + 1)
        dve.memset(self.turn[:, :], 0.0)
        dve.bn_aggr(self.mv[:, :], self.stats[:, :]).then_inc(self.step, 1)
        dve.wait_ge(self.step, at + 2)
        dve.tensor_scalar(self.var[:, :], self.mv[:, 1:2], EPS, None, ALU.add).then_inc(self.step, 1)

    def power(self, pool, b):
        pool.wait_ge(self.step, b * self.OPS + 3)
        pool.tensor_tensor(self.r0[:, :], self.var[:, :], self.mhalf[0:T, :], ALU.pow).then_inc(self.root, 1)

    def newton(self, dve, b):
        at = b * self.OPS
        dve.wait_ge(self.root, b + 1)
        dve.scalar_tensor_tensor(out=self.t[:, :], in0=self.r0[:, :], scalar=self.var[:, 0:1], in1=self.r0[:, :],
                                 op0=ALU.mult, op1=ALU.mult).then_inc(self.step, 1)
        dve.wait_ge(self.step, at + 4)
        dve.tensor_scalar(self.t[:, :], self.t[:, :], -0.5, 1.5, ALU.mult, ALU.add).then_inc(self.step, 1)
        dve.wait_ge(self.step, at + 5)
        dve.tensor_tensor(self.rstd[:, :], self.r0[:, :], self.t[:, :], ALU.mult).then_inc(self.step, 1)

    def apply(self, dve, b, out, x):
        dve.wait_ge(self.step, (b + 1) * self.OPS)
        return dve.tensor_scalar(out, x, self.mv[:, 0:1], self.rstd[:, 0:1], ALU.subtract, ALU.mult)


def twice(rows):
    return rows.unsqueeze(0).to_broadcast([2] + list(rows.shape))


def part_tile(parts):
    return parts.rearrange("p s c n -> p s (c n)")


def part_save(scratch):
    return scratch.rearrange("s p m -> p s m")


def part_rows(scratch):
    return scratch.rearrange("s (d i) m -> s d (i m)", d=DH)


def attend0(nc, consts, x_in, x_out, ctxT, Wq, bq, Wk, bk, Wv, bv, Wo, bo):
    ident, mhalf, tanhg = consts
    with ExitStack() as ctx:
        m = Pool(nc, ctx, "at0")
        ctx.callback(m.close)
        RING = 6
        KEY, NORMED, QUERY, VALUE01, VALUE2 = 0, 2, 3, 4, 5
        QUARTERS = 4
        UNITS = QUARTERS * NJ
        HU = H // QUARTERS
        wq, wk, wv = (m.sb(n, [P, KC, D]) for n in ("wq", "wk", "wv"))
        wo = m.sb("wo", [P, HG, D])
        bqs, bks = m.sb("bq", [P, KC]), m.sb("bk", [P, KC])
        bvb, bob = m.sb("bv", [P, D]), m.sb("bo", [P, D])
        ctxt = [m.sb(f"ctx{i}", [P, KC, S]) for i in range(2)]
        xin = [m.sb(f"xin{i}", [T, D]) for i in range(2)]
        xres = [m.sb(f"xres{i}", [T, D]) for i in range(2)]
        xout = [m.sb(f"xout{i}", [T, D]) for i in range(2)]
        xhat = [m.sb(f"xhat{i}", [T, D]) for i in range(2)]
        xT = [m.sb(f"xT{i}", [P, KC, T]) for i in range(2)]
        qfull, kfull = m.sb("qfull", [P, KC, T]), m.sb("kfull", [P, KC, S])
        qparts = m.sb("qparts", [P, 2, KC, T], F16)
        kparts = m.sb("kparts", [P, 2, KC, S], F16)
        qst = [m.sb(f"qst{i}", [STACK, H, T], F16) for i in range(2)]
        kst = [m.sb(f"kst{i}", [STACK, H, S], F16) for i in range(2)]
        v = [m.sb(f"v{i}", [P, NJ, D]) for i in range(2)]
        vn = [m.sb(f"vn{i}", [P, NJ, H, 32]) for i in range(2)]
        probs = [m.sb(f"probs{i}", [P, NJ, H * T]) for i in range(2)]
        den = [m.sb(f"den{i}", [P, NJ * H]) for i in range(2)]
        rden = m.sb("rden", [P, NJ * H])
        negmax = [m.sb(f"negmax{i}", [P, HU]) for i in range(QUARTERS)]
        oT = m.sb("oT", [P, HG * T])
        qd = nc.dram_tensor("at0_qd", (2, 2, P, KC * T), F16).ap()
        kd = nc.dram_tensor("at0_kd", (2, 2, P, KC * S), F16).ap()
        ps_s = m.ps("scores", [P, QUARTERS, 512])
        ps_r = m.ps("ring", [P, 2, 512])
        ps_o = m.ps("o", [P, 512])
        ps_y = m.ps("y", [P, 512])
        ln = Norm(m, mhalf)
        wk_loaded, wq_loaded, wv_loaded, wo_loaded = (m.sem(n) for n in ("wk_loaded", "wq_loaded", "wv_loaded", "wo_loaded"))
        zeroed = m.sem("zeroed")
        scaled = m.sem("scaled")
        x_loaded, ctx_loaded, res_loaded = m.sems("x_loaded"), m.sems("ctx_loaded"), m.sems("res_loaded")
        xhat_ready, ring_ready, ring_free = m.sem("xhat_ready"), m.sem("ring_ready"), m.sem("ring_free")
        q_full, q_high, q_split = m.sem("q_full"), m.sem("q_high"), m.sem("q_split")
        k_full, k_high, k_split = m.sem("k_full"), m.sem("k_high"), m.sem("k_split")
        q_saved, k_saved = m.sem("q_saved"), m.sem("k_saved")
        q_stacked, k_stacked = m.sems("q_stacked"), m.sems("k_stacked")
        scores_ready, negmax_ready, exp_done = m.sem("scores_ready"), m.sem("negmax_ready"), m.sem("exp_done")
        rden_ready, vn_ready, pv_done = m.sem("rden_ready"), m.sem("vn_ready"), m.sem("pv_done")
        oT_ready, y_ready, x_ready = m.sem("oT_ready"), m.sem("y_ready"), m.sem("x_ready")
        res_ready, x_stored, sp_turns = m.sem("res_ready"), m.sems("x_stored"), m.sem("sp_turns")
        pool_turns = m.sem("pool_turns")

        with nc.Block() as block:
            @block.sync
            def _(sp):
                def hold(sem, value):
                    need(sp, sem, value)
                    sp.sem_inc(sp_turns, 1)

                def load_inputs(b, s):
                    first = isinstance(b, int) and b < 2
                    hold(xhat_ready, 0 if first else b - 1)
                    sp.dma_start(xin[s][:, :], x_in[b]).then_inc(x_loaded[s], 16)
                    hold(ring_ready, 0 if first else (b - 1) * RING)
                    sp.dma_start(ctxt[s][:, :, :], ctxT[b].rearrange("(c p) s -> p c s", p=P)).then_inc(ctx_loaded[s], 16)

                def save_keys(b, s):
                    hold(k_split, (b + 1) * KC)
                    sp.dma_start(part_save(kd[s]), part_tile(kparts[:, :, :, :])).then_inc(k_saved, 16)

                def stack_keys(b, s):
                    hold(scores_ready, (b - 1) * UNITS)
                    hold(k_saved, (b + 1) * 16)
                    for r in range(2):
                        sp.dma_start(flat(kst[s][r * 2 * DH:(r + 1) * 2 * DH, :, :]), twice(part_rows(kd[s])[r])).then_inc(k_stacked[s], 16)

                def save_queries(b, s):
                    hold(q_split, b + 1)
                    sp.dma_start(part_save(qd[s]), part_tile(qparts[:, :, :, :])).then_inc(q_saved, 16)

                def stack_queries(b, s):
                    hold(q_saved, (b + 1) * 16)
                    sp.dma_start(flat(qst[s][:, :, :]), twice(part_rows(qd[s]).rearrange("s d m -> (s d) m"))).then_inc(q_stacked[s], 16)

                def step(b, s):
                    if on(b + 2) and not (isinstance(b, int) and b < 0):
                        load_inputs(b + 2, s)
                    if on(b + 1):
                        save_keys(b + 1, 1 - s)
                    if on(b + 1):
                        save_queries(b + 1, 1 - s)
                        stack_keys(b + 1, 1 - s)
                    if on(b - 2):
                        hold(x_ready, b - 1)
                        sp.dma_start(x_out[b - 2], xout[s][:, :]).then_inc(x_stored[s], 16)
                    if on(b):
                        sp.dma_start(xres[s][:, :], x_in[b]).then_inc(res_loaded[s], 16)
                    if on(b + 1):
                        stack_queries(b + 1, 1 - s)

                def load_weights(w, src, bias, bias_src, loaded):
                    sp.dma_start(w[:, :, :], src.rearrange("(c p) n -> p c n", p=P)).then_inc(loaded, 16)
                    with nc.allow_non_contiguous_dma("one bias a partition"):
                        sp.dma_start(bias[:, :], bias_src.rearrange("(c p) -> p c", p=P)).then_inc(loaded, 16)

                load_inputs(0, 0)
                load_weights(wk, Wk, bks, bk, wk_loaded)
                load_weights(wq, Wq, bqs, bq, wq_loaded)
                load_inputs(1, 1)
                sp.dma_start(wv[:, :, :], Wv.rearrange("(c p) n -> p c n", p=P)).then_inc(wv_loaded, 16)
                sp.dma_start(bvb[:, :], bv.partition_broadcast(P)).then_inc(wv_loaded, 16)
                sp.dma_start(bob[:, :], bo.partition_broadcast(P)).then_inc(wo_loaded, 16)
                sp.dma_start(wo[:, :, :], Wo.rearrange("g p n -> p g n")).then_inc(wo_loaded, 16)
                pipeline(sp, step, 2, 2, first=4)
                for s in range(2):
                    sp.wait_ge(x_stored[s], landed(B - 2 + s, s))

            @block.gpsimd
            def _(pool):
                def clear():
                    for i in range(2):
                        pool.memset(den[i][:, :], 1.0).then_inc(zeroed, 1)
                        pool.memset(v[i][:, :, :], 0.0).then_inc(zeroed, 1)
                        pool.memset(vn[i][:, :, :, :], 0.0).then_inc(zeroed, 1)

                def step(b, s):
                    if on(b + 1):
                        pool.wait_ge(q_full, b + 2)
                        need(pool, q_saved, (b + 1) * 16)
                        pool.sem_inc(pool_turns, 1)
                        pool.tensor_copy(qparts[:, 0], qfull[:, :, :]).then_inc(q_high, 1)
                        pool.wait_ge(q_high, b + 2)
                        pool.tensor_tensor(qparts[:, 1], qfull[:, :, :], qparts[:, 0], ALU.subtract).then_inc(q_split, 1)
                    if on(b + 2):
                        ln.power(pool, b + 2)
                    if isinstance(b, int) and b == -2:
                        clear()
                    if on(b):
                        pool.wait_ge(scaled, 3)
                        pool.wait_ge(res_loaded[s], landed(b, s))
                        pool.tensor_tensor(xres[s][:, :], xres[s][:, :], bob[0:T, :], ALU.add).then_inc(res_ready, 1)
                    if on(b + 2):
                        for i in range(KC):
                            n = (b + 2) * KC + i
                            pool.wait_ge(k_full, n + 1)
                            need(pool, k_saved, (b + 2) * 16)
                            pool.sem_inc(pool_turns, 1)
                            pool.tensor_copy(kparts[:, 0, i, :], kfull[:, i, :]).then_inc(k_high, 1)
                            pool.wait_ge(k_high, n + 1)
                            pool.tensor_tensor(kparts[:, 1, i, :], kfull[:, i, :], kparts[:, 0, i, :], ALU.subtract).then_inc(k_split, 1)

                pipeline(pool, step, 2, 2, first=4)

            @block.vector
            def _(dve):
                def norm(b, s):
                    dve.wait_ge(x_loaded[s], landed(b, s))
                    ln.moments(dve, b, xin[s][:, :])

                def normed(b, s):
                    ln.newton(dve, b)
                    need(dve, ring_ready, (b - 2) * RING + NORMED + 1)
                    ln.apply(dve, b, xhat[s][:, :], xin[s][:, :]).then_inc(xhat_ready, 1)

                def take_xT(b, s):
                    dve.wait_ge(ring_ready, b * RING + NORMED + 1)
                    dve.tensor_copy(xT[s][:, :, :], ps_r[:, NORMED % 2, 0:KC * T].rearrange("p (c t) -> p c t", c=KC)).then_inc(ring_free, 1)

                def take_q(b, s):
                    dve.wait_ge(ring_ready, b * RING + QUERY + 1)
                    need(dve, q_split, b)
                    dve.tensor_tensor(qfull[:, :, :], ps_r[:, QUERY % 2, 0:KC * T].rearrange("p (c t) -> p c t", c=KC),
                                      bqs[:, :].unsqueeze(2).to_broadcast([P, KC, T]), ALU.add).then_inc(q_full, 1)
                    dve.wait_ge(q_full, b + 1)
                    dve.sem_inc(ring_free, 1)

                def take_k(b, i):
                    dve.wait_ge(ring_ready, b * RING + KEY + i + 1)
                    need(dve, k_split, (b - 1) * KC + i + 1)
                    dve.tensor_scalar(kfull[:, i, :], ps_r[:, (KEY + i) % 2, 0:S], bks[:, i:i + 1], None, ALU.add).then_inc(k_full, 1)
                    dve.wait_ge(k_full, b * KC + i + 1)
                    dve.sem_inc(ring_free, 1)

                def take_v(b, s, js, item):
                    dve.wait_ge(ring_ready, b * RING + item + 1)
                    need(dve, vn_ready, b - 1)
                    for j in js:
                        r = CHUNKS[j][1]
                        last = dve.tensor_tensor(v[s][0:r, j, :], ps_r[0:r, item % 2, (j - js[0]) * D:(j - js[0] + 1) * D],
                                                 bvb[0:r, :], ALU.add)
                    last.then_inc(ring_free, 1)

                def maxima(b, s, u):
                    r = CHUNKS[u // QUARTERS][1]
                    q = u % QUARTERS
                    dve.wait_ge(scores_ready, b * UNITS + u + 1)
                    need(dve, exp_done, b * UNITS + u - QUARTERS + 1)
                    by_head = ps_s[0:r, q, 0:HU * T].rearrange("p (h t) -> p h t", t=T)
                    dve.tensor_reduce(negmax[q][0:r, :], by_head, AX, ALU.max, negate=True).then_inc(negmax_ready, 1)

                def scale_v(b, s):
                    dve.wait_ge(exp_done, (b + 1) * UNITS)
                    need(dve, vn_ready, b)
                    dve.reciprocal(rden[:, :], den[s][:, :]).then_inc(rden_ready, 1)
                    dve.wait_ge(rden_ready, b + 1)
                    need(dve, pv_done, b - 1)
                    dve.wait_ge(ring_free, (b + 1) * RING)
                    dve.tensor_tensor(vn[s][:, :, :, 0:DH].rearrange("p j h d -> p (j h) d"),
                                      v[s][:, :, :].rearrange("p j (h d) -> p (j h) d", d=DH),
                                      rden[:, :].unsqueeze(2).to_broadcast([P, NJ * H, DH]), ALU.mult).then_inc(vn_ready, 1)

                def take_o(b):
                    dve.wait_ge(pv_done, b + 1)
                    need(dve, y_ready, b)
                    dve.tensor_copy(oT[:, :], ps_o[:, 0:HG * T]).then_inc(oT_ready, 1)

                def residual(b, s):
                    dve.wait_ge(y_ready, b + 1)
                    dve.wait_ge(res_ready, b + 1)
                    need(dve, x_stored[s], landed(b - 2, s))
                    dve.scalar_tensor_tensor(out=xout[s][:, :], in0=ps_y[0:T, 0:D], scalar=tanhg[0:T, 0:1],
                                             in1=xres[s][:, :], op0=ALU.mult, op1=ALU.add).then_inc(x_ready, 1)

                def first(b):
                    return isinstance(b, int) and b == 0

                def step(b, s):
                    for u in range(UNITS):
                        if on(b):
                            maxima(b, s, u)
                        pair, second = u // 2, u % 2
                        if not second:
                            continue
                        if pair == 0 and on(b - 1):
                            scale_v(b - 1, 1 - s)
                        if pair == 1 and on(b - 2):
                            residual(b - 2, s)
                        if on(b + 1):
                            if pair == 0:
                                take_xT(b + 1, 1 - s)
                            if pair == 1:
                                take_q(b + 1, 1 - s)
                            if pair == 2:
                                take_v(b + 1, 1 - s, (0, 1), VALUE01)
                            if pair == 3:
                                take_v(b + 1, 1 - s, (2,), VALUE2)
                        if pair in (4, 5) and on(b + 2):
                            take_k(b + 2, pair - 4)
                        if pair == 5 and on(b - 1):
                            take_o(b - 1)
                        if pair == 3 and on(b + 2) and not first(b + 2):
                            norm(b + 2, s)
                        if pair == 4 and on(b + 2) and not first(b + 2):
                            normed(b + 2, s)
                        if pair == 1 and isinstance(b, int) and b == -1:
                            dve.wait_ge(wo_loaded, 32)
                            dve.tensor_scalar(bob[:, :], bob[:, :], tanhg[:, 0:1], None, ALU.mult).then_inc(scaled, 1)
                            dve.wait_ge(wv_loaded, 32)
                            dve.wait_ge(zeroed, 6)

                norm(0, 0)
                normed(0, 0)
                dve.wait_ge(wq_loaded, 32)
                dve.tensor_scalar(wq[:, :, :], wq[:, :, :], DH ** -0.5, None, ALU.mult).then_inc(scaled, 1)
                dve.tensor_scalar(bqs[:, :], bqs[:, :], DH ** -0.5, None, ALU.mult).then_inc(scaled, 1)
                dve.wait_ge(scaled, 2)
                dve.wait_ge(wk_loaded, 32)
                pipeline(dve, step, 2, 2, first=4)

            @block.scalar
            def _(act):
                def step(b, s):
                    if not on(b):
                        return
                    need(act, pv_done, b - 1)
                    for u in range(UNITS):
                        j, r = u // QUARTERS, CHUNKS[u // QUARTERS][1]
                        act.wait_ge(negmax_ready, b * UNITS + u + 1)
                        for hh in range(HU):
                            h = u % QUARTERS * HU + hh
                            last = act.activation(
                                probs[s][0:r, j, h * T:(h + 1) * T], ps_s[0:r, u % QUARTERS, hh * T:(hh + 1) * T], ACT.Exp,
                                bias=negmax[u % QUARTERS][0:r, hh:hh + 1], accum_out=den[s][0:r, j * H + h:j * H + h + 1])
                        last.then_inc(exp_done, 1)

                act.wait_ge(zeroed, 6)
                pipeline(act, step, 2, 2, first=4)

            @block.tensor
            def _(pe):
                def ring_slot(n):
                    need(pe, ring_free, n - 1)

                def transposes(b, s):
                    ring_slot(b * RING + NORMED)
                    pe.wait_ge(xhat_ready, b + 1)
                    for c in range(KC):
                        last = pe.transpose(ps_r[:, NORMED % 2, c * T:(c + 1) * T], xhat[s][:, c * P:(c + 1) * P], ident[0:T, 0:T])
                    last.then_inc(ring_ready, 1)

                def project_q(b, s):
                    pe.wait_ge(scaled, 2)
                    pe.wait_ge(ring_free, b * RING + NORMED + 1)
                    for i in range(KC):
                        for c in range(KC):
                            last = pe.matmul(ps_r[:, QUERY % 2, i * T:(i + 1) * T], wq[:, c, i * P:(i + 1) * P], xT[s][:, c, :],
                                             start=(c == 0), stop=(c == KC - 1))
                    last.then_inc(ring_ready, 1)

                def project_k(b, s, i):
                    ring_slot(b * RING + KEY + i)
                    if i == 0:
                        pe.wait_ge(ctx_loaded[s], landed(b, s))
                    for c in range(KC):
                        last = pe.matmul(ps_r[:, (KEY + i) % 2, 0:S], wk[:, c, i * P:(i + 1) * P], ctxt[s][:, c, :],
                                         start=(c == 0), stop=(c == KC - 1))
                    last.then_inc(ring_ready, 1)

                def project_v(b, s, js, item):
                    ring_slot(b * RING + item)
                    pe.wait_ge(wv_loaded, 32)
                    for j in js:
                        s0, r = CHUNKS[j]
                        for c in range(KC):
                            last = pe.matmul(ps_r[0:r, item % 2, (j - js[0]) * D:(j - js[0] + 1) * D],
                                             ctxt[s][:, c, s0:s0 + r], wv[:, c, :], start=(c == 0), stop=(c == KC - 1))
                    last.then_inc(ring_ready, 1)

                def scores(b, s, u):
                    s0, r = CHUNKS[u // QUARTERS]
                    if u == 0:
                        pe.wait_ge(q_stacked[s], landed(b, s))
                        pe.wait_ge(k_stacked[s], landed(b, s, 2))
                    need(pe, exp_done, b * UNITS + u - QUARTERS + 1)
                    for hh in range(HU):
                        h = u % QUARTERS * HU + hh
                        last = pe.matmul(ps_s[0:r, u % QUARTERS, hh * T:(hh + 1) * T],
                                         kst[s][:, h, s0:s0 + r], qst[s][:, h, :], start=True, stop=True)
                    last.then_inc(scores_ready, 1)

                def values(b, s, g):
                    if g == 0:
                        pe.wait_ge(vn_ready, b + 1)
                        need(pe, oT_ready, b)
                    for j, (_, r) in enumerate(CHUNKS):
                        for c in range(CT):
                            h = g * CT + c
                            last = pe.matmul(ps_o[32 * c:32 * c + 32, g * T:(g + 1) * T], vn[s][0:r, j, h, :],
                                             probs[s][0:r, j, h * T:(h + 1) * T], start=(j == 0), stop=(j == NJ - 1))
                    if g == HG - 1:
                        last.then_inc(pv_done, 1)

                def project_o(b):
                    pe.wait_ge(oT_ready, b + 1)
                    need(pe, x_ready, b)
                    pe.wait_ge(wo_loaded, 32)
                    for g in range(HG):
                        last = pe.matmul(ps_y[0:T, 0:D], oT[:, g * T:(g + 1) * T], wo[:, g, :],
                                         start=(g == 0), stop=(g == HG - 1))
                    last.then_inc(y_ready, 1)

                def step(b, s):
                    for u in range(UNITS):
                        if on(b):
                            scores(b, s, u)
                        pair, second = u // 2, u % 2
                        if not second:
                            continue
                        if on(b + 1):
                            if pair == 0:
                                transposes(b + 1, 1 - s)
                            if pair == 1:
                                project_q(b + 1, 1 - s)
                            if pair == 2:
                                project_v(b + 1, 1 - s, (0, 1), VALUE01)
                            if pair == 3:
                                project_v(b + 1, 1 - s, (2,), VALUE2)
                        if pair in (4, 5) and on(b + 2):
                            project_k(b + 2, s, pair - 4)
                        if pair == 0 and on(b - 2):
                            project_o(b - 2)
                        if 1 <= pair <= HG and on(b - 1):
                            values(b - 1, 1 - s, pair - 1)

                pe.wait_ge(wk_loaded, 32)
                pipeline(pe, step, 2, 2, first=4)


def clip(n):
    return min(max(n, 0), B) if isinstance(n, int) else n


RING1 = ((("norm_x", 1), ("turn_main", -3), ("turn_aux", -3), ("turn_mix", -3), ("value_own", 0), ("value_aux2", 0)),
         (("turn_max", -1), ("query_key", 1), ("value_aux01", 0), ("key_aux0", 2), ("key_aux1", 2), ("out", -3)))


def ring1(t, name):
    for bank, order in enumerate(RING1):
        names = [n for n, _ in order]
        if name in names:
            before = clip(t + order[0][1])
            for _, off in order[1:]:
                before = before + clip(t + off)
            return bank, before + sum(on(t + off) for _, off in order[:names.index(name)])


def attend1(nc, consts, x_in, x_out, ctxT, Wqkv, bqkv, Wqkv_a, bqkv_a, Wo, bo, g):
    ident, mhalf, tanhg = consts
    with ExitStack() as ctx:
        m = Pool(nc, ctx, "at1")
        ctx.callback(m.close)
        N = 3
        KEYS = T + S
        QUARTERS = 4
        UNITS = H
        LAG = 7
        SUM_LAG = 2
        HU = H // QUARTERS
        AUGMENTED = STACK + 2
        TILES = [(0, T, 0)] + [(T + s0, r, 1) for s0, r in CHUNKS]
        CLAMP = 60000.0

        def slots(name, shape, dt=F32):
            return [m.sb(f"{name}{i}", shape, dt) for i in range(N)]

        w = m.sb("wqkv", [P, KC, 3 * D])
        wa = m.sb("wkv_aux", [P, KC, 2 * D])
        wo = m.sb("wo", [P, KC, D])
        bqk, bka = m.sb("bqk", [P, 2 * KC]), m.sb("bka", [P, KC])
        bvb, bvab, bob = m.sb("bv", [P, D]), m.sb("bv_aux", [P, D]), m.sb("bo", [P, D])
        gate, omgate, gexp = m.sb("gate", [P, H]), m.sb("omgate", [P, H]), m.sb("gexp", [P, H])
        rows = [m.sb(f"rows{i}", [H, KEYS], F16) for i in range(2)]
        ctxt, xin, xres = slots("ctx", [P, KC, S]), slots("xin", [T, D]), slots("xres", [T, D])
        xout, xhat, xT = slots("xout", [T, D]), slots("xhat", [T, D]), slots("xT", [P, KC, T])
        qkfull, kafull = m.sb("qkfull", [P, 2 * KC, T]), m.sb("kafull", [P, KC, S])
        qkparts = m.sb("qkparts", [P, 2, 2 * KC, T], F16)
        kaparts = m.sb("kaparts", [P, 2, KC, S], F16)
        qst, kst = slots("qst", [AUGMENTED, H, T], F16), slots("kst", [AUGMENTED, H, KEYS], F16)
        vm, va = slots("vm", [T, H, 32]), slots("va", [P, NJ, H, 32])
        negmax = slots("negmax", [T, 2 * H])
        shift = m.sb("shift", [2 * H, T], F16)
        probs = [m.sb(f"probs{i}", [P, HU * T]) for i in range(QUARTERS)]
        osb = [slots("om", [P, HG * T]), slots("oa", [P, HG * T])]
        rden = m.sb("rden", [T, 2 * H])
        mixed = [m.sb(f"mixed{i}", [T, D]) for i in range(2)]
        mix, mixT = m.sb("mix", [T, D]), m.sb("mixT", [P, KC, T])
        qd, kd = (nc.dram_tensor(f"at1_{n}d", (N, 2, P, KC * T), F16).ap() for n in "qk")
        kad = nc.dram_tensor("at1_kad", (N, 2, P, KC * S), F16).ap()
        ps_q = m.ps("by_query", [P, 2, 512])
        ps_k = m.ps("by_key", [P, 2, 512])
        ps_r = m.ps("ring", [P, 2, 512])
        ps_o = m.ps("o", [P, 2, 512])
        ln = Norm(m, mhalf)
        w_loaded, gexp_ready, scaled, filled, ones_set = (m.sem(n) for n in ("w_loaded", "gexp_ready", "scaled", "filled", "ones_set"))
        wa_loaded, rest_loaded = m.sem("wa_loaded"), m.sem("rest_loaded")
        rows_set = m.sem("rows_set")
        x_loaded, ctx_loaded, res_loaded, res_ready = (m.sem(n) for n in ("x_loaded", "ctx_loaded", "res_loaded", "res_ready"))
        xhat_ready = m.sem("xhat_ready")
        ring_ready = [m.sem(f"ring_ready{i}") for i in range(2)]
        ring_free = [m.sem(f"ring_free{i}") for i in range(2)]
        qk_full, qk_high, qk_split = m.sem("qk_full"), m.sem("qk_high"), m.sem("qk_split")
        ka_full, ka_high, ka_split = m.sem("ka_full"), m.sem("ka_high"), m.sem("ka_split")
        qk_saved, ka_saved = m.sem("qk_saved"), m.sem("ka_saved")
        qk_stacked, ka_stacked = m.sem("qk_stacked"), m.sem("ka_stacked")
        by_query_ready, max_done = m.sem("by_query_ready"), m.sem("max_done")
        shift_ready, shift_stacked = m.sem("shift_ready"), m.sem("shift_stacked")
        by_key_ready, exp_done, pv_done = m.sem("by_key_ready"), m.sem("exp_done"), m.sem("pv_done")
        o_taken = [m.sem("om_taken"), m.sem("oa_taken")]
        rden_ready, mixed_ready, mix_ready = m.sem("rden_ready"), m.sem("mixed_ready"), m.sem("mix_ready")
        x_ready, x_stored, sp_turns = m.sem("x_ready"), m.sem("x_stored"), m.sem("sp_turns")

        RESTS = 7

        def lagging(i, lag):
            return (-1, i - lag) if i >= lag else (-2, i + UNITS - lag)

        def exp_unit(i):
            return lagging(i, LAG)

        def sum_unit(i):
            return lagging(i, LAG + SUM_LAG)

        def slot_of(phase):
            return lambda off: (phase + off) % N

        with nc.Block() as block:
            @block.sync
            def _(sp):
                def hold(sem, value):
                    need(sp, sem, value)
                    sp.sem_inc(sp_turns, 1)

                def load_inputs(b, s):
                    hold(xhat_ready, max(b - 2, 0) if isinstance(b, int) else b - 2)
                    hold(x_loaded, b * 16)
                    sp.dma_start(xin[s][:, :], x_in[b]).then_inc(x_loaded, 16)

                def load_context(b, s):
                    bank, n = ring1(b - 3, "value_aux2")
                    need_ring = n + 1 if not isinstance(b, int) or b >= 3 else 0
                    hold(ring_ready[bank], need_ring)
                    hold(ctx_loaded, b * 16)
                    sp.dma_start(ctxt[s][:, :, :], ctxT[b].rearrange("(c p) s -> p c s", p=P)).then_inc(ctx_loaded, 16)

                def save_context_keys(b, s):
                    hold(ka_split, (b + 1) * KC)
                    sp.dma_start(part_save(kad[s]), part_tile(kaparts[:, :, :, :])).then_inc(ka_saved, 16)

                def stack_context_keys(b, s):
                    hold(by_key_ready, (b - 2) * UNITS)
                    hold(ka_saved, (b + 1) * 16)
                    hold(ka_stacked, b * 64)
                    for r in range(2):
                        key_rows(kst[s], r, T, KEYS, kad[s], ka_stacked)

                def stack_own(b, s):
                    hold(qk_split, b + 1)
                    for i, scratch in enumerate((qd, kd)):
                        sp.dma_start(part_save(scratch[s]), part_tile(qkparts[:, :, i * KC:(i + 1) * KC, :])).then_inc(qk_saved, 16)
                    hold(qk_saved, (b + 1) * 32)
                    hold(qk_stacked, b * 80)
                    sp.dma_start(flat(qst[s][0:STACK, :, :]), twice(part_rows(qd[s]).rearrange("s d m -> (s d) m"))).then_inc(qk_stacked, 16)
                    for r in range(2):
                        key_rows(kst[s], r, 0, T, kd[s], qk_stacked)

                def key_rows(stack, r, lo, hi, scratch, stacked):
                    for i in range(2):
                        sp.dma_start(stack[(2 * r + i) * DH:(2 * r + i + 1) * DH, :, lo:hi],
                                     part_rows(scratch)[r].rearrange("d (h n) -> d h n", h=H)).then_inc(stacked, 16)

                def stack_shift(b, s):
                    hold(shift_ready, b + 1)
                    hold(shift_stacked, b * 32)
                    for i in range(2):
                        sp.dma_start(qst[s][STACK + i:STACK + i + 1, :, :], shift[i * H:(i + 1) * H, :]).then_inc(shift_stacked, 16)

                def first(b):
                    return isinstance(b, int) and b < N

                def step(t, phase):
                    s = slot_of(phase)
                    if on(t + 1):
                        save_context_keys(t + 1, s(1))
                    if on(t - 1):
                        stack_shift(t - 1, s(-1))
                    if on(t + 3) and not first(t + 3):
                        load_inputs(t + 3, s(3))
                    if on(t + 2) and not first(t + 2):
                        load_context(t + 2, s(2))
                    if on(t - 2):
                        hold(x_ready, t - 4)
                        hold(res_loaded, (t - 2) * 16)
                        sp.dma_start(xres[s(-2)][:, :], x_in[t - 2]).then_inc(res_loaded, 16)
                    if on(t + 1):
                        stack_context_keys(t + 1, s(1))
                        stack_own(t + 1, s(1))
                    if on(t - 4):
                        hold(x_ready, t - 3)
                        hold(x_stored, (t - 4) * 16)
                        sp.dma_start(x_out[t - 4], xout[s(-4)][:, :]).then_inc(x_stored, 16)

                load_inputs(0, 0)
                load_context(0, 0)
                w_rows, wa_rows = (a.rearrange("(c p) n -> p c n", p=P) for a in (Wqkv, Wqkv_a))
                sp.dma_start(wa[:, :, 0:D], wa_rows[:, :, D:2 * D]).then_inc(wa_loaded, 16)
                sp.dma_start(w[:, :, 0:2 * D], w_rows[:, :, 0:2 * D]).then_inc(w_loaded, 16)
                with nc.allow_non_contiguous_dma("one bias a partition"):
                    sp.dma_start(bqk[:, :], bqkv[0:2 * D].rearrange("(c p) -> p c", p=P)).then_inc(w_loaded, 16)
                    sp.dma_start(bka[:, :], bqkv_a[D:2 * D].rearrange("(c p) -> p c", p=P)).then_inc(wa_loaded, 16)
                for b in range(1, N):
                    load_inputs(b, b)
                    load_context(b, b)
                for tile, src in ((gexp, g), (bvb, bqkv[2 * D:3 * D]), (bvab, bqkv_a[2 * D:3 * D]), (bob, bo)):
                    sp.dma_start(tile[:, :], src.partition_broadcast(P)).then_inc(rest_loaded, 16)
                sp.dma_start(w[:, :, 2 * D:3 * D], w_rows[:, :, 2 * D:3 * D]).then_inc(rest_loaded, 16)
                sp.dma_start(wa[:, :, D:2 * D], wa_rows[:, :, 2 * D:3 * D]).then_inc(rest_loaded, 16)
                sp.dma_start(wo[:, :, :], Wo.rearrange("(c p) n -> p c n", p=P)).then_inc(rest_loaded, 16)
                pipeline(sp, step, 3, 4, N, first=6)
                sp.wait_ge(x_stored, 16 * B)

            @block.gpsimd
            def _(pool):
                def fill():
                    for r in range(2):
                        pool.memset(rows[r][:, 0:T], 1.0 - r).then_inc(rows_set, 1)
                        pool.memset(rows[r][:, T:KEYS], float(r)).then_inc(rows_set, 1)
                    for i in range(N):
                        pool.memset(vm[i][:, :, DH:32], 0.0)
                        last = pool.memset(va[i][:, :, :, DH:32], 0.0)
                    last.then_inc(filled, 1)
                    pool.wait_ge(filled, 1)
                    for i in range(N):
                        pool.memset(vm[i][:, :, DH:DH + 1], 1.0)
                        last = pool.memset(va[i][:, :, :, DH:DH + 1], 1.0)
                    last.then_inc(filled, 1)

                def step(t, phase):
                    s = slot_of(phase)
                    if on(t + 1):
                        pool.wait_ge(qk_high, t + 2)
                        pool.tensor_tensor(qkparts[:, 1], qkfull[:, :, :], qkparts[:, 0], ALU.subtract).then_inc(qk_split, 1)
                    if on(t + 2):
                        ln.power(pool, t + 2)
                    if isinstance(t, int) and t == -2:
                        fill()
                    if on(t - 2):
                        pool.wait_ge(scaled, 9)
                        pool.wait_ge(res_loaded, (t - 1) * 16)
                        pool.tensor_tensor(xres[s(-2)][:, :], xres[s(-2)][:, :], bob[0:T, :], ALU.add).then_inc(res_ready, 1)
                    if on(t + 2):
                        for j in range(KC):
                            pool.wait_ge(ka_high, (t + 2) * KC + j + 1)
                            pool.tensor_tensor(kaparts[:, 1, j, :], kafull[:, j, :], kaparts[:, 0, j, :], ALU.subtract).then_inc(ka_split, 1)

                pipeline(pool, step, 2, 4, N)

            @block.vector
            def _(dve):
                def take(t, name):
                    bank, n = ring1(t, name)
                    dve.wait_ge(ring_ready[bank], n + 1)
                    return ps_r[:, bank, :], ring_free[bank]

                def norm(b, s):
                    dve.wait_ge(x_loaded, (b + 1) * 16)
                    ln.moments(dve, b, xin[s][:, :])

                def normed(b, s):
                    ln.newton(dve, b)
                    if not isinstance(b, int) or b >= N:
                        bank, n = ring1(b - 1 - N, "norm_x")
                        dve.wait_ge(ring_ready[bank], n + 1)
                    ln.apply(dve, b, xhat[s][:, :], xin[s][:, :]).then_inc(xhat_ready, 1)

                def take_query_key(t):
                    b = t + 1
                    bank, free = take(t, "query_key")
                    need(dve, qk_split, b)
                    dve.tensor_tensor(qkfull[:, :, :], bank[:, 0:2 * KC * T].rearrange("p (c t) -> p c t", t=T),
                                      bqk[:, :].unsqueeze(2).to_broadcast([P, 2 * KC, T]), ALU.add).then_inc(qk_full, 1)
                    dve.wait_ge(qk_full, b + 1)
                    dve.sem_inc(free, 1)

                def maxima(b, s, i):
                    dve.wait_ge(by_query_ready, b * UNITS + i + 1)
                    if i == 0 and (not isinstance(b, int) or b >= N):
                        bank, n = ring1(b - N + 1, "turn_max")
                        dve.wait_ge(ring_ready[bank], n + 1)
                    dve.tensor_reduce(negmax[s][:, i:i + 1], ps_q[0:T, i % 2, 0:T], AX, ALU.max, negate=True)
                    dve.tensor_reduce(negmax[s][:, H + i:H + i + 1], ps_q[0:T, i % 2, T:KEYS], AX, ALU.max, negate=True).then_inc(max_done, 1)

                def take_max(t):
                    bank, free = take(t, "turn_max")
                    need(dve, shift_stacked, (t - 1) * 32)
                    dve.tensor_scalar(shift[:, :], bank[0:2 * H, 0:T], CLAMP, -CLAMP, ALU.min, ALU.max).then_inc(shift_ready, 1)
                    dve.wait_ge(shift_ready, t)
                    dve.sem_inc(free, 1)

                def take_values(t, s):
                    bank, free = take(t, "value_aux01")
                    need(dve, pv_done, (t - 2) * UNITS)
                    for j in (0, 1):
                        r = CHUNKS[j][1]
                        last = dve.tensor_tensor(va[s][0:r, j, :, 0:DH], heads(bank[0:r, j * D:(j + 1) * D]),
                                                 heads(bvab[0:r, :]), ALU.add)
                    last.then_inc(free, 1)

                def take_values2(t, s):
                    bank, free = take(t, "value_aux2")
                    r = CHUNKS[2][1]
                    dve.tensor_tensor(va[s][0:r, 2, :, 0:DH], heads(bank[0:r, 0:D]), heads(bvab[0:r, :]), ALU.add).then_inc(free, 1)

                def take_values_own(t, s):
                    bank, free = take(t, "value_own")
                    need(dve, pv_done, (t - 2) * UNITS)
                    dve.tensor_tensor(vm[s][:, :, 0:DH], heads(bank[0:T, 0:D]), heads(bvb[0:T, :]), ALU.add).then_inc(free, 1)

                def normalize(t, i):
                    b = t - 3
                    bank, free = take(t, ("turn_main", "turn_aux")[i])
                    by_head = bank[0:T, :].rearrange("p (h e) -> p h e", e=32)
                    need(dve, mix_ready, b)
                    dve.reciprocal(rden[:, i * H:(i + 1) * H], by_head[:, :, DH]).then_inc(rden_ready, 1)
                    dve.wait_ge(rden_ready, b * 2 + i + 1)
                    dve.tensor_tensor(heads(mixed[i][:, :]), by_head[:, :, 0:DH],
                                      rden[:, i * H:(i + 1) * H].unsqueeze(2).to_broadcast([T, H, DH]), ALU.mult).then_inc(free, 1)
                    if i == 1:
                        dve.wait_ge(free, ring1(t, "turn_aux")[1] + 1)
                        if not isinstance(b, int) or b >= 1:
                            bank1, n1 = ring1(t - 1, "turn_mix")
                            dve.wait_ge(ring_ready[bank1], n1 + 1)
                        dve.tensor_tensor(mix[:, :], mixed[0][:, :], mixed[1][:, :], ALU.add).then_inc(mix_ready, 1)

                def residual(t, s):
                    b = t - 3
                    bank, free = take(t, "out")
                    dve.wait_ge(res_ready, b + 1)
                    need(dve, x_stored, (b - 2) * 16)
                    dve.scalar_tensor_tensor(out=xout[s][:, :], in0=bank[0:T, 0:D], scalar=tanhg[0:T, 0:1],
                                             in1=xres[s][:, :], op0=ALU.mult, op1=ALU.add).then_inc(x_ready, 1)
                    dve.wait_ge(x_ready, b + 1)
                    dve.sem_inc(free, 1)

                def first(b):
                    return isinstance(b, int) and b == 0

                def step(t, phase):
                    s = slot_of(phase)
                    for u in range(UNITS):
                        if on(t):
                            maxima(t, s(0), u)
                        i = u // 2
                        if u % 2 == 0:
                            continue
                        if i == 0 and on(t - 1):
                            take_max(t)
                        if i == 1 and on(t - 3):
                            normalize(t, 0)
                        if i == 1 and on(t + 2) and not first(t + 2):
                            norm(t + 2, s(2))
                        if i == 2 and on(t + 1):
                            take_query_key(t)
                        if i == 3 and on(t - 3):
                            normalize(t, 1)
                        if i == 4 and on(t):
                            take_values(t, s(0))
                        if i == 5 and on(t + 2) and not first(t + 2):
                            normed(t + 2, s(2))
                        if i == 6 and on(t):
                            take_values_own(t, s(0))
                        if i == 3 and isinstance(t, int) and t == -1:
                            scale_rest()
                        if i == 7 and on(t):
                            take_values2(t, s(0))
                        if i == 7 and on(t - 3):
                            residual(t, s(-3))

                def scale_rest():
                    dve.wait_ge(rest_loaded, 16 * RESTS)
                    dve.tensor_scalar(bob[:, :], bob[:, :], tanhg[:, 0:1], None, ALU.mult).then_inc(scaled, 1)
                    dve.wait_ge(gexp_ready, 1)
                    dve.tensor_scalar(omgate[:, :], gexp[:, :], 1.0, None, ALU.add).then_inc(scaled, 1)
                    dve.wait_ge(scaled, 4)
                    dve.reciprocal(gate[:, :], omgate[:, :]).then_inc(scaled, 1)
                    dve.wait_ge(scaled, 5)
                    dve.tensor_scalar(omgate[:, :], gate[:, :], -1.0, 1.0, ALU.mult, ALU.add)
                    dve.tensor_tensor(heads(bvab[:, :]), heads(bvab[:, :]), gate[:, :].unsqueeze(2).to_broadcast([P, H, DH]),
                                      ALU.mult).then_inc(scaled, 1)
                    dve.wait_ge(scaled, 6)
                    dve.tensor_tensor(heads(bvb[:, :]), heads(bvb[:, :]), omgate[:, :].unsqueeze(2).to_broadcast([P, H, DH]),
                                      ALU.mult).then_inc(scaled, 1)
                    for c in range(KC):
                        dve.tensor_tensor(heads(w[:, c, 2 * D:3 * D]), heads(w[:, c, 2 * D:3 * D]),
                                          omgate[:, :].unsqueeze(2).to_broadcast([P, H, DH]), ALU.mult)
                        last = dve.tensor_tensor(heads(wa[:, c, D:2 * D]), heads(wa[:, c, D:2 * D]),
                                                 gate[:, :].unsqueeze(2).to_broadcast([P, H, DH]), ALU.mult)
                    last.then_inc(scaled, 2)
                    dve.wait_ge(scaled, 9)

                norm(0, 0)
                normed(0, 0)
                dve.wait_ge(w_loaded, 16 * 2)
                dve.tensor_scalar(w[:, :, 0:D], w[:, :, 0:D], DH ** -0.5, None, ALU.mult).then_inc(scaled, 1)
                dve.tensor_scalar(bqk[:, 0:KC], bqk[:, 0:KC], DH ** -0.5, None, ALU.mult).then_inc(scaled, 1)
                dve.wait_ge(scaled, 2)
                pipeline(dve, step, 2, 4, N)

            @block.scalar
            def _(act):
                def take(t, name):
                    bank, n = ring1(t, name)
                    act.wait_ge(ring_ready[bank], n + 1)
                    return ps_r[:, bank, :], ring_free[bank]

                def take_x(t, s):
                    bank, free = take(t, "norm_x")
                    act.activation(xT[s][:, :, :], bank[:, 0:KC * T].rearrange("p (c t) -> p c t", c=KC), ACT.Copy).then_inc(free, 1)

                def exponents(b, k):
                    n = b * UNITS + k
                    r = TILES[k // QUARTERS][1]
                    act.wait_ge(by_key_ready, n + 1)
                    need(act, pv_done, n - QUARTERS + 1)
                    act.activation(probs[k % QUARTERS][0:r, :], ps_k[0:r, k % 2, 0:HU * T], ACT.Exp).then_inc(exp_done, 1)

                def take_o(b, s, i):
                    act.wait_ge(pv_done, b * UNITS + (QUARTERS, UNITS)[i])
                    if not isinstance(b, int) or b >= N:
                        bank, n = ring1(b, ("turn_main", "turn_aux")[i])
                        act.wait_ge(ring_ready[bank], n + 1)
                    act.activation(osb[i][s][:, :], ps_o[:, i, 0:HG * T], ACT.Copy).then_inc(o_taken[i], 1)

                def step(t, phase):
                    s = slot_of(phase)
                    for u in range(UNITS):
                        off, k = exp_unit(u)
                        b = t + off
                        if on(b):
                            exponents(b, k)
                        i = u // 2
                        if u % 2 == 0:
                            continue
                        if i == 0 and on(t + 1):
                            take_x(t, s(1))
                        if i == 2 and on(t + 1):
                            act.wait_ge(qk_full, t + 2)
                            need(act, qk_saved, (t + 1) * 32)
                            act.activation(qkparts[:, 0], qkfull[:, :, :], ACT.Copy).then_inc(qk_high, 1)
                        if i == 4 and on(t - 3):
                            bank, free = take(t, "turn_mix")
                            act.activation(mixT[:, :, :], bank[:, 0:KC * T].rearrange("p (c t) -> p c t", c=KC), ACT.Copy).then_inc(free, 1)
                        if i == 4 and on(t - 2):
                            take_o(t - 2, s(-2), 1)
                        if i in (5, 6) and on(t + 2):
                            j = i - 5
                            n = (t + 2) * KC + j
                            bank, free = take(t, f"key_aux{j}")
                            need(act, ka_split, n - 1)
                            act.activation(kafull[:, j, :], bank[:, 0:S], ACT.Identity, bias=bka[:, j:j + 1]).then_inc(ka_full, 1)
                            need(act, ka_saved, (t + 2) * 16)
                            act.wait_ge(ka_full, n + 1)
                            act.sem_inc(free, 1)
                            act.activation(kaparts[:, 0, j, :], kafull[:, j, :], ACT.Copy).then_inc(ka_high, 1)
                        if i == 6 and on(t - 1):
                            take_o(t - 1, s(-1), 0)
                        if i == 3 and isinstance(t, int) and t == -1:
                            act.wait_ge(rest_loaded, 16 * RESTS)
                            act.activation(gexp[:, :], gexp[:, :], ACT.Exp, scale=-1.0).then_inc(gexp_ready, 1)
                        if i == 7 and isinstance(t, int) and t == -1:
                            act.wait_ge(rows_set, 4)
                            for stack in kst:
                                for r in range(2):
                                    act.dma_start(stack[STACK + r:STACK + r + 1, :, :], rows[r][:, :]).then_inc(ones_set, 16)

                pipeline(act, step, 2, 4, N)

            @block.tensor
            def _(pe):
                def into(t, name):
                    bank, n = ring1(t, name)
                    need(pe, ring_free[bank], n)
                    return ps_r[:, bank, :], ring_ready[bank]

                def turn_max(t, s):
                    bank, ready = into(t, "turn_max")
                    pe.wait_ge(max_done, t * UNITS)
                    pe.transpose(bank[0:2 * H, 0:T], negmax[s][:, :], ident[0:T, 0:T]).then_inc(ready, 1)

                def norm_x(t, s):
                    bank, ready = into(t, "norm_x")
                    pe.wait_ge(xhat_ready, t + 2)
                    for c in range(KC):
                        last = pe.transpose(bank[:, c * T:(c + 1) * T], xhat[s][:, c * P:(c + 1) * P], ident[0:T, 0:T])
                    last.then_inc(ready, 1)

                def query_key(t, s):
                    bank, ready = into(t, "query_key")
                    pe.wait_ge(scaled, 2)
                    b0, n0 = ring1(t, "norm_x")
                    pe.wait_ge(ring_free[b0], n0 + 1)
                    for i in range(2 * KC):
                        for c in range(KC):
                            last = pe.matmul(bank[:, i * T:(i + 1) * T], w[:, c, i * P:(i + 1) * P], xT[s][:, c, :],
                                             start=(c == 0), stop=(c == KC - 1))
                    last.then_inc(ready, 1)

                def key_aux(t, s, i):
                    bank, ready = into(t, f"key_aux{i}")
                    if i == 0:
                        pe.wait_ge(ctx_loaded, (t + 3) * 16)
                    for c in range(KC):
                        last = pe.matmul(bank[:, 0:S], wa[:, c, i * P:(i + 1) * P], ctxt[s][:, c, :],
                                         start=(c == 0), stop=(c == KC - 1))
                    last.then_inc(ready, 1)

                def value(bank, at, r, lhs, rhs):
                    for c in range(KC):
                        last = pe.matmul(bank[0:r, at:at + D], lhs(c), rhs(c), start=(c == 0), stop=(c == KC - 1))
                    return last

                def values01(t, s):
                    bank, ready = into(t, "value_aux01")
                    pe.wait_ge(scaled, 9)
                    for j in (0, 1):
                        s0, r = CHUNKS[j]
                        last = value(bank, j * D, r, lambda c: ctxt[s][:, c, s0:s0 + r], lambda c: wa[:, c, D:2 * D])
                    last.then_inc(ready, 1)

                def values2(t, s):
                    bank, ready = into(t, "value_aux2")
                    s0, r = CHUNKS[2]
                    value(bank, 0, r, lambda c: ctxt[s][:, c, s0:s0 + r], lambda c: wa[:, c, D:2 * D]).then_inc(ready, 1)

                def values_own(t, s):
                    bank, ready = into(t, "value_own")
                    value(bank, 0, T, lambda c: xT[s][:, c, :], lambda c: w[:, c, 2 * D:3 * D]).then_inc(ready, 1)

                def by_query(b, s, i):
                    if i == 0:
                        pe.wait_ge(qk_stacked, (b + 1) * 80)
                        pe.wait_ge(ka_stacked, (b + 1) * 64)
                    need(pe, max_done, b * UNITS + i - 1)
                    pe.matmul(ps_q[0:T, i % 2, 0:KEYS], qst[s][0:STACK, i, :], kst[s][0:STACK, i, :],
                              start=True, stop=True).then_inc(by_query_ready, 1)

                def by_key(b, s, k):
                    k0, r, _ = TILES[k // QUARTERS]
                    if k == 0:
                        pe.wait_ge(ones_set, 16 * 2 * N)
                        pe.wait_ge(shift_stacked, (b + 1) * 32)
                    need(pe, exp_done, b * UNITS + k - 1)
                    for hh in range(HU):
                        h = k % QUARTERS * HU + hh
                        last = pe.matmul(ps_k[0:r, k % 2, hh * T:(hh + 1) * T], kst[s][:, h, k0:k0 + r],
                                         qst[s][:, h, :], start=True, stop=True)
                    last.then_inc(by_key_ready, 1)

                def sum_up(b, s, k):
                    j, quarter = k // QUARTERS, k % QUARTERS
                    _, r, aux = TILES[j]
                    pe.wait_ge(exp_done, b * UNITS + k + 1)
                    if k == 0:
                        pe.wait_ge(filled, 2)
                    if k in (0, QUARTERS):
                        need(pe, o_taken[aux], b)
                    for hh in range(HU):
                        h = quarter * HU + hh
                        g, c = h // CT, h % CT
                        vals = va[s][0:r, j - 1, h, :] if aux else vm[s][:, h, :]
                        last = pe.matmul(ps_o[32 * c:32 * c + 32, aux, g * T:(g + 1) * T], vals,
                                         probs[quarter][0:r, hh * T:(hh + 1) * T],
                                         start=(j in (0, 1) and h < CT), stop=(j in (0, NJ)), skip_group_check=True)
                    last.then_inc(pv_done, 1)

                def turn_sums(t, s, i):
                    bank, ready = into(t, ("turn_main", "turn_aux")[i])
                    pe.wait_ge(o_taken[i], t - 2)
                    for g_ in range(HG):
                        last = pe.transpose(bank[0:T, g_ * P:(g_ + 1) * P], osb[i][s][:, g_ * T:(g_ + 1) * T], ident[:, :])
                    last.then_inc(ready, 1)

                def turn_mix(t):
                    bank, ready = into(t, "turn_mix")
                    pe.wait_ge(mix_ready, t - 2)
                    for c in range(KC):
                        last = pe.transpose(bank[:, c * T:(c + 1) * T], mix[:, c * P:(c + 1) * P], ident[0:T, 0:T])
                    last.then_inc(ready, 1)

                def project_out(t):
                    bank, ready = into(t, "out")
                    b0, n0 = ring1(t, "turn_mix")
                    pe.wait_ge(ring_free[b0], n0 + 1)
                    value(bank, 0, T, lambda c: mixT[:, c, :], lambda c: wo[:, c, :]).then_inc(ready, 1)

                def step(t, phase):
                    s = slot_of(phase)
                    for u in range(UNITS):
                        if on(t):
                            by_query(t, s(0), u)
                        off, k = exp_unit(u)
                        b = t + off
                        if on(b):
                            by_key(b, s(off), k)
                        off, k = sum_unit(u)
                        b = t + off
                        if on(b):
                            sum_up(b, s(off), k)
                        i = u // 2
                        if u % 2 == 0:
                            continue
                        if i == 0 and on(t + 1):
                            norm_x(t, s(1))
                        if i == 0 and on(t - 1):
                            turn_max(t, s(-1))
                        if i == 0 and on(t - 3):
                            turn_sums(t, s(-3), 0)
                        if i == 2 and on(t + 1):
                            query_key(t, s(1))
                        if i == 2 and on(t - 3):
                            turn_sums(t, s(-3), 1)
                        if i == 3 and on(t):
                            values01(t, s(0))
                        if i == 4 and on(t - 3):
                            turn_mix(t)
                        if i == 5 and on(t):
                            values_own(t, s(0))
                        if i in (5, 6) and on(t + 2):
                            key_aux(t, s(2), i - 5)
                        if i == 7 and on(t):
                            values2(t, s(0))
                        if i == 7 and on(t - 3):
                            project_out(t)

                pe.wait_ge(wa_loaded, 16 * 2)
                pipeline(pe, step, 2, 4, N)


class Chain:

    def __init__(self, eng, sem):
        self.eng, self.sem, self.n = eng, sem, 0

    def __call__(self, instruction):
        instruction.then_inc(self.sem, 1)
        self.n += 1
        self.eng.wait_ge(self.sem, self.n)


def rounds(eng, step, lead, tail, count, n=3):
    def placed(phase, rnd):
        return lambda off: ((phase + off) % n, rnd + (phase + off) // n)

    lo, hi = -(-tail // n), (count - lead) // n
    for t in range(-lead, lo * n):
        step(t, placed(t % n, t // n))
    with eng.Fori(lo, hi) as rnd:
        for phase in range(n):
            step(rnd * n + phase, placed(phase, rnd))
    for t in range(hi * n, count + tail):
        step(t, placed(t % n, t // n))


def experts(nc, consts, name, x_in, x_out, router, router_b, pack1, pack2, b2, top, ff, shared):
    ident, mhalf, tanhg = consts
    with ExitStack() as ctx:
        m = Pool(nc, ctx, name)
        ctx.callback(m.close)
        N = 3
        E = router.shape[1]
        TOK = B * T
        TILES = (TOK * top + E * (P - 1)) // P
        ALL = -(-TOK // P)
        NT = TILES
        FC = ff // P
        UNIT = 4
        U = FC // UNIT
        B1 = KC * ff
        GB, NG = 4, B // 4
        CB = top * B
        PAD_ROW = TOK * top
        BIG = -3.0e38

        xs, xhat = m.sb("x", [T, B, D]), m.sb("xhat", [T, B, D])
        xhd = nc.dram_tensor(f"{name}_normed", (TOK, D), F32).ap()
        ways = nc.dram_tensor(f"{name}_results", (PAD_ROW + TILES * P, D), F32).ap()
        stats, mv = m.sb("stats", [T, B, 6]), m.sb("mv", [T, B, 2])
        var, r0, newt, rstd = (m.sb(n, [T, B]) for n in ("var", "r0", "newt", "rstd"))
        rw, rb = m.sb("router", [P, KC, E]), m.sb("router_b", [P, E])
        xTr = None if shared else [m.sb(f"xTr{i}", [P, KC, 2 * T]) for i in range(2)]
        tri, ones = m.sb("tri", [T, T]), m.sb("ones", [T, P])
        cols = m.sb("cols", [P, P])
        steps_of_p = m.sb("steps_of_p", [P, ALL])
        rev = m.sb("rev", [P, E])
        before = m.sb("before", [P, E, E])
        tok = m.sb("tok", [T, B])
        pad_row = m.sb("pad_row", [P, TILES])
        sel, key, mask = (m.sb(n, [T, B, E]) for n in ("sel", "key", "mask"))
        rowmax = m.sb("rowmax", [T, B])
        value = m.sb("value", [T, top, B])
        pick = m.sb("pick", [T, top, B, E])
        gates = m.sb("gates", [T, top, B])
        norm_sum, norm_rec = m.sb("norm_sum", [T, B]), m.sb("norm_rec", [T, B])
        picked = m.sb("picked", [T, top, B, E])
        rank, first = m.sb("rank", [T, CB]), m.sb("first", [T, CB])
        above = m.sb("above", [T, CB, ALL])
        tile_of, lane_of = m.sb("tile_of", [T, CB]), m.sb("lane_of", [T, CB])
        full = m.sb("full", [T, E, ALL])
        tiles_of, start, end = (m.sb(n, [T, E]) for n in ("tiles_of", "start", "end"))
        below = m.sb("below", [T, E, E])
        ranks = m.sb("ranks", [T, B, E])
        running = [m.sb(f"running{i}", [T, B, E]) for i in range(2)]
        in_tile = m.sb("in_tile", [T, CB, TILES], F16)
        tile_vals = m.sb("tile_vals", [T, CB, 2, TILES], F16)
        in_lane = m.sb("in_lane", [T, CB, P], F16)
        passed = m.sb("passed", [1, TILES, E])
        expert_f = m.sb("expert_f", [1, TILES])
        expert_of = m.sb("expert_of", [1, NT], I32)
        row_f, empty = m.sb("row_f", [P, TILES]), m.sb("empty", [P, TILES])
        from_row, to_row = m.sb("from_row", [P, NT], U32), m.sb("to_row", [P, NT], U32)
        def slots(what, shape, dt=F32):
            return [m.sb(f"{what}{i}", shape, dt) for i in range(N)]

        w1, w2 = slots("w1_", [P, B1 + FC]), slots("w2_", [P, FC * D])
        gi, si = slots("from", [P, 1], U32), slots("to", [P, 1], U32)
        xt, xT, hT, yt = slots("xt", [P, D]), slots("xT", [P, KC, P]), slots("hT", [P, FC, P]), slots("yt", [P, D])
        PARTS_N = 2 * NG
        if not shared:
            parts = [m.sb(f"ways{i}", [T, GB, D])[:, :, :] for i in range(PARTS_N - NG)]
            b2all = m.sb("b2", [P, E, D])[:, :, :]
        else:
            sw1_in, sb1_in, sw2_in, sb2_in = shared
            FS = sw1_in.shape[1] // P
            GT = GB * T
            sw = m.sb("sw", [P, KC * FS * P + FS * D])
            sw1 = sw[:, 0:KC * FS * P].rearrange("p (c f) -> p c f", c=KC)
            sw2 = sw[:, KC * FS * P:].rearrange("p (c d) -> p c d", d=D)
            b2all = sw[:, 0:E * D].rearrange("p (e d) -> p e d", d=D)
            sb1, sb2 = m.sb("sb1", [P, FS]), m.sb("sb2", [P, D])
            sxT = m.sb("sxT", [P, KC, TOK])
            shT = [m.sb(f"shT{i}", [P, FS, GT]) for i in range(2)]
            parts = [shT[i // 2][0:T, :, :].rearrange("p f g -> p (f g)")[:, i % 2 * GB * D:(i % 2 + 1) * GB * D]
                     .rearrange("p (b d) -> p b d", d=D) for i in range(PARTS_N - NG)]
            addend = m.sb("addend", [T, B, D])
        parts += [xhat[:, g * GB:(g + 1) * GB, :] for g in range(NG)]
        ps_h = m.ps("h", [P, N, 512])
        ps_y = m.ps("y", [P, N, 512])
        ps_t = m.ps("t", [P, 2, 512])

        x_in_done = [m.sem(f"x_loaded{g}") for g in range(NG)]
        w_loaded, consts_set, half_set = m.sem("w_loaded"), m.sem("consts_set"), m.sem("half_set")
        stats_ready, root_ready, newton_step = m.sem("stats_ready"), m.sem("root_ready"), m.sem("newton_step")
        xhat_ready, xhat_saved = m.sem("xhat_ready"), m.sem("xhat_saved")
        turned, turned_taken, logits_ready = m.sem("turned"), m.sem("turned_taken"), m.sem("logits_ready")
        route_step, exp_in, exp_out = m.sem("route_step"), m.sem("exp_in"), m.sem("exp_out")
        mask_ready, ranks_ready, onehots_ready, table_ready = (m.sem(n) for n in ("mask_ready", "ranks_ready", "onehots_ready", "table_ready"))
        expert_ready, rows_ready = m.sem("expert_ready"), m.sem("rows_ready")
        w1_in, w2_in = [m.sem(f"w1_in{i}") for i in range(N)], [m.sem(f"w2_in{i}") for i in range(N)]
        gathered, scattered = [m.sem(f"gathered{i}") for i in range(N)], [m.sem(f"scattered{i}") for i in range(N)]
        from_ready, to_ready = m.sem("from_ready"), m.sem("to_ready")
        xT_ready, xT_taken, h_ready, h_taken = (m.sem(n) for n in ("xT_ready", "xT_taken", "h_ready", "h_taken"))
        y_ready, y_taken = m.sem("y_ready"), m.sem("y_taken")
        sp_turns, pool_turns, dve_turns = m.sem("sp_turns"), m.sem("pool_turns"), m.sem("dve_turns")
        ways_in = [m.sem(f"ways_in{i}") for i in range(PARTS_N)]
        b2_loaded = m.sem("b2_loaded")
        sw_loaded, sh_ready, sh_taken, sy_ready, sy_taken, sx_ready, base_step, sb2_ready = (
            m.sem(n) for n in ("sw_loaded", "sh_ready", "sh_taken", "sy_ready", "sy_taken", "sx_ready", "base_step", "sb2_ready"))
        added, x_stored = m.sem("added"), m.sem("x_stored")
        weighted, last_added = m.sem("weighted"), m.sem("last_added")
        weighted_row = [m.sb(f"weighted{i}", [T, D]) for i in range(2)]

        def turned_in(i):
            return sxT[:, :, i * 2 * T:(i + 1) * 2 * T] if shared else xTr[i % 2][:, :, :]

        def shared_bank(n):
            return (ps_h[0:T, 2, 0:D], ps_t[0:T, 1, 0:D])[n % 2]

        def col(t):
            return slice(t, t + 1) if isinstance(t, int) else bass.ds(t, 1)

        def live(t):
            return not isinstance(t, int) or 0 <= t < NT

        with nc.Block() as block:
            @block.sync
            def _(sp):
                def hold(sem, value):
                    need(sp, sem, value)
                    sp.sem_inc(sp_turns, 1)

                def expert(t):
                    return sp.value_load(expert_of[0:1, col(t)], min_val=0, max_val=pack1.shape[0] - 1)

                def load_in(t, s, rnd):
                    hold(h_ready, (t - N + 1) * U)
                    hold(h_taken, (t - N + 1) * U)
                    sp.dma_start(w1[s][:, :], pack1[bass.ds(expert(t), 1)].rearrange("o p n -> p (o n)")).then_inc(w1_in[s], 16)

                def load_out(t, s, rnd):
                    hold(y_ready, t - N + 1)
                    sp.dma_start(w2[s][:, :], pack2[bass.ds(expert(t), 1)].rearrange("o p n -> p (o n)")).then_inc(w2_in[s], 16)

                def step(t, at):
                    if live(t + 3):
                        load_in(t + 3, *at(3))
                    if live(t + 2):
                        load_out(t + 2, *at(2))

                def store(g):
                    sp.wait_ge(added, (g + 1) * top * (GB - 1))
                    sp.wait_ge(last_added, (g + 1) * top)
                    sp.dma_start(x_out[g * GB:(g + 1) * GB].rearrange("b t d -> t b d"),
                                 xs[:, g * GB:(g + 1) * GB, :]).then_inc(x_stored, 16)

                for g in range(NG):
                    sp.dma_start(xs[:, g * GB:(g + 1) * GB, :],
                                 x_in[g * GB:(g + 1) * GB].rearrange("b t d -> t b d")).then_inc(x_in_done[g], 16)
                sp.dma_start(rw[:, :, :], router.rearrange("(c p) e -> p c e", p=P)).then_inc(w_loaded, 16)
                if router_b is not None:
                    sp.dma_start(rb[:, :], router_b.partition_broadcast(P)).then_inc(w_loaded, 16)
                if shared:
                    sp.dma_start(sw1[:, :, :], sw1_in.rearrange("(c p) f -> p c f", p=P)).then_inc(sw_loaded, 16)
                    with nc.allow_non_contiguous_dma("one bias a partition"):
                        sp.dma_start(sb1[:, :], sb1_in.rearrange("(c p) -> p c", p=P)).then_inc(sw_loaded, 16)
                    sp.dma_start(sw2[:, :, :], sw2_in.rearrange("(c p) d -> p c d", p=P)).then_inc(sw_loaded, 16)
                    sp.dma_start(sb2[:, :], sb2_in.partition_broadcast(P)).then_inc(sw_loaded, 16)
                else:
                    sp.dma_start(b2all, b2.partition_broadcast(P)).then_inc(b2_loaded, 16)
                for g in range(NG):
                    sp.wait_ge(xhat_ready, (g + 1) * GB)
                    sp.dma_start(xhd[g * GB * T:(g + 1) * GB * T].rearrange("(b t) d -> t b d", t=T),
                                 xhat[:, g * GB:(g + 1) * GB, :]).then_inc(xhat_saved, 16)
                sp.wait_ge(expert_ready, 1)
                rounds(sp, step, 3, 1, NT)
                for s in range(N):
                    sp.wait_ge(scattered[s], 16 * len(range(s, NT, N)))
                if shared:
                    sp.wait_ge(sy_ready, B)
                for i in range(NG * top):
                    g, way = i // top, i % top
                    need(sp, added, (i - PARTS_N + 1) * (GB - 1))
                    need(sp, weighted, i - PARTS_N + 1)
                    row = way * TOK + g * GB * T
                    sp.dma_start(parts[i % PARTS_N][:, :, :],
                                 ways[row:row + GB * T].rearrange("(b t) d -> t b d", t=T)).then_inc(ways_in[i % PARTS_N], 16)
                    if i >= PARTS_N and (i - PARTS_N) % top == top - 1:
                        store((i - PARTS_N) // top)
                for g in range((NG * top - PARTS_N) // top, NG):
                    store(g)
                sp.wait_ge(x_stored, 16 * NG)

            @block.gpsimd
            def _(pool):
                def hold(sem, value):
                    need(pool, sem, value)
                    pool.sem_inc(pool_turns, 1)

                def gather(t, s, rnd):
                    hold(xT_ready, t - N + 1)
                    hold(from_ready, t + 1)
                    pool.indirect_dma_start(xt[s][:, :], None, xhd, bass.IndirectOffsetOnAxis(gi[s][:, :], 0)).then_inc(gathered[s], 16)

                def scatter(t, s, rnd):
                    hold(y_taken, t + 1)
                    hold(to_ready, t + 1)
                    pool.indirect_dma_start(ways, bass.IndirectOffsetOnAxis(si[s][:, :], 0), yt[s][:, :], None).then_inc(scattered[s], 16)

                def step(t, at):
                    if live(t + 3):
                        gather(t + 3, *at(3))
                    if live(t - 1):
                        scatter(t - 1, *at(-1))

                iota = pool.iota
                imprecise = dict(allow_small_or_imprecise_dtypes=True)
                pool.memset(ones[:, :], 1.0).then_inc(half_set, 1)
                pool.memset(before[:, :, :], 1.0).then_inc(half_set, 1)
                iota(cols[:, :], pattern=[[1, P]], base=0, channel_multiplier=0, **imprecise).then_inc(consts_set, 1)
                iota(steps_of_p[:, :], pattern=[[P, ALL]], base=0, channel_multiplier=0, **imprecise).then_inc(consts_set, 1)
                iota(rev[:, :], pattern=[[-1, E]], base=E, channel_multiplier=0, **imprecise).then_inc(consts_set, 1)
                iota(tok[:, :], pattern=[[T, B]], base=0, channel_multiplier=1, **imprecise).then_inc(consts_set, 1)
                iota(pad_row[:, :], pattern=[[P, TILES]], base=PAD_ROW + TOK, channel_multiplier=1, **imprecise).then_inc(consts_set, 1)
                pool.wait_ge(half_set, 2)
                pool.affine_select(out=tri[:, :], in_=ones[:, 0:T], compare_op=ALU.is_gt, fill=0.0, base=0,
                                   pattern=[[1, T]], channel_multiplier=-1).then_inc(consts_set, 1)
                pool.affine_select(out=before[:, :, :], in_=before[:, :, :], compare_op=ALU.is_gt, fill=0.0, base=0,
                                   pattern=[[1, E], [-1, E]], channel_multiplier=0).then_inc(consts_set, 1)
                for g in range(NG):
                    at = slice(g * GB, (g + 1) * GB)
                    pool.wait_ge(stats_ready, (g + 1))
                    pool.tensor_tensor(r0[:, at], var[:, at], mhalf[0:T, :].to_broadcast([T, GB]), ALU.pow).then_inc(root_ready, 1)
                def add_shared(n):
                    pool.wait_ge(sy_taken, n + 1)
                    pool.tensor_tensor(xs[:, n, :], xs[:, n, :], addend[:, n, :], ALU.add).then_inc(base_step, 1)

                if shared:
                    pool.wait_ge(sb2_ready, 1)
                    for n in range(B):
                        pool.wait_ge(sx_ready, n + 1)
                        pool.tensor_tensor(xs[:, n, :], xs[:, n, :], addend[:, n, :], ALU.add).then_inc(base_step, 1)
                    for n in range(B):
                        pool.wait_ge(base_step, B)
                        pool.tensor_tensor(xs[:, n, :], xs[:, n, :], sb2[0:T, :], ALU.add).then_inc(base_step, 1)
                    pool.wait_ge(base_step, 2 * B)
                    for n in range(B - GB):
                        add_shared(n)
                pool.wait_ge(xhat_saved, 16 * NG)
                rounds(pool, step, 3, 1, NT)
                if shared:
                    for n in range(B - GB, B):
                        add_shared(n)
                    pool.wait_ge(base_step, 3 * B)
                for i in range(NG * top):
                    b = i // top * GB + GB - 1
                    pool.wait_ge(weighted, i + 1)
                    need(pool, last_added, i if i % top else 0)
                    pool.tensor_tensor(xs[:, b, :], xs[:, b, :], weighted_row[i % 2][:, :], ALU.add).then_inc(last_added, 1)

            @block.vector
            def _(dve):
                norm_then = Chain(dve, newton_step)

                def moments(g):
                    dve.wait_ge(x_in_done[g], 16)
                    for b in range(g * GB, (g + 1) * GB):
                        last = dve.bn_stats(stats[:, b, :], xs[:, b, :])
                    norm_then(last)
                    for b in range(g * GB, (g + 1) * GB):
                        last = dve.bn_aggr(mv[:, b, :], stats[:, b, :])
                    norm_then(last)
                    at = slice(g * GB, (g + 1) * GB)
                    dve.tensor_scalar(var[:, at], mv[:, at, 1], EPS, None, ALU.add).then_inc(stats_ready, 1)

                def normed(g):
                    at = slice(g * GB, (g + 1) * GB)
                    dve.wait_ge(stats_ready, g + 1)
                    dve.wait_ge(root_ready, g + 1)
                    norm_then(dve.tensor_tensor(newt[:, at], r0[:, at], r0[:, at], ALU.mult))
                    norm_then(dve.tensor_tensor(newt[:, at], newt[:, at], var[:, at], ALU.mult))
                    norm_then(dve.tensor_scalar(newt[:, at], newt[:, at], -0.5, 1.5, ALU.mult, ALU.add))
                    norm_then(dve.tensor_tensor(rstd[:, at], r0[:, at], newt[:, at], ALU.mult))
                    for b in range(g * GB, (g + 1) * GB):
                        dve.tensor_scalar(xhat[:, b, :], xs[:, b, :], mv[:, b, 0:1], rstd[:, b:b + 1],
                                          ALU.subtract, ALU.mult).then_inc(xhat_ready, 1)

                def per_expert(ap):
                    return ap.unsqueeze(2).to_broadcast([T, B, E])

                def per_batch(ap):
                    return ap.unsqueeze(1).to_broadcast([T, B, E])

                def route():
                    then = Chain(dve, route_step)
                    dve.wait_ge(consts_set, 7)
                    dve.wait_ge(logits_ready, 1)
                    logits = ps_y[0:T, 0, 0:B * E].rearrange("p (b e) -> p b e", e=E)
                    if router_b is None:
                        then(dve.tensor_copy(sel[:, :, :], logits))
                    else:
                        then(dve.tensor_tensor(key[:, :, :], logits, per_batch(rb[0:T, :]), ALU.add))
                        then(dve.tensor_reduce(rowmax[:, :], key[:, :, :], AX, ALU.max))
                        dve.tensor_tensor(key[:, :, :], key[:, :, :], per_expert(rowmax[:, :]), ALU.subtract).then_inc(exp_in, 1)
                        dve.wait_ge(exp_out, 1)
                        then(dve.tensor_reduce(norm_sum[:, :], sel[:, :, :], AX, ALU.add))
                        then(dve.reciprocal(norm_rec[:, :], norm_sum[:, :]))
                        then(dve.tensor_tensor(sel[:, :, :], sel[:, :, :], per_expert(norm_rec[:, :]), ALU.mult))
                    for k in range(top):
                        then(dve.tensor_reduce(value[:, k, :], sel[:, :, :], AX, ALU.max))
                        then(dve.tensor_tensor(key[:, :, :], sel[:, :, :], per_expert(value[:, k, :]), ALU.is_equal))
                        then(dve.tensor_tensor(key[:, :, :], key[:, :, :], per_batch(rev[0:T, :]), ALU.mult))
                        then(dve.tensor_reduce(rowmax[:, :], key[:, :, :], AX, ALU.max))
                        then(dve.tensor_tensor(pick[:, k], key[:, :, :], per_expert(rowmax[:, :]), ALU.is_equal))
                        if k < top - 1:
                            then(dve.scalar_tensor_tensor(out=sel[:, :, :], in0=pick[:, k], scalar=BIG, in1=sel[:, :, :],
                                                          op0=ALU.mult, op1=ALU.add))
                    then(dve.tensor_tensor(mask[:, :, :], pick[:, 0], pick[:, 1], ALU.add))
                    for k in range(2, top):
                        then(dve.tensor_tensor(mask[:, :, :], mask[:, :, :], pick[:, k], ALU.add))
                    dve.sem_inc(mask_ready, 1)
                    if router_b is None:
                        dve.tensor_tensor(norm_sum[:, :], value[:, 1, :], value[:, 0, :], ALU.subtract).then_inc(exp_in, 1)
                        dve.wait_ge(exp_out, 1)
                        then(dve.tensor_scalar(norm_sum[:, :], norm_rec[:, :], 1.0, None, ALU.add))
                        then(dve.reciprocal(value[:, 0, :], norm_sum[:, :]))
                        then(dve.tensor_tensor(value[:, 1, :], value[:, 0, :], norm_rec[:, :], ALU.mult))
                    then(dve.tensor_scalar(gates[:, :, :], value[:, :, :], tanhg[0:T, 0:1], None, ALU.mult))
                    dve.wait_ge(ranks_ready, 1)
                    in_batch = ps_y[0:T, 1, 0:B * E].rearrange("p (b e) -> p b e", e=E)
                    total = ps_y[0:T, 2, 0:B * E].rearrange("p (b e) -> p b e", e=E)
                    then(dve.tensor_copy(running[0][:, :, :], total))
                    upto, d = running[0][:, :, :], 1
                    while d < B:
                        nxt = running[d.bit_length() % 2]
                        dve.tensor_copy(nxt[:, 0:d, :], upto[:, 0:d, :])
                        then(dve.tensor_tensor(nxt[:, d:B, :], upto[:, d:B, :], upto[:, 0:B - d, :], ALU.add))
                        upto, d = nxt[:, :, :], 2 * d
                    dve.tensor_copy(ranks[:, 0:1, :], in_batch[:, 0:1, :])
                    then(dve.tensor_tensor(ranks[:, 1:B, :], in_batch[:, 1:B, :], upto[:, 0:B - 1, :], ALU.add))
                    counts = upto[:, B - 1, :]
                    then(dve.tensor_tensor(full[:, :, :], counts.unsqueeze(2).to_broadcast([T, E, ALL]),
                                           steps_of_p[0:T, :].unsqueeze(1).to_broadcast([T, E, ALL]), ALU.is_gt))
                    then(dve.tensor_reduce(tiles_of[:, :], full[:, :, :], AX, ALU.add))
                    then(dve.tensor_tensor(below[:, :, :], before[0:T, :, :], tiles_of[:, :].unsqueeze(1).to_broadcast([T, E, E]), ALU.mult))
                    then(dve.tensor_reduce(start[:, :], below[:, :, :], AX, ALU.add))
                    then(dve.tensor_tensor(end[:, :], start[:, :], tiles_of[:, :], ALU.add))
                    then(dve.tensor_tensor(passed[:, :, :], cols[0:1, 0:TILES].unsqueeze(2).to_broadcast([1, TILES, E]),
                                           end[0:1, :].unsqueeze(1).to_broadcast([1, TILES, E]), ALU.is_ge))
                    then(dve.tensor_reduce(expert_f[:, :], passed[:, :, :], AX, ALU.add))
                    dve.tensor_scalar(expert_of[:, 0:NT], expert_f[:, :], float(E - 1), None, ALU.min).then_inc(expert_ready, 1)
                    for k in range(top):
                        then(dve.tensor_tensor(picked[:, k], pick[:, k], ranks[:, :, :], ALU.mult))
                    by_choice = picked[:, :, :, :].rearrange("p k b e -> p (k b) e")
                    then(dve.tensor_reduce(rank[:, :], by_choice, AX, ALU.add))
                    then(dve.tensor_tensor(by_choice, pick[:, :, :, :].rearrange("p k b e -> p (k b) e"),
                                           start[0:T, :].unsqueeze(1).to_broadcast([T, CB, E]), ALU.mult))
                    then(dve.tensor_reduce(first[:, :], by_choice, AX, ALU.add))
                    then(dve.tensor_tensor(above[:, :, 1:ALL], rank[:, :].unsqueeze(2).to_broadcast([T, CB, ALL - 1]),
                                           steps_of_p[0:T, 1:ALL].unsqueeze(1).to_broadcast([T, CB, ALL - 1]), ALU.is_ge))
                    then(dve.tensor_reduce(tile_of[:, :], above[:, :, 1:ALL], AX, ALU.add))
                    then(dve.scalar_tensor_tensor(out=lane_of[:, :], in0=tile_of[:, :], scalar=-float(P), in1=rank[:, :],
                                                  op0=ALU.mult, op1=ALU.add))
                    then(dve.tensor_tensor(tile_of[:, :], tile_of[:, :], first[:, :], ALU.add))
                    then(dve.tensor_tensor(in_tile[:, :, :], tile_of[:, :].unsqueeze(2).to_broadcast([T, CB, TILES]),
                                           cols[0:T, 0:TILES].unsqueeze(1).to_broadcast([T, CB, TILES]), ALU.is_equal))
                    for k in range(top):
                        of_k = slice(k * B, (k + 1) * B)
                        dve.tensor_tensor(tile_vals[:, of_k, 0, :], in_tile[:, of_k, :],
                                          tok[:, :].unsqueeze(2).to_broadcast([T, B, TILES]), ALU.mult)
                        then(dve.tensor_scalar(tile_vals[:, of_k, 1, :], in_tile[:, of_k, :], float(k + 1), None, ALU.mult))
                        dve.tensor_tensor(in_lane[:, of_k, :], lane_of[:, of_k].unsqueeze(2).to_broadcast([T, B, P]),
                                          cols[0:T, :].unsqueeze(1).to_broadcast([T, B, P]), ALU.is_equal).then_inc(onehots_ready, 1)
                    dve.wait_ge(table_ready, 1)
                    token, choice = ps_y[:, 0, 0:TILES], ps_y[:, 0, TILES:2 * TILES]
                    then(dve.tensor_scalar(empty[:, :], choice, 0.0, None, ALU.is_equal))
                    then(dve.tensor_tensor(empty[:, :], empty[:, :], pad_row[:, :], ALU.mult))
                    then(dve.tensor_scalar(row_f[:, :], choice, float(TOK), -float(TOK), ALU.mult, ALU.add))
                    then(dve.tensor_tensor(row_f[:, :], row_f[:, :], token, ALU.add))
                    then(dve.tensor_copy(from_row[:, 0:NT], token))
                    then(dve.tensor_tensor(to_row[:, 0:NT], row_f[:, :], empty[:, :], ALU.add))

                def index_from(t, s, rnd):
                    need(dve, gathered[s], rnd * 16)
                    dve.sem_inc(dve_turns, 1)
                    dve.tensor_copy(gi[s][:, :], from_row[:, col(t)]).then_inc(from_ready, 1)

                def index_to(t, s, rnd):
                    need(dve, scattered[s], rnd * 16)
                    dve.sem_inc(dve_turns, 1)
                    dve.tensor_copy(si[s][:, :], to_row[:, col(t)]).then_inc(to_ready, 1)

                def take_xT(t, s, rnd):
                    dve.wait_ge(xT_ready, t + 1)
                    need(dve, h_ready, (t - N + 1) * U)
                    dve.tensor_copy(xT[s][:, :, :], ps_t[:, 0, 0:D].rearrange("p (c t) -> p c t", c=KC)).then_inc(xT_taken, 1)

                def take_y(t, s, rnd):
                    dve.wait_ge(b2_loaded, 16)
                    e = dve.value_load(expert_of[0:1, col(t)], min_val=0, max_val=E - 1)
                    dve.wait_ge(y_ready, t + 1)
                    need(dve, scattered[s], rnd * 16)
                    dve.sem_inc(dve_turns, 1)
                    dve.tensor_tensor(yt[s][:, :], ps_y[:, s, 0:D], b2all[:, bass.ds(e, 1), :].rearrange("p o d -> p (o d)"),
                                      ALU.add).then_inc(y_taken, 1)

                def step(t, at):
                    if live(t + 3):
                        index_from(t + 3, *at(3))
                    if live(t + 1):
                        take_xT(t + 1, *at(1))
                    if live(t):
                        index_to(t, *at(0))
                    if live(t - 1):
                        take_y(t - 1, *at(-1))

                for g in range(NG):
                    moments(g)
                    if g > 0:
                        normed(g - 1)
                normed(NG - 1)
                route()
                dve.wait_ge(expert_ready, 1)
                rounds(dve, step, 3, 1, NT)
                if shared:
                    dve.wait_ge(base_step, 3 * B)
                for i in range(NG * top):
                    g, way = i // top, i % top
                    dve.wait_ge(ways_in[i % PARTS_N], 16 * (i // PARTS_N + 1))
                    need(dve, added, i * (GB - 1) if way else 0)
                    for j in range(GB - 1):
                        b = g * GB + j
                        dve.scalar_tensor_tensor(out=xs[:, b, :], in0=parts[i % PARTS_N][:, j, :], scalar=gates[:, way, b:b + 1], in1=xs[:, b, :],
                                                 op0=ALU.mult, op1=ALU.add).then_inc(added, 1)

            @block.scalar
            def _(act):
                def step(t, at):
                    if live(t):
                        s, _ = at(0)
                        for u in range(U):
                            act.wait_ge(h_ready, t * U + u + 1)
                            if u == 0:
                                need(act, y_ready, t - N + 1)
                            bank = (s * U + u) % N
                            for i in range(UNIT):
                                c = u * UNIT + i
                                last = act.activation(hT[s][:, c, :], ps_h[:, bank, i * P:(i + 1) * P], ACT.Gelu,
                                                      bias=w1[s][:, B1 + c:B1 + c + 1])
                            last.then_inc(h_taken, 1)

                for i in range(B // 2):
                    act.wait_ge(turned, i + 1)
                    act.activation(turned_in(i).rearrange("p c (b t) -> p b c t", b=2),
                                   ps_t[:, i % 2, 0:2 * KC * T].rearrange("p (b c t) -> p b c t", b=2, c=KC), ACT.Copy).then_inc(turned_taken, 1)
                def shared_gelu(g):
                    for f in range(FS):
                        act.wait_ge(sh_ready, g * FS + f + 1)
                        if f == 0:
                            need(act, sy_ready, (g - 1) * GB)
                        act.activation(shT[g % 2][:, f, :], ps_h[:, f % 2, 0:GT], ACT.Gelu, bias=sb1[:, f:f + 1]).then_inc(sh_taken, 1)

                def shared_take(g):
                    for n in range(g * GB, (g + 1) * GB):
                        act.wait_ge(sy_ready, n + 1)
                        act.wait_ge(base_step, B)
                        act.activation(addend[:, n, :], shared_bank(n), ACT.Copy, scale=tanhg[0:T, 0:1]).then_inc(sy_taken, 1)

                if shared:
                    for n in range(B):
                        act.wait_ge(xhat_ready, n + 1)
                        act.activation(addend[:, n, :], xhat[:, n, :], ACT.Copy, scale=tanhg[0:T, 0:1]).then_inc(sx_ready, 1)
                    act.wait_ge(sw_loaded, 64)
                    act.activation(sb2[:, :], sb2[:, :], ACT.Copy, scale=tanhg[:, 0:1]).then_inc(sb2_ready, 1)
                act.wait_ge(exp_in, 1)
                if router_b is None:
                    act.activation(norm_rec[:, :], norm_sum[:, :], ACT.Exp).then_inc(exp_out, 1)
                else:
                    act.activation(sel[:, :, :], key[:, :, :], ACT.Exp).then_inc(exp_out, 1)
                if shared:
                    shared_gelu(0)
                    shared_gelu(1)
                    shared_take(0)
                    shared_gelu(2)
                    shared_take(1)
                    shared_gelu(3)
                    shared_take(2)
                    shared_take(3)
                    act.wait_ge(sy_ready, B)
                    act.dma_start(b2all, b2.partition_broadcast(P)).then_inc(b2_loaded, 16)
                rounds(act, step, 0, 1, NT)
                for i in range(NG * top):
                    b = i // top * GB + GB - 1
                    act.wait_ge(ways_in[i % PARTS_N], 16 * (i // PARTS_N + 1))
                    need(act, last_added, i - 1)
                    act.activation(weighted_row[i % 2][:, :], parts[i % PARTS_N][:, GB - 1, :], ACT.Copy,
                                   scale=gates[:, i % top, b:b + 1]).then_inc(weighted, 1)

            @block.tensor
            def _(pe):
                def turn(t, s, rnd):
                    pe.wait_ge(gathered[s], (rnd + 1) * 16)
                    need(pe, xT_taken, t)
                    for c in range(KC):
                        last = pe.transpose(ps_t[:, 0, c * P:(c + 1) * P], xt[s][:, c * P:(c + 1) * P], ident[:, :])
                    last.then_inc(xT_ready, 1)

                def hidden(t, s, rnd):
                    pe.wait_ge(w1_in[s], (rnd + 1) * 16)
                    pe.wait_ge(xT_taken, t + 1)
                    for u in range(U):
                        need(pe, h_taken, t * U + u - N + 1)
                        bank = (s * U + u) % N
                        for i in range(UNIT):
                            f = (u * UNIT + i) * P
                            for c in range(KC):
                                last = pe.matmul(ps_h[:, bank, i * P:(i + 1) * P], w1[s][:, c * ff + f:c * ff + f + P], xT[s][:, c, :],
                                                 start=(c == 0), stop=(c == KC - 1))
                        last.then_inc(h_ready, 1)

                def result(t, s, rnd):
                    pe.wait_ge(h_taken, (t + 1) * U)
                    need(pe, y_taken, t - N + 1)
                    pe.wait_ge(w2_in[s], (rnd + 1) * 16)
                    for c in range(FC):
                        last = pe.matmul(ps_y[:, s, 0:D], hT[s][:, c, :], w2[s][:, c * D:(c + 1) * D], start=(c == 0), stop=(c == FC - 1))
                    last.then_inc(y_ready, 1)

                def step(t, at):
                    if live(t + 1):
                        turn(t + 1, *at(1))
                    if live(t):
                        hidden(t, *at(0))
                    if live(t - 1):
                        result(t - 1, *at(-1))

                pe.wait_ge(w_loaded, 16 if router_b is None else 32)
                for i in range(B // 2 + 1):
                    if i < B // 2:
                        need(pe, turned_taken, i - 1)
                        pe.wait_ge(xhat_ready, 2 * i + 2)
                        for j in range(2):
                            for c in range(KC):
                                last = pe.transpose(ps_t[:, i % 2, (j * KC + c) * T:(j * KC + c + 1) * T],
                                                    xhat[:, 2 * i + j, c * P:(c + 1) * P], ident[0:T, 0:T])
                        last.then_inc(turned, 1)
                    if i > 0:
                        pe.wait_ge(turned_taken, i)
                        for j in range(2):
                            b = 2 * (i - 1) + j
                            for c in range(KC):
                                last = pe.matmul(ps_y[0:T, 0, b * E:(b + 1) * E], turned_in(i - 1)[:, c, j * T:(j + 1) * T], rw[:, c, :],
                                                 start=(c == 0), stop=(c == KC - 1))
                last.then_inc(logits_ready, 1)
                def rank():
                    pe.wait_ge(consts_set, 7)
                    pe.wait_ge(mask_ready, 1)
                    by_lane = mask[:, :, :].rearrange("p b e -> p (b e)")
                    pe.matmul(ps_y[0:T, 1, 0:B * E], tri[:, :], by_lane, start=True, stop=True)
                    pe.matmul(ps_y[0:T, 2, 0:B * E], ones[:, 0:T], by_lane, start=True, stop=True).then_inc(ranks_ready, 1)

                def shared_hidden(g):
                    pe.wait_ge(sw_loaded, 64)
                    pe.wait_ge(turned_taken, (g + 1) * GB // 2)
                    for f in range(FS):
                        need(pe, sh_taken, g * FS + f - 1)
                        for c in range(KC):
                            last = pe.matmul(ps_h[:, f % 2, 0:GT], sw1[:, c, f * P:(f + 1) * P], sxT[:, c, g * GT:(g + 1) * GT],
                                             start=(c == 0), stop=(c == KC - 1))
                        last.then_inc(sh_ready, 1)

                def shared_result(g):
                    pe.wait_ge(sh_taken, (g + 1) * FS)
                    for n in range(g * GB, (g + 1) * GB):
                        need(pe, sy_taken, n - 1)
                        for c in range(FS):
                            last = pe.matmul(shared_bank(n), shT[g % 2][:, c, n % GB * T:(n % GB + 1) * T], sw2[:, c, :],
                                             start=(c == 0), stop=(c == FS - 1))
                        last.then_inc(sy_ready, 1)

                def table():
                    for k in range(top):
                        pe.wait_ge(onehots_ready, k + 1)
                        for b in range(B):
                            c = k * B + b
                            last = pe.matmul(ps_y[:, 0, 0:2 * TILES], in_lane[:, c, :], tile_vals[:, c, :, :].rearrange("p v t -> p (v t)"),
                                             start=(c == 0), stop=(c == CB - 1))
                    last.then_inc(table_ready, 1)

                if shared:
                    shared_hidden(0)
                    shared_hidden(1)
                    shared_result(0)
                rank()
                if shared:
                    shared_hidden(2)
                    shared_result(1)
                    shared_hidden(3)
                    shared_result(2)
                table()
                if shared:
                    shared_result(3)
                rounds(pe, step, 1, 1, NT)


def build(nc, a, out):
    with ExitStack() as ctx:
        ident, mhalf, g_att, g_ffn = constants(nc, ctx, a["g_xattn"], a["g_ffn"])
        x1, x2, x3 = (nc.dram_tensor(f"x{i}", (B, T, D), F32).ap() for i in (1, 2, 3))
        attend0(nc, (ident, mhalf, g_att[:, 0:1]), a["x"], x1, a["ctxT"], *(a[f"L0_xattn_{n}"] for n in
                ("Wq", "bq", "Wk", "bk", "Wv", "bv", "Wo", "bo")))
        experts(nc, (ident, mhalf, g_ffn[:, 0:1]), "ex0", x1, x2, a["router0"], None, a["pack0_in"], a["pack0_out"], a["L0_ffn_b2"], 2, 1024, None)
        attend1(nc, (ident, mhalf, g_att[:, 1:2]), x2, x3, a["ctxT"], *(a[f"L1_xattn_{n}"] for n in
                ("Wqkv", "bqkv", "Wqkv_aux", "bqkv_aux", "Wo", "bo", "g")))
        experts(nc, (ident, mhalf, g_ffn[:, 1:2]), "ex1", x3, out, a["L1_ffn_gW"], a["L1_ffn_gb"], a["pack1_in"], a["pack1_out"], a["L1_ffn_rb2"], 3, 512,
                [a[f"L1_ffn_{n}"] for n in ("sW1", "sb1", "sW2", "sb2")])


def packed(np, w1, w2, b1):
    e, _, f = w1.shape
    return (np.concatenate([w1.reshape(e, KC, P, f).transpose(0, 2, 1, 3).reshape(e, P, KC * f),
                            b1.reshape(e, f // P, P).transpose(0, 2, 1)], axis=2),
            w2.reshape(e, f // P, P, D).transpose(0, 2, 1, 3).reshape(e, P, f // P * D))


def by_dimension(w):
    lead = w.shape[:-1]
    n = len(lead)
    return w.reshape(*lead, H // KC, KC, DH).transpose(*range(n), n + 1, n + 2, n).reshape(*lead, D)


def kernel(**inputs):
    import numpy as np
    import concourse.bacc as bacc
    from concourse.bass_utils import run_bass_kernel_spmd as run

    a = {k: np.asarray(v) for k, v in inputs.items()}
    laid = {k: v for k, v in a.items() if k.startswith(("x", "g_", "L0_xattn", "L1_xattn"))}
    laid.update({k: a[k] for k in ("L0_ffn_b2", "L1_ffn_gW", "L1_ffn_gb")})
    laid["ctxT"] = a["ctx_1024"].transpose(0, 2, 1)
    laid["router0"] = a["L0_ffn_router_w"].T
    laid["pack0_in"], laid["pack0_out"] = packed(np, a["L0_ffn_w1"].transpose(0, 2, 1), a["L0_ffn_w2"].transpose(0, 2, 1), a["L0_ffn_b1"])
    for name in ("L0_xattn_Wq", "L0_xattn_bq", "L0_xattn_Wk", "L0_xattn_bk"):
        laid[name] = by_dimension(laid[name])
    for name in ("L1_xattn_Wqkv", "L1_xattn_bqkv", "L1_xattn_Wqkv_aux", "L1_xattn_bqkv_aux"):
        laid[name] = np.concatenate([by_dimension(part) if i < 2 else part
                                     for i, part in enumerate(np.split(laid[name], 3, axis=-1))], axis=-1)
    laid["L0_xattn_Wo"] = np.pad(a["L0_xattn_Wo"].reshape(HG, CT, DH, D), ((0, 0), (0, 0), (0, 32 - DH), (0, 0))).reshape(HG, P, D)
    laid["pack1_in"], laid["pack1_out"] = packed(np, a["L1_ffn_rW1"], a["L1_ffn_rW2"], a["L1_ffn_rb1"])
    laid["L1_ffn_rb2"] = a["L1_ffn_rb2"]
    laid.update({f"L1_ffn_{n}": a[f"L1_ffn_{n}"][0] for n in ("sW1", "sb1", "sW2", "sb2")})
    nc = bacc.Bacc("TRN2", target_bir_lowering=False, num_devices=1)
    arrays, handles = {}, {}
    for name, arr in laid.items():
        arrays[f"in_{name}"] = np.ascontiguousarray(arr)
        handles[name] = nc.dram_tensor(f"in_{name}", arr.shape, mybir.dt.from_np(arr.dtype), kind="ExternalInput").ap()
    out = nc.dram_tensor("out_x", (B, T, D), F32, kind="ExternalOutput").ap()
    build(nc, handles, out)
    return run(nc, [arrays], core_ids=[0]).results[0]["out_x"]
```
